# Optimizing a Trainium2 kernel written in Bass

```python
import numpy as np
import jax
import jax.numpy as jnp

def _softmax(x, axis=-1):
    return jax.nn.softmax(x, axis=axis)

def _gelu(x):
    return jax.nn.gelu(x, approximate=True)

def _silu(x):
    return jax.nn.silu(x)

def _sigmoid(x):
    return jax.nn.sigmoid(x)

def _layernorm(x, axis=-1, eps=1e-05):
    m = jnp.mean(x, axis=axis, keepdims=True)
    v = jnp.var(x, axis=axis, keepdims=True)
    return (x - m) / jnp.sqrt(v + eps)

def _scatter_add(tgt, idx, src, axis=0):
    return tgt.at[idx].add(src)

def _segment_sum(src, seg, n):
    return jax.ops.segment_sum(src, seg, n)
kernel_name = 'mk_flamingo_gated_d1_seqx_r2_f8ad22'

def setup_inputs(seed: int=0):
    np.random.seed(seed)
    _w = jnp.asarray

    def _rec_inputs():
        import jax
        import jax.numpy as jnp
        _rk = jax.random.key(seed)
        x = 7.22e-05 + 1 * jax.random.normal(jax.random.fold_in(_rk, 1), (2, 2048, 512), jnp.float32)
        _lenS = 2048 - jax.random.randint(jax.random.fold_in(_rk, 7), (2,), 0, max(1, 2048 // 4) + 1, jnp.int32)
        _lenS2 = 77 - jax.random.randint(jax.random.fold_in(_rk, 8), (2,), 0, max(1, 77 // 4) + 1, jnp.int32)
        _ctx_1024P = jax.random.normal(jax.random.fold_in(_rk, 11), (2, 16, 512), jnp.float32)
        _ctx_1024c = jax.random.dirichlet(jax.random.fold_in(_rk, 511), 0.3 * jnp.ones((16,), jnp.float32), (2, 77))
        _ctx_1024t = jnp.einsum('bsk,bkd->bsd', _ctx_1024c, _ctx_1024P)
        _ctx_1024t = _ctx_1024t * jax.lax.rsqrt(jnp.mean(jnp.square(_ctx_1024t)) + 1e-12) * 0.953939
        ctx_1024 = -1.52775e-05 + 0.999936 * (_ctx_1024t + 0.3 * jax.random.normal(jax.random.fold_in(_rk, 611), (2, 77, 512), jnp.float32))
        _g = jax.random.normal(jax.random.fold_in(_rk, 9001), (2, 1), jnp.float32)
        _g = jnp.sign(_g) * jnp.maximum(jnp.abs(_g), 1.0) + (_g == 0) * 1.0
        g_xattn = _g[0]
        g_ffn = _g[1]
        return (x, ctx_1024, g_xattn, g_ffn)
    x, ctx_1024, g_xattn, g_ffn = _rec_inputs()

    def _L0_xattn_setup():
        import jax, jax.numpy as jnp
        import numpy as np
        HIDDEN = 512
        key = jax.random.key(seed)
        ks = jax.random.split(key, 8)
        s = 1.0 / np.sqrt(HIDDEN)
        return {'query': jax.random.normal(ks[0], (8, 512, HIDDEN), dtype=jnp.float32), 'ref': jax.random.normal(ks[1], (8, 2048, HIDDEN), dtype=jnp.float32), 'Wq': jax.random.normal(ks[2], (HIDDEN, HIDDEN), dtype=jnp.float32) * s, 'bq': jax.random.normal(ks[3], (HIDDEN,), dtype=jnp.float32) * s, 'Wk': jax.random.normal(ks[4], (HIDDEN, HIDDEN), dtype=jnp.float32) * s, 'bk': jax.random.normal(ks[5], (HIDDEN,), dtype=jnp.float32) * s, 'Wv': jax.random.normal(ks[6], (HIDDEN, HIDDEN), dtype=jnp.float32) * s, 'bv': jax.random.normal(ks[7], (HIDDEN,), dtype=jnp.float32) * s}
    _L0_xattn_all = _L0_xattn_setup()
    _L0_xattn_in = {k: v for k, v in _L0_xattn_all.items() if k in ('Wq', 'bq', 'Wk', 'bk', 'Wv', 'bv')}
    del _L0_xattn_all

    def _L0_ffn_setup():
        import jax, jax.numpy as jnp
        import numpy as np
        NUM_EXPERTS = 8
        TOP_K = 2
        CAPACITY_FACTOR = 1.25
        key = jax.random.key(seed)
        k1, k2, k3, k4, k5 = jax.random.split(key, 5)
        B, S, H, I, E = (4, 1024, 512, 2048, NUM_EXPERTS)
        return {'hidden_states': jax.random.normal(k1, (B, S, H), dtype=jnp.float32), 'router_gate': jax.random.normal(k2, (H, E), dtype=jnp.float32) * 0.02, 'gate_w': jax.random.normal(k3, (E, H, I), dtype=jnp.float32) * 0.02, 'up_w': jax.random.normal(k4, (E, H, I), dtype=jnp.float32) * 0.02, 'down_w': jax.random.normal(k5, (E, I, H), dtype=jnp.float32) * 0.02}
    _L0_ffn_all = _L0_ffn_setup()
    _L0_ffn_in = {k: v for k, v in _L0_ffn_all.items() if k in ('router_gate', 'gate_w', 'up_w', 'down_w')}
    del _L0_ffn_all
    return {'x': x, 'ctx_1024': ctx_1024, 'g_xattn': g_xattn, 'g_ffn': g_ffn, 'L0_xattn_Wq': _L0_xattn_in['Wq'], 'L0_xattn_bq': _L0_xattn_in['bq'], 'L0_xattn_Wk': _L0_xattn_in['Wk'], 'L0_xattn_bk': _L0_xattn_in['bk'], 'L0_xattn_Wv': _L0_xattn_in['Wv'], 'L0_xattn_bv': _L0_xattn_in['bv'], 'L0_ffn_router_gate': _L0_ffn_in['router_gate'], 'L0_ffn_gate_w': _L0_ffn_in['gate_w'], 'L0_ffn_up_w': _L0_ffn_in['up_w'], 'L0_ffn_down_w': _L0_ffn_in['down_w']}

def reference(x, ctx_1024, g_xattn, g_ffn, L0_xattn_Wq, L0_xattn_bq, L0_xattn_Wk, L0_xattn_bk, L0_xattn_Wv, L0_xattn_bv, L0_ffn_router_gate, L0_ffn_gate_w, L0_ffn_up_w, L0_ffn_down_w):
    import jax
    import jax.numpy as jnp

    def _L0_xattn_ref(query, ref, Wq, bq, Wk, bk, Wv, bv):
        import jax, jax.numpy as jnp
        import numpy as np
        HIDDEN = 512
        norm_fact = 1.0 / np.sqrt(HIDDEN).astype(np.float32)
        Q = query @ Wq + bq
        K = ref @ Wk + bk
        V = ref @ Wv + bv
        scores = jnp.einsum('bqh,bkh->bqk', Q, K)
        attn = jax.nn.softmax(scores, axis=-1) * norm_fact
        return jnp.einsum('bqk,bkh->bqh', attn, V)

    def _L0_ffn_ref(hidden_states, router_gate, gate_w, up_w, down_w):
        import jax, jax.numpy as jnp
        import numpy as np
        NUM_EXPERTS = 8
        TOP_K = 2
        CAPACITY_FACTOR = 1.25
        B, S, H = hidden_states.shape
        E = router_gate.shape[1]
        K = TOP_K
        x = hidden_states.reshape(-1, H)
        T = x.shape[0]
        cap = int(CAPACITY_FACTOR * ((T * K + E - 1) // E))
        probs = jax.nn.softmax(x @ router_gate, axis=-1)
        topw, topi = jax.lax.top_k(probs, K)
        topw = topw / (topw.sum(-1, keepdims=True) + 1e-09)
        gates = jnp.zeros((T, E), x.dtype).at[jnp.arange(T)[:, None], topi].set(topw)
        top_g, tok_idx = jax.lax.top_k(gates.T, cap)
        xe = x[tok_idx]
        h = jax.nn.silu(jnp.einsum('ech,ehi->eci', xe, gate_w)) * jnp.einsum('ech,ehi->eci', xe, up_w)
        ye = jnp.einsum('eci,eih->ech', h, down_w) * top_g[..., None]
        out = jnp.zeros_like(x).at[tok_idx.reshape(-1)].add(ye.reshape(-1, H))
        return out.reshape(B, S, H)
    x = x + jnp.tanh(g_xattn[0]) * _L0_xattn_ref(_layernorm(x, axis=-1), ctx_1024, L0_xattn_Wq, L0_xattn_bq, L0_xattn_Wk, L0_xattn_bk, L0_xattn_Wv, L0_xattn_bv)
    x = x + jnp.tanh(g_ffn[0]) * _L0_ffn_ref(_layernorm(x, axis=-1), L0_ffn_router_gate, L0_ffn_gate_w, L0_ffn_up_w, L0_ffn_down_w)
    return x

_drawn_inputs = setup_inputs


def setup_inputs(seed=0):
    import zlib

    import numpy as np

    out = dict(_drawn_inputs(seed))
    spreads = {}
    factors = {'L0_xattn_bq': 23.304, 'L0_xattn_bk': 64.0, 'L0_xattn_bv': 34.303}
    for name, (base, spread) in spreads.items():
        noise = np.random.default_rng([zlib.crc32(name.encode()), seed]).standard_normal(out[name].shape)
        drawn = base * np.exp(spread * noise) if base else spread * noise
        out[name] = jnp.asarray(drawn.astype(out[name].dtype))
    for name, factor in factors.items():
        out[name] = (out[name] * factor).astype(out[name].dtype)
    return out
```

```python
import concourse.bass as bass
from concourse import mybir
from contextlib import ExitStack

f32 = mybir.dt.float32
f32r = mybir.dt.float32r
bf16 = mybir.dt.bfloat16
i32 = mybir.dt.int32
ALU = mybir.AluOpType
ACT = mybir.ActivationFunctionType
AX = mybir.AxisListType

P = 128
B, S, H = 2, 2048, 512
T = B * S
KV = 77
E = 8
TOPK = 2
I = 2048
CAP = int(1.25 * ((T * TOPK + E - 1) // E))
HC = H // P
NT = T // P
GT = 4
NG = NT // GT
ST = CAP // P
DROPPED = 1 << 20
EPS = 1e-5
IC = 256
NI = IC // P
NCH = I // IC
BLOCKS = [(0, 512), (512, 512), (1024, 256)]
UNITS = NI * len(BLOCKS)
XPREP = 3


def flamingo_layer(nc, x, ctx_in, g_xattn, g_ffn, Wq, bq, Wk, bk, Wv, bv, router, gate_w, up_w, down_w, out):
    xn2_rows = nc.dram_tensor("xn2_rows", (T, H), f32, kind="Internal").ap()
    x_v = x.rearrange("b (t p) h -> p (b t) h", p=P)
    out_v = out[0:T, :].rearrange("(t p) h -> p t h", p=P)
    xn2_v = xn2_rows.rearrange("(t p) h -> p t h", p=P)

    def row(v):
        return v.rearrange("(a n) -> a n", a=1)

    whole = ExitStack()
    with whole:
        def keeper(ctx):
            def sb(name, shape, dt=f32):
                return ctx.enter_context(nc.sbuf_tensor(name, shape, dt))

            def pb(name, shape, dt=f32):
                return ctx.enter_context(nc.psum_tensor(name, shape, dt))

            def sem(name):
                return ctx.enter_context(nc.semaphore(name))
            return sb, pb, sem

        sb, pb, sem = keeper(whole)
        waited = {name: sem(f"waited_{name}") for name in ("pool", "dve", "pe")}

        def wait_alone(eng, s, value):
            name = {nc.gpsimd.engine: "pool", nc.vector.engine: "dve", nc.tensor.engine: "pe"}[eng.engine]
            eng.wait_ge(s, value)
            eng.sem_inc(waited[name], 1)

        ident = sb("ident", [P, P])
        ffn_tanh = sb("ffn_tanh", [P, 1])
        gather_row = sb("gather_row", [P, E + 1, ST], i32)
        scatter_row = sb("scatter_row", [P, E, ST], i32)
        slot_gate = sb("slot_gate", [P, E, ST])
        w_raw = [[sb(f"w_raw{n}_{c}", [P, 1024]) for c in range(3)] for n in range(2)]
        w_loaded = [[sem(f"w_loaded{n}_{c}") for c in range(3)] for n in range(2)]

        def load_chunk(eng, e, c, n):
            for k, w in enumerate((gate_w, up_w)):
                src = w[bass.ds(e, 1), :, bass.ds(c * IC, IC)].rearrange("a (k p) i -> p (a k) i", p=P)
                eng.dma_start(w_raw[n][k][:, :].rearrange("p (k i) -> p k i", k=HC), src)\
                   .then_inc(w_loaded[n][k], 16)
            src = down_w[bass.ds(e, 1), bass.ds(c * IC, IC), :].rearrange("a (k p) h -> p (a k) h", p=P)
            eng.dma_start(w_raw[n][2][:, :].rearrange("p (k h) -> p k h", k=NI), src)\
               .then_inc(w_loaded[n][2], 16)

        routing = whole.enter_context(ExitStack())
        sb, pb, sem = keeper(routing)
        logits = pb("logits", [P, NT, 16])

        with ExitStack() as ctx:
            sb, pb, sem = keeper(ctx)
            xg = [sb(f"xg{n}", [P, GT, H]) for n in range(2)]
            xn = sb("xn", [P, GT, H])
            xnT = sb("xnT", [P, GT, HC, P])
            xn2 = [sb(f"xn2_{n}", [P, GT, H]) for n in range(2)]
            xn2T = sb("xn2T", [P, GT, HC, P])
            stats = sb("stats", [P, GT, 6])
            mv = sb("mv", [P, GT, 2])
            veps = sb("veps", [P, GT])
            rstd = sb("rstd", [P, GT])
            stats2 = sb("stats2", [P, GT, 6])
            mv2 = sb("mv2", [P, GT, 2])
            veps2 = sb("veps2", [P, GT])
            rstd2 = sb("rstd2", [P, GT])
            shift2 = sb("shift2", [P, GT])
            negmean2 = sb("negmean2", [P, GT])
            half = sb("half", [P, GT])
            negmax = sb("negmax", [P, GT])
            esum = sb("esum", [P, GT])
            rsum = sb("rsum", [P, GT])
            ex = sb("ex", [P, GT, KV])
            exT = sb("exT", [KV, GT, P])
            Wq_s = sb("Wq_s", [P, HC, H])
            Wk_s = sb("Wk_s", [P, HC, H])
            Wv_s = sb("Wv_s", [P, HC, H])
            WqT = sb("WqT", [P, HC, H])
            R_s = sb("R_s", [P, HC, E])
            ctx_s = sb("ctx_s", [KV, B, H])
            ctxT = sb("ctxT", [P, HC, B * KV])
            KT = sb("KT", [P, HC, B * KV])
            A_s = sb("A_s", [P, HC, B * KV])
            V_s = sb("V_s", [KV, B, H])
            bias_s = sb("bias_s", [1, 3, H])
            bqT = sb("bqT", [P, HC])
            bqK = sb("bqK", [1, B * KV])
            ones = sb("ones", [1, B * KV])
            g_s = sb("g_s", [P, 2])
            v_scale = sb("v_scale", [P, 1])

            tp = [pb(f"tp{n}", [P, HC, P]) for n in range(2)]
            sc = [pb(f"sc{n}", [P, GT, P]) for n in range(2)]
            ep = pb("ep", [P, GT, P])
            op = [pb(f"op{n}", [P, H]) for n in range(2)]

            ident_zero, ident_ready, ones_ready = sem("ident_zero"), sem("ident_ready"), sem("ones_ready")
            half_ready = sem("half_ready")
            k_in, q_in, v_in, small_in = sem("k_in"), sem("q_in"), sem("v_in"), sem("small_in")
            g_in, trash_filled, router_in = sem("g_in"), sem("trash_filled"), sem("router_in")
            pre_pe, pre_act = sem("pre_pe"), sem("pre_act")
            tanh_done, v_scale_ready = sem("tanh_done"), sem("v_scale_ready")
            x_in = [sem(f"x_in{n}") for n in range(2)]
            stats_done, mv_done, rstd_done = sem("stats_done"), sem("mv_done"), sem("rstd_done")
            veps_done, veps2_done = sem("veps_done"), sem("veps2_done")
            stats2_done, mv2_done, rstd2_done = sem("stats2_done"), sem("mv2_done"), sem("rstd2_done")
            shift2_done = sem("shift2_done")
            xn_ready, xn_transposed, xnT_ready = sem("xn_ready"), sem("xn_transposed"), sem("xnT_ready")
            scores_done, negmax_done, exp_done = sem("scores_done"), sem("negmax_done"), sem("exp_done")
            ex_transposed, exT_ready, rsum_done = sem("ex_transposed"), sem("exT_ready"), sem("rsum_done")
            attn_done, x1_done = sem("attn_done"), sem("x1_done")
            xn2_ready, xn2_transposed, xn2T_ready = sem("xn2_ready"), sem("xn2_transposed"), sem("xn2T_ready")
            logits_done = sem("logits_done")
            x1_stored = [sem(f"x1_stored{n}") for n in range(2)]
            xn2_stored = [sem(f"xn2_stored{n}") for n in range(2)]
            block = ctx.enter_context(nc.Block())

            @block.sync
            def _(sp):
                sp.dma_start(ctx_s[:, :, :], ctx_in.rearrange("b k h -> k b h")).then_inc(small_in, 16)
                for n, v in enumerate((bq, bk, bv)):
                    sp.dma_start(bias_s[:, n, :], row(v)).then_inc(small_in, 16)
                sp.dma_start(g_s[:, 0:1], row(g_xattn).to_broadcast([P, 1])).then_inc(g_in, 16)
                sp.dma_start(g_s[:, 1:2], row(g_ffn).to_broadcast([P, 1])).then_inc(g_in, 16)
                sp.dma_start(xg[0][:, :, :], x_v[:, 0:GT, :]).then_inc(x_in[0], 16)
                sp.dma_start(Wk_s[:, :, :], Wk.rearrange("(k p) n -> p k n", p=P)).then_inc(k_in, 16)
                sp.dma_start(Wq_s[:, :, :], Wq.rearrange("(k p) n -> p k n", p=P)).then_inc(q_in, 16)
                sp.dma_start(Wv_s[:, :, :], Wv.rearrange("(k p) n -> p k n", p=P)).then_inc(v_in, 16)
                sp.dma_start(R_s[:, :, :], router.rearrange("(k p) n -> p k n", p=P)).then_inc(router_in, 16)
                sp.dma_start(xg[1][:, :, :], x_v[:, GT:2 * GT, :]).then_inc(x_in[1], 16)
                sp.dma_start(out[T:T + CAP, :].rearrange("(p a) h -> p (a h)", p=P),
                             x.rearrange("b s h -> (b s) h")[0:CAP, :].rearrange("(p a) h -> p (a h)", p=P))\
                  .then_inc(trash_filled, 16)
                with sp.Fori(1, NG // 2) as i:
                    for n in range(2):
                        sp.wait_ge(x1_stored[n], i * 16)
                        sp.wait_ge(xn2_stored[n], i * 16)
                        sp.wait_ge(xn2_ready, i * (2 * GT) + (n - 1) * GT)
                        sp.dma_start(xg[n][:, :, :], x_v[:, bass.ds(i * (2 * GT) + n * GT, GT), :])\
                          .then_inc(x_in[n], 16)
                for n in range(2):
                    load_chunk(sp, 0, n, n)
                sp.wait_ge(trash_filled, 16)
                for n in range(2):
                    sp.wait_ge(x1_stored[n], 16 * (NG // 2))
                    sp.wait_ge(xn2_stored[n], 16 * (NG // 2))

            @block.gpsimd
            def _(pool):
                pool.memset(ident[:, :], 0.0).then_inc(ident_zero, 1)
                pool.memset(half[:, :], -0.5).then_inc(half_ready, 1)
                pool.memset(ones[:, :], 1.0).then_inc(ones_ready, 1)
                pool.wait_ge(ident_zero, 1)
                pool.affine_select(out=ident[:, :], in_=ident[:, :], compare_op=ALU.not_equal, fill=1.0,
                                   base=0, pattern=[[-1, P]], channel_multiplier=1).then_inc(ident_ready, 1)
                pool.wait_ge(half_ready, 1)
                with pool.Fori(0, NG) as g:
                    wait_alone(pool, mv_done, g * GT + GT)
                    pool.tensor_scalar(veps[:, :], mv[:, :, 1], EPS, None, ALU.add).then_inc(veps_done, 1)
                    pool.wait_ge(veps_done, g + 1)
                    pool.tensor_tensor(rstd[:, :], veps[:, :], half[:, :], ALU.pow).then_inc(rstd_done, 1)
                    wait_alone(pool, mv2_done, g * GT + GT)
                    pool.tensor_scalar(veps2[:, :], mv2[:, :, 1], EPS, None, ALU.add).then_inc(veps2_done, 1)
                    pool.wait_ge(veps2_done, g + 1)
                    pool.tensor_tensor(rstd2[:, :], veps2[:, :], half[:, :], ALU.pow).then_inc(rstd2_done, 1)
                    pool.tensor_scalar(negmean2[:, :], mv2[:, :, 0], -1.0, None, ALU.mult).then_inc(rstd2_done, 1)
                    wait_alone(pool, rstd2_done, g * 2 + 2)
                    pool.tensor_tensor(shift2[:, :], negmean2[:, :], rstd2[:, :], ALU.mult).then_inc(shift2_done, 1)

            @block.vector
            def _(dve):
                dve.wait_ge(tanh_done, 1)
                nc.vector.tensor_scalar(v_scale[:, :], g_s[:, 0:1], float(H) ** -0.5, None, ALU.mult)\
                  .then_inc(v_scale_ready, 1)

                def group(i, n):
                    t0 = i * (2 * GT) + n * GT
                    g1 = i * 2 + n + 1
                    dve.wait_ge(x_in[n], i * 16 + 16)
                    for j in range(GT):
                        nc.vector.bn_stats(stats[:, j, :], xg[n][:, j, :]).then_inc(stats_done, 1)
                    for j in range(GT):
                        wait_alone(dve, stats_done, t0 + (j + 1))
                        nc.vector.bn_aggr(mv[:, j, :], stats[:, j, :]).then_inc(mv_done, 1)
                    dve.wait_ge(mv_done, t0 + GT)
                    dve.wait_ge(rstd_done, g1)
                    for j in range(GT):
                        nc.vector.tensor_scalar(xn[:, j, :], xg[n][:, j, :], mv[:, j, 0:1], rstd[:, j:j + 1],
                                                ALU.subtract, ALU.mult).then_inc(xn_ready, 1)
                    dve.wait_ge(scores_done, t0 + GT)
                    nc.vector.tensor_reduce(negmax[:, :], sc[n][:, :, 0:KV], AX.X, ALU.max, negate=True)\
                      .then_inc(negmax_done, 1)
                    dve.wait_ge(exp_done, t0 + GT)
                    nc.vector.reciprocal(rsum[:, :], esum[:, :]).then_inc(rsum_done, 1)
                    dve.wait_ge(rsum_done, g1)
                    for j in range(GT):
                        dve.wait_ge(attn_done, t0 + (j + 1))
                        nc.vector.scalar_tensor_tensor(xg[n][:, j, :], op[j % 2][:, :], rsum[:, j:j + 1],
                                                       xg[n][:, j, :], ALU.mult, ALU.add).then_inc(x1_done, 1)
                    for j in range(GT):
                        dve.wait_ge(x1_done, t0 + (j + 1))
                        nc.vector.bn_stats(stats2[:, j, :], xg[n][:, j, :]).then_inc(stats2_done, 1)
                    for j in range(GT):
                        wait_alone(dve, stats2_done, t0 + (j + 1))
                        nc.vector.bn_aggr(mv2[:, j, :], stats2[:, j, :]).then_inc(mv2_done, 1)

                with dve.Fori(0, NG // 2) as i:
                    for n in range(2):
                        group(i, n)

            @block.scalar
            def _(act):
                act.wait_ge(g_in, 32)
                nc.scalar.activation(g_s[:, 0:1], g_s[:, 0:1], ACT.Tanh).then_inc(tanh_done, 1)
                nc.scalar.activation(ffn_tanh[:, :], g_s[:, 1:2], ACT.Tanh)
                pre = [0]

                def evacuate(dst, src, scale=None):
                    pre[0] += 1
                    act.wait_ge(pre_pe, pre[0])
                    if scale is None:
                        nc.scalar.activation(dst, src, ACT.Copy).then_inc(pre_act, 1)
                    else:
                        nc.scalar.activation(dst, src, ACT.Copy, scale=scale).then_inc(pre_act, 1)

                for b in range(B):
                    evacuate(ctxT[:, :, b * KV:(b + 1) * KV], tp[b][:, :, 0:KV])
                evacuate(bqT[:, :], tp[0][:, 0, 0:HC])
                for d in range(HC):
                    evacuate(KT[:, d, :], tp[(d + 1) % 2][:, 0:2, :].rearrange("p a n -> p (a n)")[:, 0:B * KV])
                evacuate(bqK[:, :], tp[1][0:1, 0:2, :].rearrange("p a n -> p (a n)")[:, 0:B * KV])
                for d in range(HC):
                    evacuate(WqT[:, d, :], tp[d % 2][:, :, :].rearrange("p a n -> p (a n)"))
                for d in range(HC):
                    evacuate(A_s[:, d, :], tp[d % 2][:, 0:2, :].rearrange("p a n -> p (a n)")[:, 0:B * KV])
                act.wait_ge(v_scale_ready, 1)
                for b in range(B):
                    evacuate(V_s[:, b, :], tp[b][0:KV, :, :].rearrange("p a n -> p (a n)"), v_scale[0:KV, :])

                def group(i, n):
                    t0 = i * (2 * GT) + n * GT
                    g1 = i * 2 + n + 1
                    for j in range(GT):
                        act.wait_ge(xn_transposed, t0 + (j + 1))
                        nc.scalar.activation(xnT[:, j, :, :], tp[j % 2][:, :, :], ACT.Copy).then_inc(xnT_ready, 1)
                    act.wait_ge(negmax_done, g1)
                    for j in range(GT):
                        nc.scalar.activation(ex[:, j, :], sc[n][:, j, 0:KV], ACT.Exp, bias=negmax[:, j:j + 1],
                                             scale=1.0, accum_out=esum[:, j:j + 1]).then_inc(exp_done, 1)
                    act.wait_ge(ex_transposed, t0 + GT)
                    nc.scalar.activation(exT[:, :, :], ep[0:KV, :, :], ACT.Copy).then_inc(exT_ready, 1)
                    act.wait_ge(shift2_done, g1)
                    for j in range(GT):
                        nc.scalar.activation(xn2[n][:, j, :], xg[n][:, j, :], ACT.Identity,
                                             bias=shift2[:, j:j + 1], scale=rstd2[:, j:j + 1]).then_inc(xn2_ready, 1)
                    act.wait_ge(x1_done, t0 + GT)
                    act.dma_start(out_v[:, bass.ds(t0, GT), :], xg[n][:, :, :]).then_inc(x1_stored[n], 16)
                    for j in range(GT):
                        act.wait_ge(xn2_transposed, t0 + (j + 1))
                        nc.scalar.activation(xn2T[:, j, :, :], tp[j % 2][:, :, :], ACT.Copy).then_inc(xn2T_ready, 1)
                    act.wait_ge(xn2_ready, t0 + GT)
                    act.dma_start(xn2_v[:, bass.ds(t0, GT), :], xn2[n][:, :, :]).then_inc(xn2_stored[n], 16)

                with act.Fori(0, NG // 2) as i:
                    for n in range(2):
                        group(i, n)

            @block.tensor
            def _(pe):
                pe.wait_ge(ident_ready, 1)
                pe.wait_ge(ones_ready, 1)
                pe.wait_ge(small_in, 16 * 4)
                done = [0]

                def bank_free(last_reader):
                    if last_reader > 0:
                        pe.wait_ge(pre_act, last_reader)

                def flat(n):
                    return tp[n][:, :, :].rearrange("p a n -> p (a n)")

                def ended(last):
                    last.then_inc(pre_pe, 1)
                    done[0] += 1

                for b in range(B):
                    for k in range(HC):
                        last = nc.tensor.transpose(tp[b][:, k, 0:KV], ctx_s[:, b, k * P:(k + 1) * P],
                                                   ident[0:KV, 0:KV])
                    ended(last)
                bank_free(done[0] - 1)
                for k in range(HC):
                    last = nc.tensor.matmul(tp[0][:, 0, k:k + 1], bias_s[0:1, 0, k * P:(k + 1) * P],
                                            ones[0:1, 0:1], start=True, stop=True)
                ended(last)
                pe.wait_ge(k_in, 16)
                for d in range(HC):
                    bank_free(done[0] - 1)
                    dst = flat((d + 1) % 2)[:, 0:B * KV]
                    for k in range(HC):
                        nc.tensor.matmul(dst, Wk_s[:, k, d * P:(d + 1) * P], ctxT[:, k, :], start=(k == 0), stop=False)
                    ended(nc.tensor.matmul(dst, bias_s[0:1, 1, d * P:(d + 1) * P], ones[:, :], start=False, stop=True))
                bank_free(done[0])
                for d in range(HC):
                    last = nc.tensor.matmul(flat(1)[0:1, 0:B * KV], bqT[:, d:d + 1], KT[:, d, :],
                                            start=(d == 0), stop=(d == HC - 1))
                ended(last)
                pe.wait_ge(q_in, 16)
                for d in range(HC):
                    bank_free(done[0] - 1)
                    for k in range(HC):
                        last = nc.tensor.transpose(tp[d % 2][:, k, :], Wq_s[:, k, d * P:(d + 1) * P], ident[:, :])
                    ended(last)
                bank_free(done[0])
                for h in range(HC):
                    bank_free(done[0] - 1)
                    for d in range(HC):
                        last = nc.tensor.matmul(flat(h % 2)[:, 0:B * KV], WqT[:, d, h * P:(h + 1) * P], KT[:, d, :],
                                                start=(d == 0), stop=(d == HC - 1))
                    ended(last)
                pe.wait_ge(v_in, 16)
                for b in range(B):
                    bank_free(done[0] - 1)
                    for k in range(HC):
                        nc.tensor.matmul(flat(b)[0:KV, :], ctxT[:, k, b * KV:(b + 1) * KV], Wv_s[:, k, :],
                                         start=(k == 0), stop=False)
                    ended(nc.tensor.matmul(flat(b)[0:KV, :], ones[0:1, 0:KV], bias_s[0:1, 2, :], start=False, stop=True))
                bank_free(done[0])
                pe.wait_ge(router_in, 16)

                def group(i, n):
                    t0 = i * (2 * GT) + n * GT
                    batch = i // (NG // 2 // B)

                    def transpose_xn(j):
                        pe.wait_ge(xn_ready, t0 + (j + 1))
                        if j >= 2:
                            pe.wait_ge(xnT_ready, t0 + (j - 1))
                        for k in range(HC):
                            last = nc.tensor.transpose(tp[j % 2][:, k, :], xn[:, j, k * P:(k + 1) * P], ident[:, :])
                        last.then_inc(xn_transposed, 1)

                    def scores(j):
                        pe.wait_ge(xnT_ready, t0 + (j + 1))
                        for k in range(HC):
                            nc.tensor.matmul(sc[n][:, j, 0:KV], xnT[:, j, k, :], A_s[:, k, bass.ds(batch * KV, KV)],
                                             start=(k == 0), stop=False)
                        nc.tensor.matmul(sc[n][:, j, 0:KV], ones[0:1, 0:P], bqK[0:1, bass.ds(batch * KV, KV)],
                                         start=False, stop=True).then_inc(scores_done, 1)

                    def transpose_exp(j):
                        pe.wait_ge(exp_done, t0 + (j + 1))
                        nc.tensor.transpose(ep[0:KV, j, :], ex[:, j, :], ident[:, :]).then_inc(ex_transposed, 1)

                    def attend(j):
                        pe.wait_ge(exT_ready, i * 2 + (n + 1))
                        if j >= 2:
                            pe.wait_ge(x1_done, t0 + (j - 1))
                        nc.tensor.matmul(op[j % 2][:, :], exT[:, j, :], V_s[:, bass.ds(batch, 1), :].rearrange("p a h -> p (a h)"),
                                         start=True, stop=True).then_inc(attn_done, 1)

                    def transpose_xn2(j):
                        pe.wait_ge(xn2_ready, t0 + (j + 1))
                        if j >= 2:
                            pe.wait_ge(xn2T_ready, t0 + (j - 1))
                        for k in range(HC):
                            last = nc.tensor.transpose(tp[j % 2][:, k, :], xn2[n][:, j, k * P:(k + 1) * P], ident[:, :])
                        last.then_inc(xn2_transposed, 1)

                    def route(j):
                        pe.wait_ge(xn2T_ready, t0 + (j + 1))
                        dst = logits[:, bass.ds(t0 + j, 1), 0:E].rearrange("p a e -> p (a e)")
                        for k in range(HC):
                            last = nc.tensor.matmul(dst, xn2T[:, j, k, :], R_s[:, k, :], start=(k == 0), stop=(k == HC - 1))
                        last.then_inc(logits_done, 1)

                    def staggered(first, second):
                        first(0)
                        first(1)
                        for j in range(GT):
                            second(j)
                            if j + 2 < GT:
                                first(j + 2)

                    staggered(transpose_xn, scores)
                    for j in range(GT):
                        transpose_exp(j)
                    for j in range(GT):
                        attend(j)
                    staggered(transpose_xn2, route)

                with pe.Fori(0, NG // 2) as i:
                    for n in range(2):
                        group(i, n)

        with ExitStack() as ctx:
            sb, pb, sem = keeper(ctx)
            TE = [P, NT, E]
            shifted = sb("shifted", TE)
            prob = sb("prob", TE)
            rest = sb("rest", TE)
            tie = sb("tie", TE)
            first_hot = sb("first_hot", TE)
            second_hot = sb("second_hot", TE)
            tmax = sb("tmax", [P, NT])
            psum_ = sb("psum_", [P, NT])
            prsum = sb("prsum", [P, NT])
            top1 = sb("top1", [P, NT])
            top2 = sb("top2", [P, NT])
            pick = sb("pick", [P, NT])
            wsum = sb("wsum", [P, NT])
            weight1 = sb("weight1", [P, NT])
            weight2 = sb("weight2", [P, NT])
            order = sb("order", [P, E])
            gates = sb("gates", [P, E, NT])
            gate_head = sb("gate_head", [P, E, NT], f32r)
            gate_rest = sb("gate_rest", [P, E, NT])
            kept = sb("kept", [P, E, NT], bf16)
            above = sb("above", [P, E, NT])
            level = sb("level", [P, E, NT])
            level_b = sb("level_b", [P, E, NT], bf16)
            room = sb("room", [P, E])
            n_above = sb("n_above", [P, E])
            before = sb("before", [P, P], bf16)
            all_ones = sb("all_ones", [P, P], bf16)
            scan = [sb(f"scan{n}", [P, E, 16 + NT]) for n in range(2)]
            counts = sb("counts", [P, E])
            most = sb("most", [P, 1])
            crowded = sb("crowded", [P, 1], i32)
            bit = sb("bit", [P, E], i32)
            reached = sb("reached", [P, E])
            found = sb("found", [P, E], i32)
            cut = sb("cut", [P, E], i32)
            trial = sb("trial", [P, E], i32)
            pos = sb("pos", [P, E, NT])
            drop = sb("drop", [P, E, NT])
            pos_i = sb("pos_i", [P, E, NT], i32)
            low_i = sb("low_i", [P, E, NT], i32)
            low = sb("low", [P, E, NT])
            token = sb("token", [P, NT])
            slot_no = sb("slot_no", [P, P])
            tile_edge = sb("tile_edge", [P, ST + 1])
            trash_row = sb("trash_row", [P, ST])
            at_least = sb("at_least", [P, NT, ST + 1])
            in_tile = sb("in_tile", [P, NT, ST])
            hot = [sb(f"hot{n}", [P, NT, P], f32r) for n in range(2)]
            facts = [sb(f"facts{n}", [P, NT, ST, 4], f32r) for n in range(2)]
            taken = sb("taken", [P, ST])
            spare = sb("spare", [P, ST])

            within = pb("within", [P, 2, E, NT])[:, 0, :, :]
            totals = pb("totals", [P, 2, E, NT])[:, 0, :, :]
            table = [pb(f"table{n}", [P, 512])[:, 0:ST * 4].rearrange("p (a c) -> p a c", c=4) for n in range(2)]

            consts = sem("consts")
            exp_in, exp_out = sem("exp_in"), sem("exp_out")
            step = sem("step")
            kept_ready, counted = sem("kept_ready"), sem("counted")
            crowded_ready = sem("crowded_ready")
            trial_ready, trial_counted = sem("trial_ready"), sem("trial_counted")
            level_ready, level_counted = sem("level_ready"), sem("level_counted")
            hot_ready, table_done, table_read = sem("hot_ready"), sem("table_done"), sem("table_read")
            block = ctx.enter_context(nc.Block())
            N_CONSTS = 11
            BITS = 30

            @block.gpsimd
            def _(pool):
                pool.memset(all_ones[:, :], 1.0).then_inc(consts, 1)
                pool.memset(before[:, :], 1.0).then_inc(consts, 1)
                pool.wait_ge(consts, 2)
                pool.affine_select(out=before[:, :], in_=before[:, :], compare_op=ALU.is_gt, fill=0.0,
                                   base=0, pattern=[[1, P]], channel_multiplier=-1).then_inc(consts, 1)
                pool.iota(order[:, :], [[-1, E]], base=E, channel_multiplier=0,
                          allow_small_or_imprecise_dtypes=True).then_inc(consts, 1)
                pool.iota(token[:, :], [[P, NT]], base=0, channel_multiplier=1,
                          allow_small_or_imprecise_dtypes=True).then_inc(consts, 1)
                pool.iota(slot_no[:, :], [[1, P]], base=0, channel_multiplier=0,
                          allow_small_or_imprecise_dtypes=True).then_inc(consts, 1)
                pool.iota(tile_edge[:, :], [[P, ST + 1]], base=0, channel_multiplier=0,
                          allow_small_or_imprecise_dtypes=True).then_inc(consts, 1)
                pool.iota(trash_row[:, :], [[P, ST]], base=T, channel_multiplier=1,
                          allow_small_or_imprecise_dtypes=True).then_inc(consts, 1)
                for n in range(2):
                    pool.memset(scan[n][:, :, 0:16], 0.0).then_inc(consts, 1)
                pool.memset(gather_row[:, E, :], 0).then_inc(consts, 1)

            @block.scalar
            def _(act):
                act.wait_ge(exp_in, 1)
                nc.scalar.activation(prob[:, :, :], shifted[:, :, :], ACT.Exp).then_inc(exp_out, 1)

            @block.vector
            def _(dve):
                chain = [0]

                def then(ins):
                    ins.then_inc(step, 1)
                    chain[0] += 1
                    dve.wait_ge(step, chain[0])

                def over_e(v):
                    return v.unsqueeze(2).to_broadcast(TE)

                dve.wait_ge(consts, N_CONSTS)
                lg = logits[:, :, 0:E]
                then(nc.vector.tensor_reduce(tmax[:, :], lg, AX.X, ALU.max))
                nc.vector.tensor_tensor(shifted[:, :, :], lg, over_e(tmax[:, :]), ALU.subtract).then_inc(exp_in, 1)
                dve.wait_ge(exp_out, 1)
                then(nc.vector.tensor_reduce(psum_[:, :], prob[:, :, :], AX.X, ALU.add))
                then(nc.vector.reciprocal(prsum[:, :], psum_[:, :]))
                then(nc.vector.tensor_tensor(prob[:, :, :], prob[:, :, :], over_e(prsum[:, :]), ALU.mult))

                def top(values, best, hot_one):
                    then(nc.vector.tensor_reduce(best, values, AX.X, ALU.max))
                    then(nc.vector.tensor_tensor(tie[:, :, :], values, over_e(best), ALU.is_equal))
                    then(nc.vector.tensor_tensor(tie[:, :, :], tie[:, :, :], order[:, :].unsqueeze(1).to_broadcast(TE), ALU.mult))
                    then(nc.vector.tensor_reduce(pick[:, :], tie[:, :, :], AX.X, ALU.max))
                    then(nc.vector.tensor_tensor(hot_one, tie[:, :, :], over_e(pick[:, :]), ALU.is_equal))

                top(prob[:, :, :], top1[:, :], first_hot[:, :, :])
                then(nc.vector.scalar_tensor_tensor(rest[:, :, :], first_hot[:, :, :], -2.0, prob[:, :, :], ALU.mult, ALU.add))
                top(rest[:, :, :], top2[:, :], second_hot[:, :, :])
                then(nc.vector.scalar_tensor_tensor(wsum[:, :], top1[:, :], 1.0, top2[:, :], ALU.mult, ALU.add))
                then(nc.vector.tensor_scalar(wsum[:, :], wsum[:, :], 1e-9, None, ALU.add))
                then(nc.vector.reciprocal(wsum[:, :], wsum[:, :]))
                then(nc.vector.tensor_tensor(weight1[:, :], top1[:, :], wsum[:, :], ALU.mult))
                then(nc.vector.tensor_tensor(weight2[:, :], top2[:, :], wsum[:, :], ALU.mult))
                then(nc.vector.tensor_tensor(first_hot[:, :, :], first_hot[:, :, :], over_e(weight1[:, :]), ALU.mult))
                then(nc.vector.tensor_tensor(second_hot[:, :, :], second_hot[:, :, :], over_e(weight2[:, :]), ALU.mult))
                then(nc.vector.tensor_tensor(gates[:, :, :].rearrange("p e t -> p t e"), first_hot[:, :, :],
                                             second_hot[:, :, :], ALU.add))

                def running(dst, src):
                    then(nc.vector.tensor_copy(scan[0][:, :, 16:], src))
                    for k in range(5):
                        a, b = scan[k % 2], scan[(k + 1) % 2]
                        then(nc.vector.tensor_tensor(b[:, :, 16:], a[:, :, 16:], a[:, :, 16 - (1 << k):16 + NT - (1 << k)], ALU.add))
                    then(nc.vector.tensor_tensor(dst, scan[1][:, :, 16:], src, ALU.subtract))

                then(nc.vector.tensor_scalar(kept[:, :, :], gates[:, :, :], 0.0, None, ALU.is_gt))
                dve.sem_inc(kept_ready, 1)
                dve.wait_ge(counted, 1)
                then(nc.vector.tensor_reduce(counts[:, :], totals[:, :, :], AX.X, ALU.add))
                then(nc.vector.tensor_reduce(most[:, :], counts[:, :], AX.X, ALU.max))
                then(nc.vector.tensor_scalar(crowded[:, :], most[:, :], float(CAP), None, ALU.is_gt))
                dve.sem_inc(crowded_ready, 1)
                is_crowded = dve.value_load(crowded[0:1, 0:1], min_val=0, max_val=1)
                dve.nop()
                with dve.If(is_crowded == 1):
                    nc.vector.memset(cut[:, :], 0).then_inc(step, 1)
                    nc.vector.memset(bit[:, :], 1 << (BITS - 1)).then_inc(step, 1)
                    dve.wait_ge(step, chain[0] + 2)
                    base = chain[0] + 2
                    with dve.Fori(0, BITS) as r:
                        at = base + r * 7
                        nc.vector.tensor_tensor(trial[:, :], cut[:, :], bit[:, :], ALU.bitwise_or).then_inc(step, 1)
                        dve.wait_ge(step, at + 1)
                        nc.vector.tensor_tensor(kept[:, :, :], gates[:, :, :],
                                                trial[:, :].bitcast(f32).unsqueeze(2).to_broadcast([P, E, NT]),
                                                ALU.is_ge).then_inc(step, 1)
                        dve.wait_ge(step, at + 2)
                        dve.sem_inc(trial_ready, 1)
                        dve.wait_ge(trial_counted, r + 1)
                        nc.vector.tensor_reduce(reached[:, :], totals[:, :, :], AX.X, ALU.add).then_inc(step, 1)
                        dve.wait_ge(step, at + 3)
                        nc.vector.tensor_scalar(reached[:, :], reached[:, :], float(CAP), None, ALU.is_ge).then_inc(step, 1)
                        dve.wait_ge(step, at + 4)
                        nc.vector.tensor_tensor(found[:, :], reached[:, :], bit[:, :], ALU.mult).then_inc(step, 1)
                        dve.wait_ge(step, at + 5)
                        nc.vector.tensor_tensor(cut[:, :], cut[:, :], found[:, :], ALU.bitwise_or).then_inc(step, 1)
                        nc.vector.tensor_scalar(bit[:, :], bit[:, :], 1, None, ALU.logical_shift_right).then_inc(step, 1)
                        dve.wait_ge(step, at + 7)
                    chain[0] = base + BITS * 7
                    cut_f = cut[:, :].bitcast(f32).unsqueeze(2).to_broadcast([P, E, NT])
                    then(nc.vector.tensor_tensor(above[:, :, :], gates[:, :, :], cut_f, ALU.is_gt))
                    then(nc.vector.tensor_copy(kept[:, :, :], above[:, :, :]))
                    dve.sem_inc(trial_ready, 1)
                    dve.wait_ge(trial_counted, BITS + 1)
                    then(nc.vector.tensor_reduce(n_above[:, :], totals[:, :, :], AX.X, ALU.add))
                    then(nc.vector.tensor_scalar(room[:, :], n_above[:, :], -1.0, float(CAP), ALU.mult, ALU.add))
                    then(nc.vector.tensor_tensor(level[:, :, :], gates[:, :, :], cut_f, ALU.is_equal))
                    then(nc.vector.tensor_scalar(drop[:, :, :], gates[:, :, :], 0.0, None, ALU.is_gt))
                    then(nc.vector.tensor_tensor(level[:, :, :], level[:, :, :], drop[:, :, :], ALU.mult))
                    then(nc.vector.tensor_copy(kept[:, :, :], level[:, :, :]))
                    dve.sem_inc(trial_ready, 1)
                    dve.wait_ge(trial_counted, BITS + 2)
                    running(pos[:, :, :], totals[:, :, :])
                    then(nc.vector.tensor_tensor(pos[:, :, :], pos[:, :, :], within[:, :, :], ALU.add))
                    then(nc.vector.tensor_tensor(pos[:, :, :], pos[:, :, :], room[:, :].unsqueeze(2).to_broadcast([P, E, NT]), ALU.is_lt))
                    then(nc.vector.tensor_tensor(level[:, :, :], level[:, :, :], pos[:, :, :], ALU.mult))
                    then(nc.vector.tensor_tensor(kept[:, :, :], above[:, :, :], level[:, :, :], ALU.add))
                    dve.sem_inc(trial_ready, 1)
                    dve.wait_ge(trial_counted, BITS + 3)
                    end_of_search = chain[0]
                with dve.Else():
                    dve.sem_inc(step, end_of_search - (base - 2))
                dve.nop()

                running(pos[:, :, :], totals[:, :, :])
                then(nc.vector.tensor_tensor(pos[:, :, :], pos[:, :, :], within[:, :, :], ALU.add))
                then(nc.vector.tensor_scalar(drop[:, :, :], kept[:, :, :], -float(DROPPED), float(DROPPED), ALU.mult, ALU.add))
                then(nc.vector.tensor_tensor(pos[:, :, :], pos[:, :, :], kept[:, :, :], ALU.mult))
                then(nc.vector.tensor_tensor(pos[:, :, :], pos[:, :, :], drop[:, :, :], ALU.add))
                then(nc.vector.tensor_copy(pos_i[:, :, :], pos[:, :, :]))
                then(nc.vector.tensor_scalar(low_i[:, :, :], pos_i[:, :, :], P - 1, None, ALU.bitwise_and))
                then(nc.vector.tensor_copy(low[:, :, :], low_i[:, :, :]))
                then(nc.vector.tensor_scalar(gates[:, :, :], gates[:, :, :], ffn_tanh[:, 0:1], None, ALU.mult))
                then(nc.vector.tensor_copy(gate_head[:, :, :], gates[:, :, :]))
                then(nc.vector.tensor_tensor(gate_rest[:, :, :], gates[:, :, :], gate_head[:, :, :].bitcast(f32), ALU.subtract))

                def mark(e):
                    n = e % 2
                    grid = [P, NT, ST]
                    if e >= 2:
                        dve.wait_ge(table_done, e - 1)
                    nc.vector.tensor_tensor(hot[n][:, :, :], slot_no[:, :].unsqueeze(1).to_broadcast([P, NT, P]),
                                            low[:, e, :].unsqueeze(2).to_broadcast([P, NT, P]), ALU.is_equal)\
                      .then_inc(hot_ready, 1)
                    then(nc.vector.tensor_tensor(at_least[:, :, :], pos[:, e, :].unsqueeze(2).to_broadcast([P, NT, ST + 1]),
                                                 tile_edge[:, :].unsqueeze(1).to_broadcast([P, NT, ST + 1]), ALU.is_ge))
                    then(nc.vector.tensor_tensor(in_tile[:, :, :], at_least[:, :, 0:ST], at_least[:, :, 1:ST + 1], ALU.subtract))
                    for c, fact in enumerate((token[:, :], gate_head[:, e, :].bitcast(f32), gate_rest[:, e, :])):
                        nc.vector.tensor_tensor(facts[n][:, :, :, c], in_tile[:, :, :], fact.unsqueeze(2).to_broadcast(grid),
                                                ALU.mult).then_inc(hot_ready, 1)
                    then(nc.vector.tensor_copy(facts[n][:, :, :, 3], in_tile[:, :, :]))
                    dve.sem_inc(hot_ready, 1)

                def read(e):
                    n = e % 2
                    dve.wait_ge(table_done, e + 1)
                    nc.vector.tensor_copy(gather_row[:, e, :], table[n][:, :, 0])
                    then(nc.vector.tensor_copy(slot_gate[:, e, :], table[n][:, :, 1]))
                    then(nc.vector.tensor_tensor(slot_gate[:, e, :], slot_gate[:, e, :], table[n][:, :, 2], ALU.add))
                    then(nc.vector.tensor_tensor(taken[:, :], table[n][:, :, 3], trash_row[:, :], ALU.mult))
                    then(nc.vector.tensor_tensor(spare[:, :], trash_row[:, :], taken[:, :], ALU.subtract))
                    nc.vector.tensor_tensor(scatter_row[:, e, :], table[n][:, :, 0], spare[:, :], ALU.add).then_inc(table_read, 1)

                for e in range(E):
                    mark(e)
                    if e:
                        read(e - 1)
                read(E - 1)

            @block.tensor
            def _(pe):
                pe.wait_ge(consts, N_CONSTS)
                kept_v = kept[:, :, :].rearrange("p e t -> p (e t)")

                def count():
                    nc.tensor.matmul(totals[:, :, :].rearrange("p e t -> p (e t)"), all_ones[:, :], kept_v, start=True, stop=True)
                    return nc.tensor.matmul(within[:, :, :].rearrange("p e t -> p (e t)"), before[:, :], kept_v, start=True, stop=True)

                pe.wait_ge(kept_ready, 1)
                count().then_inc(counted, 1)
                pe.wait_ge(crowded_ready, 1)
                is_crowded = pe.value_load(crowded[0:1, 0:1], min_val=0, max_val=1)
                pe.nop()
                with pe.If(is_crowded == 1):
                    with pe.Fori(0, BITS + 3) as r:
                        pe.wait_ge(trial_ready, r + 1)
                        count().then_inc(trial_counted, 1)
                pe.nop()
                for e in range(E):
                    pe.wait_ge(hot_ready, 5 * (e + 1))
                    if e >= 2:
                        pe.wait_ge(table_read, e - 1)
                    for t in range(NT):
                        last = nc.tensor.matmul(table[e % 2][:, :, :].rearrange("p a c -> p (a c)"), hot[e % 2][:, t, :],
                                                facts[e % 2][:, t, :, :].rearrange("p a c -> p (a c)"),
                                                start=(t == 0), stop=(t == NT - 1))
                    last.then_inc(table_done, 1)

        routing.close()

        with ExitStack() as ctx:
            sb, pb, sem = keeper(ctx)
            wg_hd = [sb(f"wg_hd{n}", [P, HC, IC], f32r) for n in range(2)]
            wg_rs = [sb(f"wg_rs{n}", [P, HC, IC], f32r) for n in range(2)]
            wu_hd = [sb(f"wu_hd{n}", [P, HC, IC], f32r) for n in range(2)]
            wu_rs = [sb(f"wu_rs{n}", [P, HC, IC], f32r) for n in range(2)]
            wd_hd = [sb(f"wd_hd{n}", [P, NI, H], f32r) for n in range(2)]
            wd_rs = [sb(f"wd_rs{n}", [P, NI, H], f32r) for n in range(2)]
            xT_hd = [sb(f"xT_hd{n}", [P, HC, CAP], f32r) for n in range(2)]
            xT_rs = [sb(f"xT_rs{n}", [P, HC, CAP], f32r) for n in range(2)]
            xrow = [sb(f"xrow{n}", [P, H]) for n in range(XPREP)]
            h_hd = sb("h_hd", [P, NI, CAP], f32r)
            h_rs = sb("h_rs", [P, NI, CAP], f32r)
            silu = [sb(f"silu{n}", [P, 512]) for n in range(2)]
            hfull = [sb(f"hfull{n}", [P, 512]) for n in range(2)]
            y = sb("y", [P, ST, H])
            gate_now = sb("gate_now", [P, ST])
            gather_now = sb("gather_now", [P, XPREP], i32)
            scatter_now = sb("scatter_now", [P, ST], i32)
            heads = (wg_hd, wu_hd, wd_hd)
            rests = (wg_rs, wu_rs, wd_rs)

            pg = [pb(f"pg{n}", [P, 512]) for n in range(2)]
            pu = [pb(f"pu{n}", [P, 512]) for n in range(2)]
            py = [pb(f"py{n}", [P, H]) for n in range(2)]
            px = [pb(f"px{n}", [P, HC, P]) for n in range(2)]

            w_head_done, w_split = sem("w_head_done"), sem("w_split")
            row_in = [sem(f"row_in{n}") for n in range(XPREP)]
            row_transposed, xT_head_done, xT_split = sem("row_transposed"), sem("xT_head_done"), sem("xT_split")
            gate_done, up_done = sem("gate_done"), sem("up_done")
            silu_done, hfull_done, h_head_done, h_split = sem("silu_done"), sem("hfull_done"), sem("h_head_done"), sem("h_split")
            down_done, y_added, y_gated, y_scattered = sem("down_done"), sem("y_added"), sem("y_gated"), sem("y_scattered")
            gate_copied, index_copied = sem("gate_copied"), sem("index_copied")
            y_free = sem("y_free")
            block = ctx.enter_context(nc.Block())
            PAIRS = NCH // 2
            XE = PAIRS * XPREP

            def row_buffer(t):
                return (t - ST) % XPREP

            def row_count(t):
                return 16 * sum(row_buffer(u) == row_buffer(t) for u in range(t + 1))

            FIRST = [row_count(ST - XPREP + j) for j in range(XPREP)]

            def first_tile(k):
                return (k * 5) // 2

            UNIT = [(c0, w, it) for c0, w in BLOCKS for it in range(NI)]

            @block.sync
            def _(sp):
                with sp.Fori(1, PAIRS) as k:
                    for n in range(2):
                        sp.wait_ge(w_split, k * 6 + (n * 3 - 3))
                        load_chunk(sp, 0, k * 2 + n, n)
                with sp.Fori(1, E) as e:
                    with sp.Fori(0, PAIRS) as k:
                        for n in range(2):
                            sp.wait_ge(w_split, e * (PAIRS * 6) + k * 6 + (n * 3 - 3))
                            load_chunk(sp, e, k * 2 + n, n)
                sp.wait_ge(w_split, 3 * (E * NCH - 1))
                load_chunk(sp, E - 1, NCH - 1, 0)

            @block.gpsimd
            def _(pool):
                gather_flat = gather_row[:, :, :].rearrange("p e t -> p (e t)")
                scatter_flat = scatter_row[:, :, :].rearrange("p e t -> p (e t)")
                for t in range(ST):
                    if t >= XPREP:
                        pool.wait_ge(row_transposed, t - XPREP + 1)
                    pool.indirect_dma_start(xrow[row_buffer(t)][:, :], None, xn2_rows,
                                            bass.IndirectOffsetOnAxis(ap=gather_row[:, 0, t:t + 1], axis=0))\
                        .then_inc(row_in[row_buffer(t)], 16)
                pool.sem_inc(y_free, 1)
                with pool.Fori(0, E) as e:
                    with pool.Fori(0, PAIRS) as k:
                        for j in range(XPREP):
                            pool.wait_ge(row_transposed, e * XE + k * XPREP + (ST + j - XPREP + 1))
                            pool.tensor_copy(gather_now[:, j:j + 1],
                                             gather_flat[:, bass.ds(e * ST + first_tile(k) + (ST + j), 1)])\
                                .then_inc(index_copied, 1)
                            wait_alone(pool, index_copied, e * (XE + 1) + k * XPREP + (j + 1))
                            pool.indirect_dma_start(xrow[j][:, :], None, xn2_rows,
                                                    bass.IndirectOffsetOnAxis(ap=gather_now[:, j:j + 1], axis=0))\
                                .then_inc(row_in[j], 16)
                    pool.tensor_copy(scatter_now[:, :], scatter_flat[:, bass.ds(e * ST, ST)]).then_inc(index_copied, 1)
                    pool.wait_ge(index_copied, e * (XE + 1) + (XE + 1))
                    for t in range(ST):
                        wait_alone(pool, y_gated, e * ST + (t + 1))
                        pool.indirect_dma_start(out, bass.IndirectOffsetOnAxis(ap=scatter_now[:, t:t + 1], axis=0),
                                                y[:, t, :], None, compute_op=ALU.add).then_inc(y_scattered, 16)
                    pool.wait_ge(y_scattered, e * (ST * 16) + ST * 16)
                    pool.sem_inc(y_free, 1)

            @block.scalar
            def _(act):
                def split_weights(n, c, loaded):
                    act.wait_ge(w_loaded[n][c], loaded)
                    nc.scalar.activation(heads[c][n][:, :, :].rearrange("p a b -> p (a b)"), w_raw[n][c][:, :],
                                         ACT.Copy).then_inc(w_head_done, 1)

                def head_of_rows(par, t, bank, number):
                    act.wait_ge(row_transposed, number)
                    nc.scalar.activation(xT_hd[par][:, :, bass.ds(t * P, P)], px[bank][:, :, :], ACT.Copy)\
                      .then_inc(xT_head_done, 1)

                for c in range(3):
                    split_weights(0, c, 16)
                for t in range(ST):
                    head_of_rows(0, t, t % 2, t + 1)
                with act.Fori(0, E // 2) as p:
                    for par in range(2):
                        e = p * 2 + par
                        with act.Fori(0, PAIRS) as k:
                            m = e * PAIRS + k
                            for w in range(2):
                                u0 = m * (2 * UNITS) + w * UNITS
                                for q, (c0, width, it) in enumerate(UNIT):
                                    b = q % 2
                                    act.wait_ge(gate_done, u0 + (q + 1))
                                    nc.scalar.activation(silu[b][:, 0:width], pg[b][:, 0:width], ACT.Silu)\
                                      .then_inc(silu_done, 1)
                                    act.wait_ge(hfull_done, u0 + (q + 1))
                                    nc.scalar.activation(h_hd[:, it, c0:c0 + width], hfull[b][:, 0:width], ACT.Copy)\
                                      .then_inc(h_head_done, 1)
                                    if q < 3:
                                        split_weights(1 - w, q, m * 16 + (16 + 16 * w))
                                    elif w == 0:
                                        head_of_rows(1 - par, first_tile(k) + (q - 3), (q - 3) % 2,
                                                     m * XPREP + (ST + q - 2))
                        nc.scalar.activation(gate_now[:, :], slot_gate[:, bass.ds(e, 1), :].rearrange("p a t -> p (a t)"),
                                             ACT.Copy).then_inc(gate_copied, 1)
                        act.wait_ge(gate_copied, e + 1)
                        for t in range(ST):
                            act.wait_ge(y_added, e * (NCH * ST) + ((NCH - 1) * ST + t + 2))
                            nc.scalar.activation(y[:, t, :], y[:, t, :], ACT.Copy, scale=gate_now[:, t:t + 1])\
                              .then_inc(y_gated, 1)

            @block.vector
            def _(dve):
                def rest_of_weights(n, c, number):
                    dve.wait_ge(w_head_done, number)
                    nc.vector.tensor_tensor(rests[c][n][:, :, :].rearrange("p a b -> p (a b)"), w_raw[n][c][:, :],
                                            heads[c][n][:, :, :].rearrange("p a b -> p (a b)").bitcast(f32),
                                            ALU.subtract).then_inc(w_split, 1)

                def rest_of_rows(par, t, bank, number):
                    dve.wait_ge(xT_head_done, number)
                    nc.vector.tensor_tensor(xT_rs[par][:, :, bass.ds(t * P, P)], px[bank][:, :, :],
                                            xT_hd[par][:, :, bass.ds(t * P, P)].bitcast(f32), ALU.subtract)\
                      .then_inc(xT_split, 1)

                dve.sem_inc(y_added, 1)
                for c in range(3):
                    rest_of_weights(0, c, c + 1)
                for t in range(ST):
                    rest_of_rows(0, t, t % 2, t + 1)
                with dve.Fori(0, E // 2) as p:
                    for par in range(2):
                        e = p * 2 + par
                        with dve.Fori(0, PAIRS) as k:
                            m = e * PAIRS + k
                            for w in range(2):
                                u0 = m * (2 * UNITS) + w * UNITS
                                y0 = m * (2 * ST) + w * ST
                                for q, (c0, width, it) in enumerate(UNIT):
                                    b = q % 2
                                    dve.wait_ge(up_done, u0 + (q + 1))
                                    dve.wait_ge(silu_done, u0 + (q + 1))
                                    nc.vector.tensor_tensor(hfull[b][:, 0:width], silu[b][:, 0:width], pu[b][:, 0:width],
                                                            ALU.mult).then_inc(hfull_done, 1)
                                    dve.wait_ge(h_head_done, u0 + (q + 1))
                                    nc.vector.tensor_tensor(h_rs[:, it, c0:c0 + width], hfull[b][:, 0:width],
                                                            h_hd[:, it, c0:c0 + width].bitcast(f32), ALU.subtract)\
                                      .then_inc(h_split, 1)
                                    if q < 3:
                                        rest_of_weights(1 - w, q, m * 6 + (3 * w + 4 + q))
                                    elif w == 0:
                                        rest_of_rows(1 - par, first_tile(k) + (q - 3), (q - 3) % 2,
                                                     m * XPREP + (ST + q - 2))

                                def add_up(t):
                                    dve.wait_ge(down_done, y0 + (t + 1))
                                    nc.vector.tensor_tensor(y[:, t, :], py[t % 2][:, :], y[:, t, :], ALU.add)\
                                      .then_inc(y_added, 1)

                                if w == 0:
                                    dve.nop()
                                    with dve.If(k == 0):
                                        dve.wait_ge(y_free, e + 1)
                                        for t in range(ST):
                                            dve.wait_ge(down_done, y0 + (t + 1))
                                            nc.vector.tensor_copy(y[:, t, :], py[t % 2][:, :]).then_inc(y_added, 1)
                                    with dve.Else():
                                        for t in range(ST):
                                            add_up(t)
                                    dve.nop()
                                else:
                                    for t in range(ST):
                                        add_up(t)

            @block.tensor
            def _(pe):
                def transpose_rows(j, bank):
                    for k in range(HC):
                        last = nc.tensor.transpose(px[bank][:, k, :], xrow[j][:, k * P:(k + 1) * P], ident[:, :])
                    last.then_inc(row_transposed, 1)

                def three_passes(dst, pairs):
                    last = None
                    for n, ((lhd, lrs), (rhd, rrs)) in enumerate(pairs):
                        nc.tensor.matmul(dst, lhd, rhd, start=(n == 0), stop=False)
                        nc.tensor.matmul(dst, lhd, rrs, start=False, stop=False)
                        last = nc.tensor.matmul(dst, lrs, rhd, start=False, stop=(n == len(pairs) - 1))
                    return last

                for t in range(ST):
                    pe.wait_ge(row_in[row_buffer(t)], row_count(t))
                    if t >= 2:
                        pe.wait_ge(xT_split, t - 1)
                    transpose_rows(row_buffer(t), t % 2)
                with pe.Fori(0, E // 2) as p:
                    for par in range(2):
                        e = p * 2 + par
                        wait_alone(pe, xT_split, e * XE + ST)
                        with pe.Fori(0, PAIRS) as k:
                            m = e * PAIRS + k
                            for w in range(2):
                                u0 = m * (2 * UNITS) + w * UNITS
                                y0 = m * (2 * ST) + w * ST
                                pe.wait_ge(w_split, m * 6 + (3 * w + 3))
                                for q, (c0, width, it) in enumerate(UNIT):
                                    b = q % 2
                                    if q >= 2:
                                        pe.wait_ge(hfull_done, u0 + (q - 1))
                                    ic = slice(it * P, (it + 1) * P)
                                    for (hd, rs), dst, s in (((wg_hd, wg_rs), pg, gate_done), ((wu_hd, wu_rs), pu, up_done)):
                                        three_passes(dst[b][:, 0:width],
                                                     [((hd[w][:, c, ic], rs[w][:, c, ic]),
                                                       (xT_hd[par][:, c, c0:c0 + width], xT_rs[par][:, c, c0:c0 + width]))
                                                      for c in range(HC)]).then_inc(s, 1)
                                    if w == 0 and q >= 3:
                                        j = q - 3
                                        pe.wait_ge(row_in[j], m * 16 + (FIRST[j] + 16))
                                        if j != 1:
                                            pe.wait_ge(xT_split, m * XPREP + (ST + j // 2))
                                        transpose_rows(j, j % 2)
                                for t in range(ST):
                                    if t * P in (c0 for c0, _ in BLOCKS):
                                        ready = [n for n, (c0, _) in enumerate(BLOCKS) if c0 == t * P][0]
                                        pe.wait_ge(h_split, u0 + (ready + 1) * NI)
                                    pe.wait_ge(y_added, y0 + max(t, 1))
                                    sl = slice(t * P, (t + 1) * P)
                                    three_passes(py[t % 2][:, :],
                                                 [((h_hd[:, it, sl], h_rs[:, it, sl]), (wd_hd[w][:, it, :], wd_rs[w][:, it, :]))
                                                  for it in range(NI)]).then_inc(down_done, 1)


_INS = ['x', 'ctx_1024', 'g_xattn', 'g_ffn', 'L0_xattn_Wq', 'L0_xattn_bq', 'L0_xattn_Wk', 'L0_xattn_bk',
        'L0_xattn_Wv', 'L0_xattn_bv', 'L0_ffn_router_gate', 'L0_ffn_gate_w', 'L0_ffn_up_w', 'L0_ffn_down_w']


def kernel(**inputs):
    import numpy as _np
    import concourse.bacc as _bacc
    from concourse import mybir as _mybir
    from concourse.bass_utils import run_bass_kernel_spmd as _run

    nc = _bacc.Bacc("TRN2", target_bir_lowering=False, num_devices=1)
    arrays, args = {}, []
    for name in _INS:
        a = _np.ascontiguousarray(inputs[name])
        arrays[f"in_{name}_dram"] = a
        args.append(nc.dram_tensor(f"in_{name}_dram", a.shape, _mybir.dt.from_np(a.dtype), kind="ExternalInput").ap())
    args.append(nc.dram_tensor("out_dram", (T + CAP, H), _mybir.dt.float32, kind="ExternalOutput").ap())
    flamingo_layer(nc, *args)
    r = _run(nc, [arrays], core_ids=[0])
    return r.results[0]["out_dram"][:T].reshape(B, S, H)
```

```python
import concourse.bass as bass
from concourse import mybir
from contextlib import ExitStack

f32 = mybir.dt.float32
f32r = mybir.dt.float32r
bf16 = mybir.dt.bfloat16
i32 = mybir.dt.int32
ALU = mybir.AluOpType
ACT = mybir.ActivationFunctionType
AX = mybir.AxisListType

P = 128
B, S, H = 2, 2048, 512
T = B * S
KV = 77
E = 8
TOPK = 2
I = 2048
CAP = int(1.25 * ((T * TOPK + E - 1) // E))
HC = H // P
NT = T // P
GT = 4
NG = NT // GT
ST = CAP // P
DROPPED = 1 << 20
EPS = 1e-5
IC = 256
NI = IC // P
NCH = I // IC
BLOCKS = [(0, 512), (512, 512), (1024, 256)]
UNITS = NI * len(BLOCKS)
XPREP = 3
TAIL = 1024
PIECE = 8
NP = NT // PIECE
AHEAD = 2


def flamingo_layer(nc, x, ctx_in, g_xattn, g_ffn, Wq, bq, Wk, bk, Wv, bv, router, gate_w, up_w, down_w, out):
    xn2_rows = nc.dram_tensor("xn2_rows", (T, H), f32, kind="Internal").ap()
    x_v = x.rearrange("b (t p) h -> p (b t) h", p=P)
    out_v = out[0:T, :].rearrange("(t p) h -> p t h", p=P)
    xn2_v = xn2_rows.rearrange("(t p) h -> p t h", p=P)

    def row(v):
        return v.rearrange("(a n) -> a n", a=1)

    whole = ExitStack()
    with whole:
        def keeper(ctx):
            def sb(name, shape, dt=f32):
                return ctx.enter_context(nc.sbuf_tensor(name, shape, dt))

            def pb(name, shape, dt=f32):
                return ctx.enter_context(nc.psum_tensor(name, shape, dt))

            def sem(name):
                return ctx.enter_context(nc.semaphore(name))
            return sb, pb, sem

        sb, pb, sem = keeper(whole)
        waited = {name: sem(f"waited_{name}") for name in ("pool", "dve", "pe")}

        def wait_alone(eng, s, value):
            name = {nc.gpsimd.engine: "pool", nc.vector.engine: "dve", nc.tensor.engine: "pe"}[eng.engine]
            eng.wait_ge(s, value)
            eng.sem_inc(waited[name], 1)

        ident = sb("ident", [P, P])
        ffn_tanh = sb("ffn_tanh", [P, 1])
        gather_row = sb("gather_row", [P, (E + AHEAD) * ST], i32)
        scatter_row = sb("scatter_row", [P, (E + AHEAD) * ST], i32)
        slot_gate = sb("slot_gate", [P, (E + AHEAD) * ST])
        n_kept = sb("n_kept", [P, E], i32)
        pos = sb("pos", [P, (E + AHEAD) * NT])
        low = sb("low", [P, (E + AHEAD) * NT])
        gate_head = sb("gate_head", [P, (E + AHEAD) * NT], f32r)
        gate_rest = sb("gate_rest", [P, (E + AHEAD) * NT])
        token = sb("token", [P, NT])
        slot_no = sb("slot_no", [P, P])
        tile_edge = sb("tile_edge", [P, ST + 1])
        trash_row = sb("trash_row", [P, ST])
        at_least = sb("at_least", [P, PIECE, ST + 1])
        in_tile = sb("in_tile", [P, PIECE, ST])
        hot = sb("hot", [P, PIECE, P], f32r)
        facts = sb("facts", [P, PIECE, ST, 4], f32r)
        fact = sb("fact", [P, ST, 4])
        spare = sb("spare", [P, ST])
        marked, tallied, table_read = sem("marked"), sem("tallied"), sem("table_read")
        MARKS, READS = 7, 6

        def mark_piece(e, c, number):
            dve = nc.vector
            grid = [P, PIECE, ST]
            edges = [P, PIECE, ST + 1]
            at = e * NT + c * PIECE
            dve.wait_ge(tallied, number + 1)
            if not isinstance(number, int) or number > 0:
                dve.wait_ge(marked, number * MARKS)
            dve.tensor_tensor(hot[:, :, :], slot_no[:, :].unsqueeze(1).to_broadcast([P, PIECE, P]),
                              low[:, bass.ds(at, PIECE)].unsqueeze(2).to_broadcast([P, PIECE, P]),
                              ALU.is_equal).then_inc(marked, 1)
            dve.tensor_tensor(at_least[:, :, :], pos[:, bass.ds(at, PIECE)].unsqueeze(2).to_broadcast(edges),
                              tile_edge[:, :].unsqueeze(1).to_broadcast(edges), ALU.is_ge).then_inc(marked, 1)
            dve.wait_ge(marked, number * MARKS + 2)
            dve.tensor_tensor(in_tile[:, :, :], at_least[:, :, 0:ST], at_least[:, :, 1:ST + 1], ALU.subtract)\
               .then_inc(marked, 1)
            dve.wait_ge(marked, number * MARKS + 3)
            for n, fact in enumerate((token[:, bass.ds(c * PIECE, PIECE)],
                                      gate_head[:, bass.ds(at, PIECE)].bitcast(f32),
                                      gate_rest[:, bass.ds(at, PIECE)])):
                dve.tensor_tensor(facts[:, :, :, n], in_tile[:, :, :], fact.unsqueeze(2).to_broadcast(grid),
                                  ALU.mult).then_inc(marked, 1)
            dve.tensor_copy(facts[:, :, :, 3], in_tile[:, :, :]).then_inc(marked, 1)

        def tally_piece(bank, c, number):
            nc.tensor.wait_ge(marked, number * MARKS + MARKS)
            for t in range(PIECE):
                last = nc.tensor.matmul(bank[:, bass.ds(c * (ST * 4), ST * 4)], hot[:, t, :],
                                        facts[:, t, :, :].rearrange("p a c -> p (a c)"),
                                        start=(t == 0), stop=(t == PIECE - 1))
            last.then_inc(tallied, 1)

        def read_table(bank, e, number):
            dve = nc.vector
            at = bass.ds(e * ST, ST)
            dve.wait_ge(tallied, number * NP + NP + 1)
            if not isinstance(number, int) or number > 0:
                dve.wait_ge(table_read, number * READS)
            dve.tensor_reduce(fact[:, :, :].rearrange("p a c -> p (a c)"),
                              bank[:, 0:NP * ST * 4].rearrange("p (n f) -> p f n", n=NP), AX.X, ALU.add)\
               .then_inc(table_read, 1)
            dve.wait_ge(table_read, number * READS + 1)
            dve.tensor_copy(gather_row[:, at], fact[:, :, 0]).then_inc(table_read, 1)
            dve.tensor_tensor(spare[:, :], fact[:, :, 3], trash_row[:, :], ALU.mult).then_inc(table_read, 1)
            dve.tensor_tensor(slot_gate[:, at], fact[:, :, 1], fact[:, :, 2], ALU.add).then_inc(table_read, 1)
            dve.wait_ge(table_read, number * READS + 3)
            dve.tensor_tensor(spare[:, :], trash_row[:, :], spare[:, :], ALU.subtract).then_inc(table_read, 1)
            dve.wait_ge(table_read, number * READS + 5)
            dve.tensor_tensor(scatter_row[:, at], fact[:, :, 0], spare[:, :], ALU.add).then_inc(table_read, 1)

        w_raw = [sb(f"w_raw{c}", [P, 1024]) for c in range(3)]
        w_loaded = [sem(f"w_loaded{c}") for c in range(3)]

        def load_part(eng, e, c, part):
            if part < 2:
                src = (gate_w, up_w)[part][bass.ds(e, 1), :, bass.ds(c * IC, IC)].rearrange("a (k p) i -> p (a k) i", p=P)
                dst = w_raw[part][:, :].rearrange("p (k i) -> p k i", k=HC)
            else:
                src = down_w[bass.ds(e, 1), bass.ds(c * IC, IC), :].rearrange("a (k p) h -> p (a k) h", p=P)
                dst = w_raw[part][:, :].rearrange("p (k h) -> p k h", k=NI)
            eng.dma_start(dst, src).then_inc(w_loaded[part], 16)

        routing = whole.enter_context(ExitStack())
        sb, pb, sem = keeper(routing)
        logits = sb("logits", [P, NT, E])

        with ExitStack() as ctx:
            sb, pb, sem = keeper(ctx)
            XS = 4
            xg = [sb(f"xg{n}", [P, GT, H]) for n in range(XS)]
            xn = sb("xn", [P, GT, H])
            xnT = sb("xnT", [P, GT, HC, P])
            x1 = [sb(f"x1_{n}", [P, GT, H]) for n in range(2)]
            xn2 = [sb(f"xn2_{n}", [P, GT, H]) for n in range(2)]
            xn2T = sb("xn2T", [P, GT, HC, P])

            def pair(name, shape):
                return [sb(f"{name}_{n}", shape) for n in range(2)]

            stats, stats2 = pair("stats", [P, GT, 6]), pair("stats2", [P, GT, 6])
            mv, mv2 = pair("mv", [P, GT, 2]), pair("mv2", [P, GT, 2])
            veps, veps2 = pair("veps", [P, GT]), pair("veps2", [P, GT])
            negmean, negmean2 = pair("negmean", [P, GT]), pair("negmean2", [P, GT])
            rstd, rstd2 = pair("rstd", [P, GT]), pair("rstd2", [P, GT])
            shift, shift2 = pair("shift", [P, GT]), pair("shift2", [P, GT])
            half = sb("half", [P, GT])
            negmax, esum, rsum = pair("negmax", [P, GT]), pair("esum", [P, GT]), pair("rsum", [P, GT])
            ex = sb("ex", [P, GT, KV])
            exT = sb("exT", [KV, GT, P])
            Wq_s = sb("Wq_s", [P, HC, H])
            Wk_s = sb("Wk_s", [P, HC, H])
            Wv_s = sb("Wv_s", [P, HC, H])
            WqT = sb("WqT", [P, HC, H])
            R_s = sb("R_s", [P, HC, E])
            ctx_s = sb("ctx_s", [KV, B, H])
            ctxT = sb("ctxT", [P, HC, B * KV])
            KT = sb("KT", [P, HC, B * KV])
            A_s = sb("A_s", [P, HC, B * KV])
            V_s = sb("V_s", [KV, B, H])
            bias_s = sb("bias_s", [1, 3, H])
            bqT = sb("bqT", [P, HC])
            bqK = sb("bqK", [1, B * KV])
            ones = sb("ones", [1, B * KV])
            g_s = sb("g_s", [P, 2])
            v_scale = sb("v_scale", [P, 1])

            tp = [pb(f"tp{n}", [P, HC, P]) for n in range(2)]
            sc = [pb(f"sc{n}", [P, GT, P]) for n in range(2)]
            ep = pb("ep", [P, GT, P])
            op = [pb(f"op{n}", [P, H]) for n in range(2)]
            rt = pb("rt", [P, 512])[:, 0:GT * E].rearrange("p (t e) -> p t e", t=GT)

            ident_zero, ident_ready, ones_ready = sem("ident_zero"), sem("ident_ready"), sem("ones_ready")
            half_ready = sem("half_ready")
            k_in, q_in, v_in, small_in = sem("k_in"), sem("q_in"), sem("v_in"), sem("small_in")
            g_in, trash_filled, router_in = sem("g_in"), sem("trash_filled"), sem("router_in")
            pre_pe, pre_act = sem("pre_pe"), sem("pre_act")
            tanh_done, v_scale_ready = sem("tanh_done"), sem("v_scale_ready")
            x_in = [sem(f"x_in{n}") for n in range(XS)]
            stats_done, stats2_done = sem("stats_done"), sem("stats2_done")
            mv_done, mv2_done = sem("mv_done"), sem("mv2_done")
            veps_done, veps2_done = sem("veps_done"), sem("veps2_done")
            rstd_done, rstd2_done = sem("rstd_done"), sem("rstd2_done")
            shift_done, shift2_done = sem("shift_done"), sem("shift2_done")
            xn_ready, xn_transposed, xnT_ready = sem("xn_ready"), sem("xn_transposed"), sem("xnT_ready")
            scores_done, negmax_done, exp_done = sem("scores_done"), sem("negmax_done"), sem("exp_done")
            ex_transposed, exT_ready, rsum_done = sem("ex_transposed"), sem("exT_ready"), sem("rsum_done")
            attn_done, x1_done = sem("attn_done"), sem("x1_done")
            xn2_ready, xn2_transposed, xn2T_ready = sem("xn2_ready"), sem("xn2_transposed"), sem("xn2T_ready")
            logits_done, logits_copied = sem("logits_done"), sem("logits_copied")
            x1_stored = [sem(f"x1_stored{n}") for n in range(2)]
            xn2_stored = [sem(f"xn2_stored{n}") for n in range(2)]
            block = ctx.enter_context(nc.Block())

            STEPS = NG + 2

            def all_of(g):
                return (g + 1) * GT

            @block.sync
            def _(sp):
                sp.dma_start(ctx_s[:, :, :], ctx_in.rearrange("b k h -> k b h")).then_inc(small_in, 16)
                for n, v in enumerate((bq, bk, bv)):
                    sp.dma_start(bias_s[:, n, :], row(v)).then_inc(small_in, 16)
                sp.dma_start(g_s[:, 0:1], row(g_xattn).to_broadcast([P, 1])).then_inc(g_in, 16)
                sp.dma_start(g_s[:, 1:2], row(g_ffn).to_broadcast([P, 1])).then_inc(g_in, 16)
                sp.dma_start(xg[0][:, :, :], x_v[:, 0:GT, :]).then_inc(x_in[0], 16)
                sp.dma_start(Wk_s[:, :, :], Wk.rearrange("(k p) n -> p k n", p=P)).then_inc(k_in, 16)
                sp.dma_start(Wq_s[:, :, :], Wq.rearrange("(k p) n -> p k n", p=P)).then_inc(q_in, 16)
                sp.dma_start(Wv_s[:, :, :], Wv.rearrange("(k p) n -> p k n", p=P)).then_inc(v_in, 16)
                sp.dma_start(R_s[:, :, :], router.rearrange("(k p) n -> p k n", p=P)).then_inc(router_in, 16)
                for g in range(1, XS):
                    sp.dma_start(xg[g][:, :, :], x_v[:, g * GT:all_of(g), :]).then_inc(x_in[g], 16)
                sp.dma_start(out[T:T + CAP, :].rearrange("(p a) h -> p (a h)", p=P),
                             x.rearrange("b s h -> (b s) h")[0:CAP, :].rearrange("(p a) h -> p (a h)", p=P))\
                  .then_inc(trash_filled, 16)
                for g in range(NG):
                    tiles = slice(g * GT, all_of(g))
                    sp.wait_ge(x1_done, all_of(g))
                    sp.dma_start(out_v[:, tiles, :], x1[g % 2][:, :, :]).then_inc(x1_stored[g % 2], 16)
                    if g + XS < NG:
                        sp.dma_start(xg[g % XS][:, :, :], x_v[:, (g + XS) * GT:all_of(g + XS), :])\
                          .then_inc(x_in[g % XS], 16)
                    sp.wait_ge(xn2_ready, all_of(g))
                    sp.dma_start(xn2_v[:, tiles, :], xn2[g % 2][:, :, :]).then_inc(xn2_stored[g % 2], 16)
                for part in range(3):
                    load_part(sp, 0, 0, part)
                sp.wait_ge(trash_filled, 16)
                for n in range(2):
                    sp.wait_ge(x1_stored[n], 16 * (NG // 2))
                    sp.wait_ge(xn2_stored[n], 16 * (NG // 2))

            @block.gpsimd
            def _(pool):
                pool.memset(ident[:, :], 0.0).then_inc(ident_zero, 1)
                pool.memset(half[:, :], -0.5).then_inc(half_ready, 1)
                pool.memset(ones[:, :], 1.0).then_inc(ones_ready, 1)
                pool.wait_ge(ident_zero, 1)
                pool.affine_select(out=ident[:, :], in_=ident[:, :], compare_op=ALU.not_equal, fill=1.0,
                                   base=0, pattern=[[-1, P]], channel_multiplier=1).then_inc(ident_ready, 1)
                pool.wait_ge(half_ready, 1)
                def norm(g, mv, mv_done, veps, veps_done, negmean, rstd, rstd_done, shift, shift_done):
                    n = g % 2
                    pool.wait_ge(mv_done, all_of(g))
                    pool.tensor_scalar(veps[n][:, :], mv[n][:, :, 1], EPS, None, ALU.add).then_inc(veps_done, 1)
                    pool.tensor_scalar(negmean[n][:, :], mv[n][:, :, 0], -1.0, None, ALU.mult).then_inc(veps_done, 1)
                    pool.wait_ge(veps_done, 2 * g + 2)
                    pool.tensor_tensor(rstd[n][:, :], veps[n][:, :], half[:, :], ALU.pow).then_inc(rstd_done, 1)
                    pool.wait_ge(rstd_done, g + 1)
                    pool.tensor_tensor(shift[n][:, :], negmean[n][:, :], rstd[n][:, :], ALU.mult).then_inc(shift_done, 1)

                for s in range(-1, STEPS):
                    if 0 <= s - 1 < NG:
                        norm(s - 1, mv2, mv2_done, veps2, veps2_done, negmean2, rstd2, rstd2_done, shift2, shift2_done)
                    if 0 <= s + 1 < NG:
                        norm(s + 1, mv, mv_done, veps, veps_done, negmean, rstd, rstd_done, shift, shift_done)

            @block.vector
            def _(dve):
                dve.wait_ge(tanh_done, 1)
                nc.vector.tensor_scalar(v_scale[:, :], g_s[:, 0:1], float(H) ** -0.5, None, ALU.mult)\
                  .then_inc(v_scale_ready, 1)

                def statistics(g, src, stats, stats_done, mv, mv_done):
                    n = g % 2
                    for j in range(GT):
                        nc.vector.bn_stats(stats[n][:, j, :], src[:, j, :]).then_inc(stats_done, 1)
                    for j in range(GT):
                        dve.wait_ge(stats_done, g * GT + j + 1)
                        nc.vector.bn_aggr(mv[n][:, j, :], stats[n][:, j, :]).then_inc(mv_done, 1)

                def residual(g):
                    n = g % 2
                    dve.wait_ge(exp_done, all_of(g))
                    nc.vector.reciprocal(rsum[n][:, :], esum[n][:, :]).then_inc(rsum_done, 1)
                    dve.wait_ge(rsum_done, g + 1)
                    if g >= 2:
                        dve.wait_ge(x1_stored[n], 16 * (g // 2))
                        dve.wait_ge(xn2_ready, all_of(g - 2))
                    for j in range(GT):
                        dve.wait_ge(attn_done, g * GT + j + 1)
                        nc.vector.scalar_tensor_tensor(x1[n][:, j, :], op[j % 2][:, :], rsum[n][:, j:j + 1],
                                                       xg[g % XS][:, j, :], ALU.mult, ALU.add).then_inc(x1_done, 1)

                for s in range(-1, STEPS):
                    if 0 <= s - 1 < NG:
                        residual(s - 1)
                        dve.wait_ge(x1_done, all_of(s - 1))
                        statistics(s - 1, x1[(s - 1) % 2], stats2, stats2_done, mv2, mv2_done)
                    if 0 <= s < NG:
                        dve.wait_ge(scores_done, all_of(s))
                        nc.vector.tensor_reduce(negmax[s % 2][:, :], sc[s % 2][:, :, 0:KV], AX.X, ALU.max, negate=True)\
                          .then_inc(negmax_done, 1)
                    if 0 <= s + 1 < NG:
                        dve.wait_ge(x_in[(s + 1) % XS], 16 * ((s + 1) // XS + 1))
                        statistics(s + 1, xg[(s + 1) % XS], stats, stats_done, mv, mv_done)
                    if 0 <= s - 2 < NG:
                        dve.wait_ge(logits_done, all_of(s - 2))
                        nc.vector.tensor_copy(logits[:, (s - 2) * GT:all_of(s - 2), :], rt).then_inc(logits_copied, 1)

            @block.scalar
            def _(act):
                act.wait_ge(g_in, 32)
                nc.scalar.activation(g_s[:, 0:1], g_s[:, 0:1], ACT.Tanh).then_inc(tanh_done, 1)
                nc.scalar.activation(ffn_tanh[:, :], g_s[:, 1:2], ACT.Tanh)
                def normalise(g, src, shift, shift_done, rstd, dst, ready):
                    act.wait_ge(shift_done, g + 1)
                    for j in range(GT):
                        nc.scalar.activation(dst[:, j, :], src[:, j, :], ACT.Identity, bias=shift[g % 2][:, j:j + 1],
                                             scale=rstd[g % 2][:, j:j + 1]).then_inc(ready, 1)

                pre = [0]

                def evacuate(dst, src, scale=None):
                    pre[0] += 1
                    act.wait_ge(pre_pe, pre[0])
                    if scale is None:
                        nc.scalar.activation(dst, src, ACT.Copy).then_inc(pre_act, 1)
                    else:
                        nc.scalar.activation(dst, src, ACT.Copy, scale=scale).then_inc(pre_act, 1)

                for b in range(B):
                    evacuate(ctxT[:, :, b * KV:(b + 1) * KV], tp[b][:, :, 0:KV])
                evacuate(bqT[:, :], tp[0][:, 0, 0:HC])
                for d in range(HC):
                    evacuate(KT[:, d, :], tp[(d + 1) % 2][:, 0:2, :].rearrange("p a n -> p (a n)")[:, 0:B * KV])
                evacuate(bqK[:, :], tp[1][0:1, 0:2, :].rearrange("p a n -> p (a n)")[:, 0:B * KV])
                normalise(0, xg[0], shift, shift_done, rstd, xn, xn_ready)
                for d in range(HC):
                    evacuate(WqT[:, d, :], tp[d % 2][:, :, :].rearrange("p a n -> p (a n)"))
                for d in range(HC):
                    evacuate(A_s[:, d, :], tp[d % 2][:, 0:2, :].rearrange("p a n -> p (a n)")[:, 0:B * KV])
                act.wait_ge(v_scale_ready, 1)
                for b in range(B):
                    evacuate(V_s[:, b, :], tp[b][0:KV, :, :].rearrange("p a n -> p (a n)"), v_scale[0:KV, :])

                for s in range(STEPS):
                    if s < NG:
                        for j in range(GT):
                            act.wait_ge(xn_transposed, s * GT + j + 1)
                            nc.scalar.activation(xnT[:, j, :, :], tp[j % 2][:, :, :], ACT.Copy).then_inc(xnT_ready, 1)
                    if s >= 2:
                        for j in range(GT):
                            act.wait_ge(xn2_transposed, (s - 2) * GT + j + 1)
                            nc.scalar.activation(xn2T[:, j, :, :], tp[j % 2][:, :, :], ACT.Copy).then_inc(xn2T_ready, 1)
                    if s < NG:
                        n = s % 2
                        act.wait_ge(negmax_done, s + 1)
                        for j in range(GT):
                            nc.scalar.activation(ex[:, j, :], sc[n][:, j, 0:KV], ACT.Exp, bias=negmax[n][:, j:j + 1],
                                                 scale=1.0, accum_out=esum[n][:, j:j + 1]).then_inc(exp_done, 1)
                        act.wait_ge(ex_transposed, all_of(s))
                        nc.scalar.activation(exT[:, :, :], ep[0:KV, :, :], ACT.Copy).then_inc(exT_ready, 1)
                    if s + 1 < NG:
                        normalise(s + 1, xg[(s + 1) % XS], shift, shift_done, rstd, xn, xn_ready)
                    if 0 <= s - 1 < NG:
                        if s - 1 >= 2:
                            act.wait_ge(xn2_stored[(s - 1) % 2], 16 * ((s - 1) // 2))
                        normalise(s - 1, x1[(s - 1) % 2], shift2, shift2_done, rstd2, xn2[(s - 1) % 2], xn2_ready)

            @block.tensor
            def _(pe):
                pe.wait_ge(ident_ready, 1)
                pe.wait_ge(ones_ready, 1)
                pe.wait_ge(small_in, 16 * 4)
                done = [0]

                def bank_free(last_reader):
                    if last_reader > 0:
                        pe.wait_ge(pre_act, last_reader)

                def flat(n):
                    return tp[n][:, :, :].rearrange("p a n -> p (a n)")

                def ended(last):
                    last.then_inc(pre_pe, 1)
                    done[0] += 1

                for b in range(B):
                    for k in range(HC):
                        last = nc.tensor.transpose(tp[b][:, k, 0:KV], ctx_s[:, b, k * P:(k + 1) * P],
                                                   ident[0:KV, 0:KV])
                    ended(last)
                bank_free(done[0] - 1)
                for k in range(HC):
                    last = nc.tensor.matmul(tp[0][:, 0, k:k + 1], bias_s[0:1, 0, k * P:(k + 1) * P],
                                            ones[0:1, 0:1], start=True, stop=True)
                ended(last)
                pe.wait_ge(k_in, 16)
                for d in range(HC):
                    bank_free(done[0] - 1)
                    dst = flat((d + 1) % 2)[:, 0:B * KV]
                    for k in range(HC):
                        nc.tensor.matmul(dst, Wk_s[:, k, d * P:(d + 1) * P], ctxT[:, k, :], start=(k == 0), stop=False)
                    ended(nc.tensor.matmul(dst, bias_s[0:1, 1, d * P:(d + 1) * P], ones[:, :], start=False, stop=True))
                bank_free(done[0])
                for d in range(HC):
                    last = nc.tensor.matmul(flat(1)[0:1, 0:B * KV], bqT[:, d:d + 1], KT[:, d, :],
                                            start=(d == 0), stop=(d == HC - 1))
                ended(last)
                pe.wait_ge(q_in, 16)
                for d in range(HC):
                    bank_free(done[0] - 1)
                    for k in range(HC):
                        last = nc.tensor.transpose(tp[d % 2][:, k, :], Wq_s[:, k, d * P:(d + 1) * P], ident[:, :])
                    ended(last)
                bank_free(done[0])
                for h in range(HC):
                    bank_free(done[0] - 1)
                    for d in range(HC):
                        last = nc.tensor.matmul(flat(h % 2)[:, 0:B * KV], WqT[:, d, h * P:(h + 1) * P], KT[:, d, :],
                                                start=(d == 0), stop=(d == HC - 1))
                    ended(last)
                pe.wait_ge(v_in, 16)
                for b in range(B):
                    bank_free(done[0] - 1)
                    for k in range(HC):
                        nc.tensor.matmul(flat(b)[0:KV, :], ctxT[:, k, b * KV:(b + 1) * KV], Wv_s[:, k, :],
                                         start=(k == 0), stop=False)
                    ended(nc.tensor.matmul(flat(b)[0:KV, :], ones[0:1, 0:KV], bias_s[0:1, 2, :], start=False, stop=True))
                bank_free(done[0])
                pe.wait_ge(router_in, 16)

                def transpose(src, j, s):
                    for k in range(HC):
                        last = nc.tensor.transpose(tp[j % 2][:, k, :], src[:, j, k * P:(k + 1) * P], ident[:, :])
                    last.then_inc(s, 1)

                def scores(g, j):
                    batch = g // (NG // B)
                    keys = slice(batch * KV, (batch + 1) * KV)
                    pe.wait_ge(xnT_ready, g * GT + j + 1)
                    for k in range(HC):
                        nc.tensor.matmul(sc[g % 2][:, j, 0:KV], xnT[:, j, k, :], A_s[:, k, keys], start=(k == 0), stop=False)
                    nc.tensor.matmul(sc[g % 2][:, j, 0:KV], ones[0:1, 0:P], bqK[0:1, keys], start=False, stop=True)\
                      .then_inc(scores_done, 1)

                def attend(g, j):
                    pe.wait_ge(exT_ready, g + 1)
                    if g or j >= 2:
                        pe.wait_ge(x1_done, g * GT + j - 1)
                    nc.tensor.matmul(op[j % 2][:, :], exT[:, j, :], V_s[:, g // (NG // B), :], start=True, stop=True)\
                      .then_inc(attn_done, 1)

                for s in range(STEPS):
                    for j in range(GT):
                        if s < NG:
                            pe.wait_ge(xn_ready, s * GT + j + 1)
                            if j >= 2:
                                pe.wait_ge(xnT_ready, s * GT + j - 1)
                            transpose(xn, j, xn_transposed)
                        if 0 <= s - 1 < NG:
                            attend(s - 1, j)
                    for j in range(GT):
                        if s >= 2:
                            g = s - 2
                            pe.wait_ge(xn2_ready, g * GT + j + 1)
                            if j >= 2:
                                pe.wait_ge(xn2T_ready, g * GT + j - 1)
                            elif s < NG:
                                pe.wait_ge(xnT_ready, s * GT + j + 3)
                            transpose(xn2[g % 2], j, xn2_transposed)
                        if s < NG:
                            scores(s, j)
                    if s >= 2:
                        g = s - 2
                        if g:
                            pe.wait_ge(logits_copied, g)
                        for j in range(GT):
                            pe.wait_ge(xn2T_ready, g * GT + j + 1)
                            for k in range(HC):
                                last = nc.tensor.matmul(rt[:, j, :], xn2T[:, j, k, :], R_s[:, k, :],
                                                        start=(k == 0), stop=(k == HC - 1))
                            last.then_inc(logits_done, 1)
                    if s < NG:
                        for j in range(GT):
                            pe.wait_ge(exp_done, s * GT + j + 1)
                            nc.tensor.transpose(ep[0:KV, j, :], ex[:, j, :], ident[:, :]).then_inc(ex_transposed, 1)

        with ExitStack() as ctx:
            sb, pb, sem = keeper(ctx)
            TE = [P, NT, E]
            shifted = sb("shifted", TE)
            prob = sb("prob", TE)
            rest = sb("rest", TE)
            tie = sb("tie", TE)
            first_hot = sb("first_hot", TE)
            second_hot = sb("second_hot", TE)
            tmax = sb("tmax", [P, NT])
            psum_ = sb("psum_", [P, NT])
            prsum = sb("prsum", [P, NT])
            top1 = sb("top1", [P, NT])
            top2 = sb("top2", [P, NT])
            pick = sb("pick", [P, NT])
            wsum = sb("wsum", [P, NT])
            weight1 = sb("weight1", [P, NT])
            weight2 = sb("weight2", [P, NT])
            order = sb("order", [P, E])
            gates = sb("gates", [P, E, NT])
            kept = sb("kept", [P, E, NT], bf16)
            above = sb("above", [P, E, NT])
            level = sb("level", [P, E, NT])
            level_b = sb("level_b", [P, E, NT], bf16)
            room = sb("room", [P, E])
            n_above = sb("n_above", [P, E])
            before = sb("before", [P, P], bf16)
            all_ones = sb("all_ones", [P, P], bf16)
            scan = [sb(f"scan{n}", [P, E, 16 + NT]) for n in range(2)]
            counts = sb("counts", [P, E])
            most = sb("most", [P, 1])
            crowded = sb("crowded", [P, 1], i32)
            bit = sb("bit", [P, E], i32)
            reached = sb("reached", [P, E])
            found = sb("found", [P, E], i32)
            cut = sb("cut", [P, E], i32)
            trial = sb("trial", [P, E], i32)
            position = sb("position", [P, E, NT])
            drop = sb("drop", [P, E, NT])
            pos_i = sb("pos_i", [P, E, NT], i32)
            low_i = sb("low_i", [P, E, NT], i32)

            within = pb("within", [P, 2, E, NT])[:, 0, :, :]
            totals = pb("totals", [P, 2, E, NT])[:, 0, :, :]
            table = [pb(f"table{n}", [P, 512]) for n in range(2)]

            consts = sem("consts")
            exp_in, exp_out = sem("exp_in"), sem("exp_out")
            step = sem("step")
            kept_ready, counted = sem("kept_ready"), sem("counted")
            crowded_ready = sem("crowded_ready")
            trial_ready, trial_counted = sem("trial_ready"), sem("trial_counted")
            level_ready, level_counted = sem("level_ready"), sem("level_counted")
            block = ctx.enter_context(nc.Block())
            N_CONSTS = 14
            BITS = 30

            @block.gpsimd
            def _(pool):
                pool.memset(all_ones[:, :], 1.0).then_inc(consts, 1)
                pool.memset(before[:, :], 1.0).then_inc(consts, 1)
                pool.wait_ge(consts, 2)
                pool.affine_select(out=before[:, :], in_=before[:, :], compare_op=ALU.is_gt, fill=0.0,
                                   base=0, pattern=[[1, P]], channel_multiplier=-1).then_inc(consts, 1)
                pool.iota(order[:, :], [[-1, E]], base=E, channel_multiplier=0,
                          allow_small_or_imprecise_dtypes=True).then_inc(consts, 1)
                pool.iota(token[:, :], [[P, NT]], base=0, channel_multiplier=1,
                          allow_small_or_imprecise_dtypes=True).then_inc(consts, 1)
                pool.iota(slot_no[:, :], [[1, P]], base=0, channel_multiplier=0,
                          allow_small_or_imprecise_dtypes=True).then_inc(consts, 1)
                pool.iota(tile_edge[:, :], [[P, ST + 1]], base=0, channel_multiplier=0,
                          allow_small_or_imprecise_dtypes=True).then_inc(consts, 1)
                pool.iota(trash_row[:, :], [[P, ST]], base=T, channel_multiplier=1,
                          allow_small_or_imprecise_dtypes=True).then_inc(consts, 1)
                for n in range(2):
                    pool.memset(scan[n][:, :, 0:16], 0.0).then_inc(consts, 1)
                past = slice(E * NT, (E + AHEAD) * NT)
                pool.memset(pos[:, past], float(DROPPED)).then_inc(consts, 1)
                pool.memset(low[:, past], 0.0).then_inc(consts, 1)
                pool.memset(gate_head[:, past].bitcast(f32), 0.0).then_inc(consts, 1)
                pool.memset(gate_rest[:, past], 0.0).then_inc(consts, 1)

            @block.scalar
            def _(act):
                act.wait_ge(exp_in, 1)
                nc.scalar.activation(prob[:, :, :], shifted[:, :, :], ACT.Exp).then_inc(exp_out, 1)

            @block.vector
            def _(dve):
                chain = [0]

                def then(ins):
                    ins.then_inc(step, 1)
                    chain[0] += 1
                    dve.wait_ge(step, chain[0])

                def over_e(v):
                    return v.unsqueeze(2).to_broadcast(TE)

                dve.wait_ge(consts, N_CONSTS)
                lg = logits[:, :, :]
                then(nc.vector.tensor_reduce(tmax[:, :], lg, AX.X, ALU.max))
                nc.vector.tensor_tensor(shifted[:, :, :], lg, over_e(tmax[:, :]), ALU.subtract).then_inc(exp_in, 1)
                dve.wait_ge(exp_out, 1)
                then(nc.vector.tensor_reduce(psum_[:, :], prob[:, :, :], AX.X, ALU.add))
                then(nc.vector.reciprocal(prsum[:, :], psum_[:, :]))
                then(nc.vector.tensor_tensor(prob[:, :, :], prob[:, :, :], over_e(prsum[:, :]), ALU.mult))

                def top(values, best, hot_one):
                    then(nc.vector.tensor_reduce(best, values, AX.X, ALU.max))
                    then(nc.vector.tensor_tensor(tie[:, :, :], values, over_e(best), ALU.is_equal))
                    then(nc.vector.tensor_tensor(tie[:, :, :], tie[:, :, :], order[:, :].unsqueeze(1).to_broadcast(TE), ALU.mult))
                    then(nc.vector.tensor_reduce(pick[:, :], tie[:, :, :], AX.X, ALU.max))
                    then(nc.vector.tensor_tensor(hot_one, tie[:, :, :], over_e(pick[:, :]), ALU.is_equal))

                top(prob[:, :, :], top1[:, :], first_hot[:, :, :])
                then(nc.vector.scalar_tensor_tensor(rest[:, :, :], first_hot[:, :, :], -2.0, prob[:, :, :], ALU.mult, ALU.add))
                top(rest[:, :, :], top2[:, :], second_hot[:, :, :])
                then(nc.vector.scalar_tensor_tensor(wsum[:, :], top1[:, :], 1.0, top2[:, :], ALU.mult, ALU.add))
                then(nc.vector.tensor_scalar(wsum[:, :], wsum[:, :], 1e-9, None, ALU.add))
                then(nc.vector.reciprocal(wsum[:, :], wsum[:, :]))
                then(nc.vector.tensor_tensor(weight1[:, :], top1[:, :], wsum[:, :], ALU.mult))
                then(nc.vector.tensor_tensor(weight2[:, :], top2[:, :], wsum[:, :], ALU.mult))
                then(nc.vector.tensor_tensor(first_hot[:, :, :], first_hot[:, :, :], over_e(weight1[:, :]), ALU.mult))
                then(nc.vector.tensor_tensor(second_hot[:, :, :], second_hot[:, :, :], over_e(weight2[:, :]), ALU.mult))
                then(nc.vector.tensor_tensor(gates[:, :, :].rearrange("p e t -> p t e"), first_hot[:, :, :],
                                             second_hot[:, :, :], ALU.add))

                def running(dst, src):
                    then(nc.vector.tensor_copy(scan[0][:, :, 16:], src))
                    for k in range(5):
                        a, b = scan[k % 2], scan[(k + 1) % 2]
                        then(nc.vector.tensor_tensor(b[:, :, 16:], a[:, :, 16:], a[:, :, 16 - (1 << k):16 + NT - (1 << k)], ALU.add))
                    then(nc.vector.tensor_tensor(dst, scan[1][:, :, 16:], src, ALU.subtract))

                then(nc.vector.tensor_scalar(kept[:, :, :], gates[:, :, :], 0.0, None, ALU.is_gt))
                dve.sem_inc(kept_ready, 1)
                dve.wait_ge(counted, 1)
                then(nc.vector.tensor_reduce(counts[:, :], totals[:, :, :], AX.X, ALU.add))
                then(nc.vector.tensor_reduce(most[:, :], counts[:, :], AX.X, ALU.max))
                then(nc.vector.tensor_scalar(crowded[:, :], most[:, :], float(CAP), None, ALU.is_gt))
                dve.sem_inc(crowded_ready, 1)
                is_crowded = dve.value_load(crowded[0:1, 0:1], min_val=0, max_val=1)
                dve.nop()
                with dve.If(is_crowded == 1):
                    nc.vector.memset(cut[:, :], 0).then_inc(step, 1)
                    nc.vector.memset(bit[:, :], 1 << (BITS - 1)).then_inc(step, 1)
                    dve.wait_ge(step, chain[0] + 2)
                    base = chain[0] + 2
                    with dve.Fori(0, BITS) as r:
                        at = base + r * 7
                        nc.vector.tensor_tensor(trial[:, :], cut[:, :], bit[:, :], ALU.bitwise_or).then_inc(step, 1)
                        dve.wait_ge(step, at + 1)
                        nc.vector.tensor_tensor(kept[:, :, :], gates[:, :, :],
                                                trial[:, :].bitcast(f32).unsqueeze(2).to_broadcast([P, E, NT]),
                                                ALU.is_ge).then_inc(step, 1)
                        dve.wait_ge(step, at + 2)
                        dve.sem_inc(trial_ready, 1)
                        dve.wait_ge(trial_counted, r + 1)
                        nc.vector.tensor_reduce(reached[:, :], totals[:, :, :], AX.X, ALU.add).then_inc(step, 1)
                        dve.wait_ge(step, at + 3)
                        nc.vector.tensor_scalar(reached[:, :], reached[:, :], float(CAP), None, ALU.is_ge).then_inc(step, 1)
                        dve.wait_ge(step, at + 4)
                        nc.vector.tensor_tensor(found[:, :], reached[:, :], bit[:, :], ALU.mult).then_inc(step, 1)
                        dve.wait_ge(step, at + 5)
                        nc.vector.tensor_tensor(cut[:, :], cut[:, :], found[:, :], ALU.bitwise_or).then_inc(step, 1)
                        nc.vector.tensor_scalar(bit[:, :], bit[:, :], 1, None, ALU.logical_shift_right).then_inc(step, 1)
                        dve.wait_ge(step, at + 7)
                    chain[0] = base + BITS * 7
                    cut_f = cut[:, :].bitcast(f32).unsqueeze(2).to_broadcast([P, E, NT])
                    then(nc.vector.tensor_tensor(above[:, :, :], gates[:, :, :], cut_f, ALU.is_gt))
                    then(nc.vector.tensor_copy(kept[:, :, :], above[:, :, :]))
                    dve.sem_inc(trial_ready, 1)
                    dve.wait_ge(trial_counted, BITS + 1)
                    then(nc.vector.tensor_reduce(n_above[:, :], totals[:, :, :], AX.X, ALU.add))
                    then(nc.vector.tensor_scalar(room[:, :], n_above[:, :], -1.0, float(CAP), ALU.mult, ALU.add))
                    then(nc.vector.tensor_tensor(level[:, :, :], gates[:, :, :], cut_f, ALU.is_equal))
                    then(nc.vector.tensor_scalar(drop[:, :, :], gates[:, :, :], 0.0, None, ALU.is_gt))
                    then(nc.vector.tensor_tensor(level[:, :, :], level[:, :, :], drop[:, :, :], ALU.mult))
                    then(nc.vector.tensor_copy(kept[:, :, :], level[:, :, :]))
                    dve.sem_inc(trial_ready, 1)
                    dve.wait_ge(trial_counted, BITS + 2)
                    running(position[:, :, :], totals[:, :, :])
                    then(nc.vector.tensor_tensor(position[:, :, :], position[:, :, :], within[:, :, :], ALU.add))
                    then(nc.vector.tensor_tensor(position[:, :, :], position[:, :, :], room[:, :].unsqueeze(2).to_broadcast([P, E, NT]), ALU.is_lt))
                    then(nc.vector.tensor_tensor(level[:, :, :], level[:, :, :], position[:, :, :], ALU.mult))
                    then(nc.vector.tensor_tensor(kept[:, :, :], above[:, :, :], level[:, :, :], ALU.add))
                    dve.sem_inc(trial_ready, 1)
                    dve.wait_ge(trial_counted, BITS + 3)
                    end_of_search = chain[0]
                with dve.Else():
                    dve.sem_inc(step, end_of_search - (base - 2))
                dve.nop()

                live = slice(0, E * NT)

                def flat(v):
                    return v.rearrange("p e t -> p (e t)")

                running(position[:, :, :], totals[:, :, :])
                then(nc.vector.tensor_copy(n_kept[:, :], scan[1][:, :, 16 + NT - 1]))
                then(nc.vector.tensor_tensor(position[:, :, :], position[:, :, :], within[:, :, :], ALU.add))
                then(nc.vector.tensor_scalar(drop[:, :, :], kept[:, :, :], -float(DROPPED), float(DROPPED), ALU.mult, ALU.add))
                then(nc.vector.tensor_tensor(position[:, :, :], position[:, :, :], kept[:, :, :], ALU.mult))
                then(nc.vector.tensor_tensor(pos[:, live], flat(position[:, :, :]), flat(drop[:, :, :]), ALU.add))
                then(nc.vector.tensor_copy(flat(pos_i[:, :, :]), pos[:, live]))
                then(nc.vector.tensor_scalar(low_i[:, :, :], pos_i[:, :, :], P - 1, None, ALU.bitwise_and))
                then(nc.vector.tensor_copy(low[:, live], flat(low_i[:, :, :])))
                then(nc.vector.tensor_scalar(gates[:, :, :], gates[:, :, :], ffn_tanh[:, 0:1], None, ALU.mult))
                then(nc.vector.tensor_copy(gate_head[:, live], flat(gates[:, :, :])))
                then(nc.vector.tensor_tensor(gate_rest[:, live], flat(gates[:, :, :]), gate_head[:, live].bitcast(f32), ALU.subtract))
                dve.sem_inc(tallied, 1)
                for e in range(AHEAD):
                    for c in range(NP):
                        mark_piece(e, c, e * NP + c)
                for e in range(AHEAD):
                    read_table(table[e], e, e)

            @block.tensor
            def _(pe):
                pe.wait_ge(consts, N_CONSTS)
                kept_v = kept[:, :, :].rearrange("p e t -> p (e t)")

                def count():
                    nc.tensor.matmul(totals[:, :, :].rearrange("p e t -> p (e t)"), all_ones[:, :], kept_v, start=True, stop=True)
                    return nc.tensor.matmul(within[:, :, :].rearrange("p e t -> p (e t)"), before[:, :], kept_v, start=True, stop=True)

                pe.wait_ge(kept_ready, 1)
                count().then_inc(counted, 1)
                pe.wait_ge(crowded_ready, 1)
                is_crowded = pe.value_load(crowded[0:1, 0:1], min_val=0, max_val=1)
                pe.nop()
                with pe.If(is_crowded == 1):
                    with pe.Fori(0, BITS + 3) as r:
                        pe.wait_ge(trial_ready, r + 1)
                        count().then_inc(trial_counted, 1)
                pe.nop()
                for e in range(AHEAD):
                    for c in range(NP):
                        tally_piece(table[e], c, e * NP + c)

        routing.close()

        with ExitStack() as ctx:
            sb, pb, sem = keeper(ctx)
            wg_hd = [sb(f"wg_hd{n}", [P, HC, IC], f32r) for n in range(2)]
            wg_rs = [sb(f"wg_rs{n}", [P, HC, IC], f32r) for n in range(2)]
            wu_hd = [sb(f"wu_hd{n}", [P, HC, IC], f32r) for n in range(2)]
            wu_rs = [sb(f"wu_rs{n}", [P, HC, IC], f32r) for n in range(2)]
            wd_hd = [sb(f"wd_hd{n}", [P, NI, H], f32r) for n in range(2)]
            wd_rs = [sb(f"wd_rs{n}", [P, NI, H], f32r) for n in range(2)]
            xT_hd = [sb(f"xT_hd{n}", [P, HC, CAP], f32r) for n in range(2)]
            xT_rs = [sb(f"xT_rs{n}", [P, HC, CAP], f32r) for n in range(2)]
            xrow = [sb(f"xrow{n}", [P, H]) for n in range(XPREP)]
            h_hd = sb("h_hd", [P, NI, CAP], f32r)
            h_rs = sb("h_rs", [P, NI, CAP], f32r)
            silu = sb("silu", [P, 512])
            hfull = sb("hfull", [P, 512])
            y = sb("y", [P, ST, H])
            gate_now = sb("gate_now", [P, ST])
            gather_now = sb("gather_now", [P, XPREP], i32)
            scatter_now = sb("scatter_now", [P, ST], i32)
            heads = (wg_hd, wu_hd, wd_hd)
            rests = (wg_rs, wu_rs, wd_rs)

            pg = [pb(f"pg{n}", [P, 512]) for n in range(2)]
            pu = [pb(f"pu{n}", [P, 512]) for n in range(2)]
            py = [pb(f"py{n}", [P, H]) for n in range(2)]
            px = pb("px", [P, HC, P])
            table_bank = pb("table_bank", [P, 512])

            w_head_done, w_split = sem("w_head_done"), sem("w_split")
            row_in = [sem(f"row_in{n}") for n in range(XPREP)]
            row_transposed, xT_head_done, xT_split = sem("row_transposed"), sem("xT_head_done"), sem("xT_split")
            gate_done, up_done = sem("gate_done"), sem("up_done")
            tail_gate_done, tail_up_done = sem("tail_gate_done"), sem("tail_up_done")
            tail_down_done = [sem(f"tail_down_done{n}") for n in range(ST - TAIL // P)]
            silu_done, hfull_done, h_head_done, h_split = sem("silu_done"), sem("hfull_done"), sem("h_head_done"), sem("h_split")
            down_done, y_added, y_gated, y_scattered = sem("down_done"), sem("y_added"), sem("y_gated"), sem("y_scattered")
            gate_copied, index_copied = sem("gate_copied"), sem("index_copied")
            y_free = sem("y_free")
            block = ctx.enter_context(nc.Block())
            PAIRS = NCH // 2
            XE = PAIRS * XPREP

            def row_buffer(t):
                return (t - ST) % XPREP

            def row_count(t):
                return 16 * sum(row_buffer(u) == row_buffer(t) for u in range(t + 1))

            FIRST = [row_count(ST - XPREP + j) for j in range(XPREP)]

            def first_tile(k):
                return (k * 5) // 2

            UNIT = [(c0, w, it) for c0, w in BLOCKS for it in range(NI)]
            MAIN = [u for u in UNIT if u[0] < TAIL]
            TAILS = [u for u in UNIT if u[0] >= TAIL]
            NM, NTL = len(MAIN), len(TAILS)
            MT = TAIL // P

            @block.sync
            def _(sp):
                def fetch(e, c, number):
                    for part in range(3):
                        sp.wait_ge(w_split, number * 3 + (part - 2))
                        load_part(sp, e, c, part)

                fetch(0, 1, 1)
                with sp.Fori(1, PAIRS) as k:
                    for n in range(2):
                        fetch(0, k * 2 + n, k * 2 + n)
                with sp.Fori(1, E) as e:
                    with sp.Fori(0, PAIRS) as k:
                        for n in range(2):
                            fetch(e, k * 2 + n, e * NCH + k * 2 + n)
                fetch(E - 1, NCH - 1, E * NCH)

            @block.gpsimd
            def _(pool):
                for t in range(ST):
                    if t >= XPREP:
                        pool.wait_ge(row_transposed, t - XPREP + 1)
                    pool.indirect_dma_start(xrow[row_buffer(t)][:, :], None, xn2_rows,
                                            bass.IndirectOffsetOnAxis(ap=gather_row[:, t:t + 1], axis=0))\
                        .then_inc(row_in[row_buffer(t)], 16)
                pool.sem_inc(y_free, 1)

                def gather_pair(e, k, copies):
                    for j in range(XPREP):
                        pool.wait_ge(row_transposed, (e - 1) * XE + k * XPREP + (ST + j - XPREP + 1))
                        pool.tensor_copy(gather_now[:, j:j + 1], gather_row[:, bass.ds(e * ST + first_tile(k) + j, 1)])\
                            .then_inc(index_copied, 1)
                        wait_alone(pool, index_copied, copies + (j + 1))
                        pool.indirect_dma_start(xrow[j][:, :], None, xn2_rows,
                                                bass.IndirectOffsetOnAxis(ap=gather_now[:, j:j + 1], axis=0))\
                            .then_inc(row_in[j], 16)

                gather_pair(1, 0, 0)
                with pool.Fori(0, E) as e:
                    with pool.Fori(1, PAIRS) as k:
                        gather_pair(e + 1, k, e * (XE + 1) + k * XPREP)
                    wait_alone(pool, table_read, e * READS + (AHEAD + 1) * READS)
                    gather_pair(e + 2, 0, e * (XE + 1) + XE)
                    pool.tensor_copy(scatter_now[:, :], scatter_row[:, bass.ds(e * ST, ST)]).then_inc(index_copied, 1)
                    pool.wait_ge(index_copied, e * (XE + 1) + (XE + XPREP + 1))
                    for t in range(ST):
                        wait_alone(pool, y_gated, e * ST + (t + 1))
                        pool.indirect_dma_start(out, bass.IndirectOffsetOnAxis(ap=scatter_now[:, t:t + 1], axis=0),
                                                y[:, t, :], None, compute_op=ALU.add).then_inc(y_scattered, 16)
                    pool.wait_ge(y_scattered, e * (ST * 16) + ST * 16)
                    pool.sem_inc(y_free, 1)

            @block.scalar
            def _(act):
                def split_weights(n, c, loaded):
                    act.wait_ge(w_loaded[c], loaded)
                    nc.scalar.activation(heads[c][n][:, :, :].rearrange("p a b -> p (a b)"), w_raw[c][:, :],
                                         ACT.Copy).then_inc(w_head_done, 1)

                def head_of_rows(par, t, number):
                    act.wait_ge(row_transposed, number)
                    nc.scalar.activation(xT_hd[par][:, :, bass.ds(t * P, P)], px[:, :, :], ACT.Copy)\
                      .then_inc(xT_head_done, 1)

                def silu_and_head(q, gate_ready, number, c0, width, it):
                    b = q % 2
                    act.wait_ge(*gate_ready)
                    nc.scalar.activation(silu[:, 0:width], pg[b][:, 0:width], ACT.Silu).then_inc(silu_done, 1)
                    act.wait_ge(hfull_done, number + 2)
                    nc.scalar.activation(h_hd[:, it, c0:c0 + width], hfull[:, 0:width], ACT.Copy)\
                      .then_inc(h_head_done, 1)

                for c in range(3):
                    split_weights(0, c, 16)
                for t in range(ST):
                    head_of_rows(0, t, t + 1)
                with act.Fori(0, E // 2) as p:
                    for par in range(2):
                        e = p * 2 + par
                        with act.Fori(0, PAIRS) as k:
                            m = e * PAIRS + k
                            for w in range(2):
                                u0 = m * (2 * UNITS) + w * UNITS
                                for q, (c0, width, it) in enumerate(UNIT):
                                    if q < NM:
                                        ready = (gate_done, m * (2 * NM) + (w * NM + q + 1))
                                    else:
                                        ready = (tail_gate_done, m * (2 * NTL) + (w * NTL + q - NM + 1))
                                    silu_and_head(q, ready, u0 + (q + 1), c0, width, it)
                                    if q < 3:
                                        split_weights(1 - w, q, m * 32 + (32 + 16 * w))
                                    if w == 0 and q < XPREP:
                                        head_of_rows(1 - par, first_tile(k) + q, m * XPREP + (ST + q + 1))
                        nc.scalar.activation(gate_now[:, :], slot_gate[:, bass.ds(e * ST, ST)], ACT.Copy)\
                          .then_inc(gate_copied, 1)
                        act.wait_ge(gate_copied, e + 1)
                        for t in range(ST):
                            act.wait_ge(y_added, e * (NCH * ST) + ((NCH - 1) * ST + t + 2))
                            nc.scalar.activation(y[:, t, :], y[:, t, :], ACT.Copy, scale=gate_now[:, t:t + 1])\
                              .then_inc(y_gated, 1)

            @block.vector
            def _(dve):
                def rest_of_weights(n, c, number):
                    dve.wait_ge(w_head_done, number)
                    nc.vector.tensor_tensor(rests[c][n][:, :, :].rearrange("p a b -> p (a b)"), w_raw[c][:, :],
                                            heads[c][n][:, :, :].rearrange("p a b -> p (a b)").bitcast(f32),
                                            ALU.subtract).then_inc(w_split, 1)

                def rest_of_rows(par, t, number):
                    dve.wait_ge(xT_head_done, number)
                    nc.vector.tensor_tensor(xT_rs[par][:, :, bass.ds(t * P, P)], px[:, :, :],
                                            xT_hd[par][:, :, bass.ds(t * P, P)].bitcast(f32), ALU.subtract)\
                      .then_inc(xT_split, 1)

                def product(q, up_ready, number, c0, width, it):
                    dve.wait_ge(*up_ready)
                    dve.wait_ge(silu_done, number)
                    dve.wait_ge(h_split, number)
                    nc.vector.tensor_tensor(hfull[:, 0:width], silu[:, 0:width], pu[q % 2][:, 0:width],
                                            ALU.mult).then_inc(hfull_done, 1)

                def rest_of_h(q, up_ready, number, c0, width, it):
                    dve.wait_ge(h_head_done, number)
                    nc.vector.tensor_tensor(h_rs[:, it, c0:c0 + width], hfull[:, 0:width],
                                            h_hd[:, it, c0:c0 + width].bitcast(f32), ALU.subtract)\
                      .then_inc(h_split, 1)

                dve.sem_inc(y_added, 1)
                dve.sem_inc(hfull_done, 2)
                dve.sem_inc(h_split, 1)
                for c in range(3):
                    rest_of_weights(0, c, c + 1)
                for t in range(ST):
                    rest_of_rows(0, t, t + 1)
                with dve.Fori(0, E // 2) as p:
                    for par in range(2):
                        e = p * 2 + par
                        with dve.Fori(0, PAIRS) as k:
                            m = e * PAIRS + k
                            for w in range(2):
                                u0 = m * (2 * UNITS) + w * UNITS
                                unit = [(q, (up_done, m * (2 * NM) + (w * NM + q + 1)) if q < NM else
                                         (tail_up_done, m * (2 * NTL) + (w * NTL + q - NM + 1)), u0 + (q + 1)) + u
                                        for q, u in enumerate(UNIT)]
                                for q in range(NM):
                                    product(*unit[q])
                                    if q < NM - 1:
                                        rest_of_h(*unit[q])
                                        rest_of_weights(1 - w, q, m * 6 + (3 * w + 4 + q))
                                    if w == 0 and q < XPREP:
                                        rest_of_rows(1 - par, first_tile(k) + q, m * XPREP + (ST + q + 1))

                                between = {0: (rest_of_h, NM - 1), 1: (product, NM), 2: (rest_of_h, NM),
                                           3: (product, NM + 1), 4: (rest_of_h, NM + 1)}

                                def sums(anew):
                                    for t in range(ST):
                                        if t < MT:
                                            dve.wait_ge(down_done, m * (2 * MT) + (w * MT + t + 1))
                                        else:
                                            dve.wait_ge(tail_down_done[t - MT], m * 2 + (w + 1))
                                        if anew:
                                            nc.vector.tensor_copy(y[:, t, :], py[t % 2][:, :]).then_inc(y_added, 1)
                                        else:
                                            nc.vector.tensor_tensor(y[:, t, :], py[t % 2][:, :], y[:, t, :], ALU.add)\
                                              .then_inc(y_added, 1)
                                        if t in between:
                                            what, q = between[t]
                                            what(*unit[q])

                                if w == 0:
                                    dve.nop()
                                    with dve.If(k == 0):
                                        dve.wait_ge(y_free, e + 1)
                                        sums(True)
                                    with dve.Else():
                                        sums(False)
                                    dve.nop()
                                    mark_piece(e + AHEAD, k, (e + AHEAD) * NP + k)
                                else:
                                    sums(False)
                        read_table(table_bank, e + AHEAD, e + AHEAD)

            @block.tensor
            def _(pe):
                def transpose_rows(j):
                    for k in range(HC):
                        last = nc.tensor.transpose(px[:, k, :], xrow[j][:, k * P:(k + 1) * P], ident[:, :])
                    last.then_inc(row_transposed, 1)

                def three_passes(dst, pairs):
                    last = None
                    for n, ((lhd, lrs), (rhd, rrs)) in enumerate(pairs):
                        nc.tensor.matmul(dst, lhd, rhd, start=(n == 0), stop=False)
                        nc.tensor.matmul(dst, lhd, rrs, start=False, stop=False)
                        last = nc.tensor.matmul(dst, lrs, rhd, start=False, stop=(n == len(pairs) - 1))
                    return last

                def gate_and_up(q, w, par, u0, c0, width, it, gate_sem, up_sem):
                    pe.wait_ge(hfull_done, u0 + (q + 1))
                    ic = slice(it * P, (it + 1) * P)
                    for (hd, rs), dst, s in (((wg_hd, wg_rs), pg, gate_sem), ((wu_hd, wu_rs), pu, up_sem)):
                        three_passes(dst[q % 2][:, 0:width],
                                     [((hd[w][:, c, ic], rs[w][:, c, ic]),
                                       (xT_hd[par][:, c, c0:c0 + width], xT_rs[par][:, c, c0:c0 + width]))
                                      for c in range(HC)]).then_inc(s, 1)

                def down(t, w, y0, s):
                    pe.wait_ge(y_added, y0 + max(t, 1))
                    sl = slice(t * P, (t + 1) * P)
                    three_passes(py[t % 2][:, :],
                                 [((h_hd[:, it, sl], h_rs[:, it, sl]), (wd_hd[w][:, it, :], wd_rs[w][:, it, :]))
                                  for it in range(NI)]).then_inc(s, 1)

                for t in range(ST):
                    pe.wait_ge(row_in[row_buffer(t)], row_count(t))
                    if t >= 1:
                        pe.wait_ge(xT_split, t)
                    transpose_rows(row_buffer(t))
                with pe.Fori(0, E // 2) as p:
                    for par in range(2):
                        e = p * 2 + par
                        filled = pe.value_load(n_kept[0:1, bass.ds(e, 1)], min_val=0, max_val=T)
                        wait_alone(pe, xT_split, e * XE + ST)
                        with pe.Fori(0, PAIRS) as k:
                            m = e * PAIRS + k
                            for w in range(2):
                                u0 = m * (2 * UNITS) + w * UNITS
                                y0 = m * (2 * ST) + w * ST
                                pe.wait_ge(w_split, m * 6 + (3 * w + 3))
                                for q, (c0, width, it) in enumerate(MAIN):
                                    gate_and_up(q, w, par, u0, c0, width, it, gate_done, up_done)
                                    if w == 0 and q < XPREP:
                                        j = q
                                        pe.wait_ge(row_in[j], m * 16 + (FIRST[j] + 16))
                                        pe.wait_ge(xT_split, m * XPREP + (ST + j))
                                        transpose_rows(j)
                                    if w == 1 and q == 0:
                                        tally_piece(table_bank, k, (e + AHEAD) * NP + k)

                                def tail_units(width):
                                    for n, (c0, _, it) in enumerate(TAILS):
                                        gate_and_up(NM + n, w, par, u0, c0, width, it, tail_gate_done, tail_up_done)

                                pe.nop()
                                with pe.If(filled > TAIL + P):
                                    tail_units(2 * P)
                                with pe.Else():
                                    pe.nop()
                                    with pe.If(filled > TAIL):
                                        tail_units(P)
                                    with pe.Else():
                                        pe.sem_inc(tail_gate_done, NTL)
                                        pe.sem_inc(tail_up_done, NTL)
                                    pe.nop()
                                pe.nop()
                                for t in range(MT):
                                    for n, (c0, _) in enumerate(BLOCKS):
                                        if c0 == t * P:
                                            pe.wait_ge(h_split, u0 + (n + 1) * NI + 1)
                                    down(t, w, y0, down_done)
                                pe.nop()
                                with pe.If(filled > TAIL):
                                    pe.wait_ge(h_split, u0 + UNITS + 1)
                                    down(MT, w, y0, tail_down_done[0])
                                with pe.Else():
                                    pe.sem_inc(tail_down_done[0], 1)
                                pe.nop()
                                with pe.If(filled > TAIL + P):
                                    down(MT + 1, w, y0, tail_down_done[1])
                                with pe.Else():
                                    pe.sem_inc(tail_down_done[1], 1)
                                pe.nop()


_INS = ['x', 'ctx_1024', 'g_xattn', 'g_ffn', 'L0_xattn_Wq', 'L0_xattn_bq', 'L0_xattn_Wk', 'L0_xattn_bk',
        'L0_xattn_Wv', 'L0_xattn_bv', 'L0_ffn_router_gate', 'L0_ffn_gate_w', 'L0_ffn_up_w', 'L0_ffn_down_w']


def kernel(**inputs):
    import numpy as _np
    import concourse.bacc as _bacc
    from concourse import mybir as _mybir
    from concourse.bass_utils import run_bass_kernel_spmd as _run

    nc = _bacc.Bacc("TRN2", target_bir_lowering=False, num_devices=1)
    arrays, args = {}, []
    for name in _INS:
        a = _np.ascontiguousarray(inputs[name])
        arrays[f"in_{name}_dram"] = a
        args.append(nc.dram_tensor(f"in_{name}_dram", a.shape, _mybir.dt.from_np(a.dtype), kind="ExternalInput").ap())
    args.append(nc.dram_tensor("out_dram", (T + CAP, H), _mybir.dt.float32, kind="ExternalOutput").ap())
    flamingo_layer(nc, *args)
    r = _run(nc, [arrays], core_ids=[0])
    return r.results[0]["out_dram"][:T].reshape(B, S, H)
```

```python
import concourse.bass as bass
from concourse import mybir
from contextlib import ExitStack

f32 = mybir.dt.float32
f32r = mybir.dt.float32r
bf16 = mybir.dt.bfloat16
i32 = mybir.dt.int32
ALU = mybir.AluOpType
ACT = mybir.ActivationFunctionType
AX = mybir.AxisListType

P = 128
B, S, H = 2, 2048, 512
T = B * S
KV = 77
E = 8
TOPK = 2
I = 2048
CAP = int(1.25 * ((T * TOPK + E - 1) // E))
HC = H // P
NT = T // P
GT = 4
NG = NT // GT
ST = CAP // P
DROPPED = 1 << 20
EPS = 1e-5
IC = 256
NI = IC // P
NCH = I // IC
BLOCKS = [(0, 512), (512, 512), (1024, 256)]
UNITS = NI * len(BLOCKS)
XPREP = 3
TAIL = 1024
STEP = 16
LEAST = 384
PIECE = 8
NP = NT // PIECE
GATHERS_EARLY = 4
AHEAD = 2


def flamingo_layer(nc, x, ctx_in, g_xattn, g_ffn, Wq, bq, Wk, bk, Wv, bv, router, gate_w, up_w, down_w, out):
    xn2_rows = nc.dram_tensor("xn2_rows", (T, H), f32, kind="Internal").ap()
    x_v = x.rearrange("b (t p) h -> p (b t) h", p=P)
    out_v = out[0:T, :].rearrange("(t p) h -> p t h", p=P)
    xn2_v = xn2_rows.rearrange("(t p) h -> p t h", p=P)

    def row(v):
        return v.rearrange("(a n) -> a n", a=1)

    whole = ExitStack()
    with whole:
        def keeper(ctx):
            def sb(name, shape, dt=f32):
                return ctx.enter_context(nc.sbuf_tensor(name, shape, dt))

            def pb(name, shape, dt=f32):
                return ctx.enter_context(nc.psum_tensor(name, shape, dt))

            def sem(name):
                return ctx.enter_context(nc.semaphore(name))
            return sb, pb, sem

        sb, pb, sem = keeper(whole)
        waited = {name: sem(f"waited_{name}") for name in ("pool", "dve", "pe", "act")}

        def wait_alone(eng, s, value):
            name = {nc.gpsimd.engine: "pool", nc.vector.engine: "dve", nc.tensor.engine: "pe",
                    nc.scalar.engine: "act"}[eng.engine]
            eng.wait_ge(s, value)
            eng.sem_inc(waited[name], 1)

        ident = sb("ident", [P, P])
        ffn_tanh = sb("ffn_tanh", [P, 1])
        gather_row = sb("gather_row", [P, (E + AHEAD) * ST], i32)
        scatter_row = sb("scatter_row", [P, (E + AHEAD) * ST], i32)
        slot_gate = sb("slot_gate", [P, (E + AHEAD) * ST])
        n_kept = sb("n_kept", [P, E], i32)
        tail_at = sb("tail_at", [P, E], i32)
        pos = sb("pos", [P, (E + AHEAD) * NT])
        low = sb("low", [P, (E + AHEAD) * NT])
        gate_head = sb("gate_head", [P, (E + AHEAD) * NT], f32r)
        gate_rest = sb("gate_rest", [P, (E + AHEAD) * NT])
        token = sb("token", [P, NT])
        slot_no = sb("slot_no", [P, P])
        tile_edge = sb("tile_edge", [P, ST + 1])
        trash_row = sb("trash_row", [P, ST])
        at_least = sb("at_least", [P, PIECE, ST + 1])
        in_tile = sb("in_tile", [P, PIECE, ST])
        hot = sb("hot", [P, PIECE, P], f32r)
        facts = sb("facts", [P, PIECE, ST, 4], f32r)
        fact = sb("fact", [P, ST, 4])
        spare = sb("spare", [P, ST])
        tallied_1 = sem("tallied_1")
        marked, tallied, table_read = sem("marked"), sem("tallied"), sem("table_read")
        MARKS, READS = 7, 6

        def mark_piece(e, c, number, hot, facts, buffers=1):
            dve = nc.vector
            grid = [P, PIECE, ST]
            edges = [P, PIECE, ST + 1]
            at = e * NT + c * PIECE
            if not isinstance(number, int) or number >= buffers:
                dve.wait_ge(tallied, number + (2 - buffers))
            if not isinstance(number, int) or number > 0:
                dve.wait_ge(marked, number * MARKS)
            dve.tensor_tensor(hot[:, :, :], slot_no[:, :].unsqueeze(1).to_broadcast([P, PIECE, P]),
                              low[:, bass.ds(at, PIECE)].unsqueeze(2).to_broadcast([P, PIECE, P]),
                              ALU.is_equal).then_inc(marked, 1)
            dve.tensor_tensor(at_least[:, :, :], pos[:, bass.ds(at, PIECE)].unsqueeze(2).to_broadcast(edges),
                              tile_edge[:, :].unsqueeze(1).to_broadcast(edges), ALU.is_ge).then_inc(marked, 1)
            dve.wait_ge(marked, number * MARKS + 2)
            dve.tensor_tensor(in_tile[:, :, :], at_least[:, :, 0:ST], at_least[:, :, 1:ST + 1], ALU.subtract)\
               .then_inc(marked, 1)
            dve.wait_ge(marked, number * MARKS + 3)
            for n, fact in enumerate((token[:, bass.ds(c * PIECE, PIECE)],
                                      gate_head[:, bass.ds(at, PIECE)].bitcast(f32),
                                      gate_rest[:, bass.ds(at, PIECE)])):
                dve.tensor_tensor(facts[:, :, :, n], in_tile[:, :, :], fact.unsqueeze(2).to_broadcast(grid),
                                  ALU.mult).then_inc(marked, 1)
            dve.tensor_copy(facts[:, :, :, 3], in_tile[:, :, :]).then_inc(marked, 1)

        def tally_marks(bank, c, hot, facts, tallied):
            for t in range(PIECE):
                last = nc.tensor.matmul(bank[:, bass.ds(c * (ST * 4), ST * 4)], hot[:, t, :],
                                        facts[:, t, :, :].rearrange("p a c -> p (a c)"),
                                        start=(t == 0), stop=(t == PIECE - 1))
            last.then_inc(tallied, 1)

        def tally_piece(bank, c, number, hot, facts):
            nc.tensor.wait_ge(marked, number * MARKS + MARKS)
            tally_marks(bank, c, hot, facts, tallied)

        def read_table(bank, e, number):
            dve = nc.vector
            at = bass.ds(e * ST, ST)
            if isinstance(number, int) and number == 0:
                dve.wait_ge(tallied, NP + 1)
            elif isinstance(number, int) and number == 1:
                dve.wait_ge(tallied_1, NP)
            else:
                dve.wait_ge(tallied, number * NP + 1)
            if not isinstance(number, int) or number > 0:
                dve.wait_ge(table_read, number * READS)
            dve.tensor_reduce(fact[:, :, :].rearrange("p a c -> p (a c)"),
                              bank[:, 0:NP * ST * 4].rearrange("p (n f) -> p f n", n=NP), AX.X, ALU.add)\
               .then_inc(table_read, 1)
            dve.wait_ge(table_read, number * READS + 1)
            dve.tensor_copy(gather_row[:, at], fact[:, :, 0]).then_inc(table_read, 1)
            dve.tensor_tensor(spare[:, :], fact[:, :, 3], trash_row[:, :], ALU.mult).then_inc(table_read, 1)
            dve.tensor_tensor(slot_gate[:, at], fact[:, :, 1], fact[:, :, 2], ALU.add).then_inc(table_read, 1)
            dve.wait_ge(table_read, number * READS + 3)
            dve.tensor_tensor(spare[:, :], trash_row[:, :], spare[:, :], ALU.subtract).then_inc(table_read, 1)
            dve.wait_ge(table_read, number * READS + 5)
            dve.tensor_tensor(scatter_row[:, at], fact[:, :, 0], spare[:, :], ALU.add).then_inc(table_read, 1)

        y = sb("y", [P, ST, H])
        first_row_in = [sem(f"first_row_in{t}") for t in range(ST)]

        def gather_first(t):
            nc.gpsimd.indirect_dma_start(y[:, t, :], None, xn2_rows,
                                         bass.IndirectOffsetOnAxis(ap=gather_row[:, t:t + 1], axis=0))\
              .then_inc(first_row_in[t], 16)

        w_raw = [sb(f"w_raw{c}", [P, 1024]) for c in range(3)]
        w_loaded = [sem(f"w_loaded{c}") for c in range(3)]

        def load_part(eng, e, c, part):
            if part < 2:
                src = (gate_w, up_w)[part][bass.ds(e, 1), :, bass.ds(c * IC, IC)].rearrange("a (k p) i -> p (a k) i", p=P)
                dst = w_raw[part][:, :].rearrange("p (k i) -> p k i", k=HC)
            else:
                src = down_w[bass.ds(e, 1), bass.ds(c * IC, IC), :].rearrange("a (k p) h -> p (a k) h", p=P)
                dst = w_raw[part][:, :].rearrange("p (k h) -> p k h", k=NI)
            eng.dma_start(dst, src).then_inc(w_loaded[part], 16)

        routing = whole.enter_context(ExitStack())
        sb, pb, sem = keeper(routing)
        logits = sb("logits", [P, NT, E])

        with ExitStack() as ctx:
            sb, pb, sem = keeper(ctx)
            XS = 4
            xg = [sb(f"xg{n}", [P, GT, H]) for n in range(XS)]
            xn = sb("xn", [P, GT, H])
            xnT = sb("xnT", [P, GT, HC, P])
            x1 = [sb(f"x1_{n}", [P, GT, H]) for n in range(2)]
            xn2 = [sb(f"xn2_{n}", [P, GT, H]) for n in range(2)]
            xn2T = sb("xn2T", [P, GT, HC, P])

            def pair(name, shape):
                return [sb(f"{name}_{n}", shape) for n in range(2)]

            stats, stats2 = pair("stats", [P, GT, 6]), pair("stats2", [P, GT, 6])
            mv, mv2 = pair("mv", [P, GT, 2]), pair("mv2", [P, GT, 2])
            veps, veps2 = pair("veps", [P, GT]), pair("veps2", [P, GT])
            negmean, negmean2 = pair("negmean", [P, GT]), pair("negmean2", [P, GT])
            rstd, rstd2 = pair("rstd", [P, GT]), pair("rstd2", [P, GT])
            shift, shift2 = pair("shift", [P, GT]), pair("shift2", [P, GT])
            half = sb("half", [P, GT])
            negmax, esum, rsum = pair("negmax", [P, GT]), pair("esum", [P, GT]), pair("rsum", [P, GT])
            biased = pair("biased", [P, GT, KV])
            ex = sb("ex", [P, GT, KV])
            exT = sb("exT", [KV, GT, P])
            logitsT = sb("logitsT", [E, GT, P])
            Wq_s = sb("Wq_s", [P, HC, H])
            Wk_s = sb("Wk_s", [P, HC, H])
            Wv_s = sb("Wv_s", [P, HC, H])
            WqT = sb("WqT", [P, HC, H])
            R_s = sb("R_s", [P, HC, E])
            ctx_s = sb("ctx_s", [KV, B, H])
            ctxT = sb("ctxT", [P, HC, B * KV])
            KT = sb("KT", [P, HC, B * KV])
            A_s = sb("A_s", [P, HC, B * KV])
            V_s = sb("V_s", [KV, B, H])
            bias_s = sb("bias_s", [1, 3, H])
            bqT = sb("bqT", [P, HC])
            bqK = sb("bqK", [P, B * KV])
            ones = sb("ones", [1, B * KV])
            g_s = sb("g_s", [P, 2])
            v_scale = sb("v_scale", [P, 1])

            tp = [pb(f"tp{n}", [P, HC, P]) for n in range(2)]
            sc = [pb(f"sc{n}", [P, GT, P]) for n in range(2)]
            ep = pb("ep", [P, GT, P])
            op = [pb(f"op{n}", [P, H]) for n in range(2)]
            rt = pb("rt", [P, 512])[:, 0:GT * E].rearrange("p (t e) -> p t e", t=GT)

            ident_zero, ident_ready, ones_ready = sem("ident_zero"), sem("ident_ready"), sem("ones_ready")
            half_ready = sem("half_ready")
            k_in, q_in, v_in, small_in = sem("k_in"), sem("q_in"), sem("v_in"), sem("small_in")
            g_in, trash_filled, router_in = sem("g_in"), sem("trash_filled"), sem("router_in")
            made, copied_act, copied_dve = sem("made"), sem("copied_act"), sem("copied_dve")
            tanh_done, v_scale_ready = sem("tanh_done"), sem("v_scale_ready")
            x_in = [sem(f"x_in{n}") for n in range(XS)]
            stats_done, stats2_done = sem("stats_done"), sem("stats2_done")
            mv_done, mv2_done = sem("mv_done"), sem("mv2_done")
            veps_done, veps2_done = sem("veps_done"), sem("veps2_done")
            rstd_done, rstd2_done = sem("rstd_done"), sem("rstd2_done")
            shift_done, shift2_done = sem("shift_done"), sem("shift2_done")
            xn_ready, xn_transposed, xnT_ready = sem("xn_ready"), sem("xn_transposed"), sem("xnT_ready")
            scores_done, bias_added = sem("scores_done"), sem("bias_added")
            negmax_done, exp_done = sem("negmax_done"), sem("exp_done")
            ex_transposed, exT_ready, rsum_done = sem("ex_transposed"), sem("exT_ready"), sem("rsum_done")
            attn_done, x1_done = sem("attn_done"), sem("x1_done")
            xn2_ready, xn2_transposed, xn2T_ready = sem("xn2_ready"), sem("xn2_transposed"), sem("xn2T_ready")
            logitsT_done, logitsT_copied = sem("logitsT_done"), sem("logitsT_copied")
            logits_done, logits_copied = sem("logits_done"), sem("logits_copied")
            x1_stored = [sem(f"x1_stored{n}") for n in range(2)]
            xn2_stored = [sem(f"xn2_stored{n}") for n in range(2)]
            block = ctx.enter_context(nc.Block())

            STEPS = NG + 4

            CTX_T, BQ_T, K_T = 0, B, B + 1
            WQ_T = K_T + HC
            BQ_K = WQ_T + HC
            A_ = BQ_K + 1
            V_ = A_ + HC
            ring = [op[0], op[1], sc[0].rearrange("p a n -> p (a n)"), sc[1].rearrange("p a n -> p (a n)")]

            def bank(i, cols, rows=P):
                return ring[i % 4][0:rows, 0:cols]

            def all_of(g):
                return (g + 1) * GT

            @block.sync
            def _(sp):
                sp.dma_start(ctx_s[:, :, :], ctx_in.rearrange("b k h -> k b h")).then_inc(small_in, 16)
                sp.dma_start(Wk_s[:, :, :], Wk.rearrange("(k p) n -> p k n", p=P)).then_inc(k_in, 16)
                for n, v in enumerate((bq, bk, bv)):
                    sp.dma_start(bias_s[:, n, :], row(v)).then_inc(small_in, 16)
                sp.dma_start(g_s[:, 0:1], row(g_xattn).to_broadcast([P, 1])).then_inc(g_in, 16)
                sp.dma_start(g_s[:, 1:2], row(g_ffn).to_broadcast([P, 1])).then_inc(g_in, 16)
                sp.dma_start(Wq_s[:, :, :], Wq.rearrange("(k p) n -> p k n", p=P)).then_inc(q_in, 16)
                sp.dma_start(xg[0][:, :, :], x_v[:, 0:GT, :]).then_inc(x_in[0], 16)
                sp.dma_start(Wv_s[:, :, :], Wv.rearrange("(k p) n -> p k n", p=P)).then_inc(v_in, 16)
                sp.dma_start(R_s[:, :, :], router.rearrange("(k p) n -> p k n", p=P)).then_inc(router_in, 16)
                for g in range(1, XS):
                    sp.dma_start(xg[g][:, :, :], x_v[:, g * GT:all_of(g), :]).then_inc(x_in[g], 16)
                sp.dma_start(out[T:T + CAP, :].rearrange("(p a) h -> p (a h)", p=P),
                             x.rearrange("b s h -> (b s) h")[0:CAP, :].rearrange("(p a) h -> p (a h)", p=P))\
                  .then_inc(trash_filled, 16)
                for g in range(NG):
                    tiles = slice(g * GT, all_of(g))
                    sp.wait_ge(x1_done, all_of(g))
                    sp.dma_start(out_v[:, tiles, :], x1[g % 2][:, :, :]).then_inc(x1_stored[g % 2], 16)
                    if g + XS < NG:
                        sp.dma_start(xg[g % XS][:, :, :], x_v[:, (g + XS) * GT:all_of(g + XS), :])\
                          .then_inc(x_in[g % XS], 16)
                    sp.wait_ge(xn2_ready, all_of(g))
                    sp.dma_start(xn2_v[:, tiles, :], xn2[g % 2][:, :, :]).then_inc(xn2_stored[g % 2], 16)
                for part in range(3):
                    load_part(sp, 0, 0, part)
                sp.wait_ge(trash_filled, 16)
                for n in range(2):
                    sp.wait_ge(x1_stored[n], 16 * (NG // 2))
                    sp.wait_ge(xn2_stored[n], 16 * (NG // 2))

            @block.gpsimd
            def _(pool):
                pool.memset(ident[:, :], 0.0).then_inc(ident_zero, 1)
                pool.memset(half[:, :], -0.5).then_inc(half_ready, 1)
                pool.memset(ones[:, :], 1.0).then_inc(ones_ready, 1)
                pool.wait_ge(ident_zero, 1)
                pool.affine_select(out=ident[:, :], in_=ident[:, :], compare_op=ALU.not_equal, fill=1.0,
                                   base=0, pattern=[[-1, P]], channel_multiplier=1).then_inc(ident_ready, 1)
                pool.wait_ge(half_ready, 1)
                def norm(g, mv, mv_done, veps, veps_done, negmean, rstd, rstd_done, shift, shift_done):
                    n = g % 2
                    pool.wait_ge(mv_done, all_of(g))
                    pool.tensor_scalar(veps[n][:, :], mv[n][:, :, 1], EPS, None, ALU.add).then_inc(veps_done, 1)
                    pool.tensor_scalar(negmean[n][:, :], mv[n][:, :, 0], -1.0, None, ALU.mult).then_inc(veps_done, 1)
                    pool.wait_ge(veps_done, 2 * g + 2)
                    pool.tensor_tensor(rstd[n][:, :], veps[n][:, :], half[:, :], ALU.pow).then_inc(rstd_done, 1)
                    pool.wait_ge(rstd_done, g + 1)
                    pool.tensor_tensor(shift[n][:, :], negmean[n][:, :], rstd[n][:, :], ALU.mult).then_inc(shift_done, 1)

                for s in range(-1, STEPS):
                    if 0 <= s + 1 < NG:
                        norm(s + 1, mv, mv_done, veps, veps_done, negmean, rstd, rstd_done, shift, shift_done)
                    if 0 <= s - 1 < NG:
                        norm(s - 1, mv2, mv2_done, veps2, veps2_done, negmean2, rstd2, rstd2_done, shift2, shift2_done)

            @block.vector
            def _(dve):
                def copy_out(i, dst, src):
                    dve.wait_ge(made, i + 1)
                    nc.vector.tensor_copy(dst, src).then_inc(copied_dve, 1)

                def statistics(g, src, stats, stats_done, mv, mv_done):
                    n = g % 2
                    for j in range(GT):
                        nc.vector.bn_stats(stats[n][:, j, :], src[:, j, :]).then_inc(stats_done, 1)
                    for j in range(GT):
                        dve.wait_ge(stats_done, g * GT + j + 1)
                        nc.vector.bn_aggr(mv[n][:, j, :], stats[n][:, j, :]).then_inc(mv_done, 1)

                def residual(g):
                    n = g % 2
                    dve.wait_ge(exp_done, all_of(g))
                    nc.vector.reciprocal(rsum[n][:, :], esum[n][:, :]).then_inc(rsum_done, 1)
                    dve.wait_ge(rsum_done, g + 1)
                    if g >= 2:
                        dve.wait_ge(x1_stored[n], 16 * (g // 2))
                        dve.wait_ge(xn2_ready, all_of(g - 2))
                    for j in range(GT):
                        dve.wait_ge(attn_done, g * GT + j + 1)
                        nc.vector.scalar_tensor_tensor(x1[n][:, j, :], op[j % 2][:, :], rsum[n][:, j:j + 1],
                                                       xg[g % XS][:, j, :], ALU.mult, ALU.add).then_inc(x1_done, 1)

                for i in range(K_T + HC + 2):
                    if i == K_T + HC:
                        dve.wait_ge(tanh_done, 1)
                        nc.vector.tensor_scalar(v_scale[:, :], g_s[:, 0:1], float(H) ** -0.5, None, ALU.mult)\
                          .then_inc(v_scale_ready, 1)
                    if i % 2 == 0:
                        continue
                    if i < BQ_T:
                        b = i - CTX_T
                        copy_out(i, ctxT[:, :, b * KV:(b + 1) * KV],
                                 bank(i, HC * P).rearrange("p (k n) -> p k n", k=HC)[:, :, 0:KV])
                    elif i < WQ_T:
                        copy_out(i, KT[:, i - K_T, :], bank(i, B * KV))
                    else:
                        copy_out(i, WqT[:, i - WQ_T, :], bank(i, H))

                for s in range(-1, STEPS):
                    if 0 <= s + 1 < NG:
                        dve.wait_ge(x_in[(s + 1) % XS], 16 * ((s + 1) // XS + 1))
                        statistics(s + 1, xg[(s + 1) % XS], stats, stats_done, mv, mv_done)
                    if s == -1:
                        for i in range(WQ_T + 2, V_):
                            if i % 2 == 0:
                                continue
                            if i < BQ_K:
                                copy_out(i, WqT[:, i - WQ_T, :], bank(i, H))
                            elif i == BQ_K:
                                copy_out(i, bqK[:, :], bank(i, B * KV))
                            else:
                                copy_out(i, A_s[:, i - A_, :], bank(i, B * KV))
                    if 0 <= s - 4 < NG:
                        dve.wait_ge(logits_done, all_of(s - 4))
                        nc.vector.tensor_copy(logits[:, (s - 4) * GT:all_of(s - 4), :], rt).then_inc(logits_copied, 1)
                    if 0 <= s < NG:
                        batch = s // (NG // B)
                        dve.wait_ge(scores_done, all_of(s))
                        nc.vector.tensor_tensor(biased[s % 2][:, :, :], sc[s % 2][:, :, 0:KV],
                                                bqK[:, batch * KV:(batch + 1) * KV].unsqueeze(1).to_broadcast([P, GT, KV]),
                                                ALU.add).then_inc(bias_added, 1)
                        dve.wait_ge(bias_added, s + 1)
                        nc.vector.tensor_reduce(negmax[s % 2][:, :], biased[s % 2][:, :, :], AX.X, ALU.max, negate=True)\
                          .then_inc(negmax_done, 1)
                    if s == 0:
                        dve.wait_ge(v_scale_ready, 1)
                        dve.wait_ge(made, V_ + 2)
                        nc.vector.tensor_scalar(V_s[:, 1, :], bank(V_ + 1, H, KV), v_scale[0:KV, 0:1], None, ALU.mult)\
                          .then_inc(copied_dve, 1)
                    if 0 <= s - 1 < NG:
                        residual(s - 1)
                        dve.wait_ge(x1_done, all_of(s - 1))
                        statistics(s - 1, x1[(s - 1) % 2], stats2, stats2_done, mv2, mv2_done)

            @block.scalar
            def _(act):
                act.wait_ge(g_in, 32)
                nc.scalar.activation(g_s[:, 0:1], g_s[:, 0:1], ACT.Tanh).then_inc(tanh_done, 1)
                nc.scalar.activation(ffn_tanh[:, :], g_s[:, 1:2], ACT.Tanh)
                def normalise(g, src, shift, shift_done, rstd, dst, ready):
                    act.wait_ge(shift_done, g + 1)
                    for j in range(GT):
                        nc.scalar.activation(dst[:, j, :], src[:, j, :], ACT.Identity, bias=shift[g % 2][:, j:j + 1],
                                             scale=rstd[g % 2][:, j:j + 1]).then_inc(ready, 1)

                def copy_out(i, dst, src):
                    act.wait_ge(made, i + 1)
                    nc.scalar.activation(dst, src, ACT.Copy).then_inc(copied_act, 1)

                for i in range(0, V_, 2):
                    if i < BQ_T:
                        b = i - CTX_T
                        copy_out(i, ctxT[:, :, b * KV:(b + 1) * KV],
                                 bank(i, HC * P).rearrange("p (k n) -> p k n", k=HC)[:, :, 0:KV])
                    elif i == BQ_T:
                        copy_out(i, bqT[:, :], bank(i, HC))
                    elif i < WQ_T:
                        copy_out(i, KT[:, i - K_T, :], bank(i, B * KV))
                    elif i < BQ_K:
                        copy_out(i, WqT[:, i - WQ_T, :], bank(i, H))
                    else:
                        if i == A_:
                            normalise(0, xg[0], shift, shift_done, rstd, xn, xn_ready)
                        copy_out(i, A_s[:, i - A_, :], bank(i, B * KV))

                for s in range(STEPS):
                    if s >= 4:
                        act.wait_ge(logitsT_done, s - 3)
                        nc.scalar.activation(logitsT[:, :, :], ep[0:E, :, :], ACT.Copy).then_inc(logitsT_copied, 1)
                    if s < NG:
                        for j in range(GT):
                            act.wait_ge(xn_transposed, s * GT + j + 1)
                            nc.scalar.activation(xnT[:, j, :, :], tp[j % 2][:, :, :], ACT.Copy).then_inc(xnT_ready, 1)
                    if 0 <= s - 1 < NG:
                        act.wait_ge(ex_transposed, all_of(s - 1))
                        nc.scalar.activation(exT[:, :, :], ep[0:KV, :, :], ACT.Copy).then_inc(exT_ready, 1)
                    if 3 <= s < NG + 3:
                        for j in range(GT):
                            act.wait_ge(xn2_transposed, (s - 3) * GT + j + 1)
                            nc.scalar.activation(xn2T[:, j, :, :], tp[j % 2][:, :, :], ACT.Copy).then_inc(xn2T_ready, 1)
                    if 0 <= s - 2 < NG:
                        if s - 2 >= 2:
                            act.wait_ge(xn2_stored[s % 2], 16 * ((s - 2) // 2))
                        normalise(s - 2, x1[s % 2], shift2, shift2_done, rstd2, xn2[s % 2], xn2_ready)
                    if s < NG:
                        n = s % 2
                        act.wait_ge(negmax_done, s + 1)
                        for j in range(GT):
                            nc.scalar.activation(ex[:, j, :], biased[n][:, j, :], ACT.Exp, bias=negmax[n][:, j:j + 1],
                                                 scale=1.0, accum_out=esum[n][:, j:j + 1]).then_inc(exp_done, 1)
                    if s + 1 < NG:
                        normalise(s + 1, xg[(s + 1) % XS], shift, shift_done, rstd, xn, xn_ready)
                    if s == 0:
                        act.wait_ge(v_scale_ready, 1)
                        act.wait_ge(made, V_ + 1)
                        nc.scalar.activation(V_s[:, 0, :], bank(V_, H, KV), ACT.Copy, scale=v_scale[0:KV, :])\
                          .then_inc(copied_act, 1)

            @block.tensor
            def _(pe):
                pe.wait_ge(ident_ready, 1)
                pe.wait_ge(ones_ready, 1)
                pe.wait_ge(small_in, 16 * 4)
                def copied(i):
                    pe.wait_ge(copied_dve if i % 2 else copied_act, i // 2 + 1)

                def free(i):
                    if i >= 4:
                        copied(i - 4)

                for b in range(B):
                    for k in range(HC):
                        last = nc.tensor.transpose(bank(CTX_T + b, HC * P)[:, k * P:k * P + KV],
                                                   ctx_s[:, b, k * P:(k + 1) * P], ident[0:KV, 0:KV])
                    last.then_inc(made, 1)
                for k in range(HC):
                    last = nc.tensor.matmul(bank(BQ_T, HC)[:, k:k + 1], bias_s[0:1, 0, k * P:(k + 1) * P],
                                            ones[0:1, 0:1], start=True, stop=True)
                last.then_inc(made, 1)
                for b in range(B):
                    copied(CTX_T + b)
                pe.wait_ge(k_in, 16)
                for d in range(HC):
                    free(K_T + d)
                    dst = bank(K_T + d, B * KV)
                    for k in range(HC):
                        nc.tensor.matmul(dst, Wk_s[:, k, d * P:(d + 1) * P], ctxT[:, k, :], start=(k == 0), stop=False)
                    nc.tensor.matmul(dst, bias_s[0:1, 1, d * P:(d + 1) * P], ones[:, :], start=False, stop=True)\
                      .then_inc(made, 1)
                pe.wait_ge(q_in, 16)
                for d in range(HC):
                    free(WQ_T + d)
                    for k in range(HC):
                        last = nc.tensor.transpose(bank(WQ_T + d, H)[:, k * P:(k + 1) * P],
                                                   Wq_s[:, k, d * P:(d + 1) * P], ident[:, :])
                    last.then_inc(made, 1)
                free(BQ_K)
                copied(BQ_T)
                copied(K_T + HC - 2)
                copied(K_T + HC - 1)
                for d in range(HC):
                    last = nc.tensor.matmul(bank(BQ_K, B * KV), bqT[:, d:d + 1].to_broadcast([P, P]), KT[:, d, :],
                                            start=(d == 0), stop=(d == HC - 1))
                last.then_inc(made, 1)
                copied(WQ_T + HC - 2)
                copied(WQ_T + HC - 1)
                for h in range(HC):
                    free(A_ + h)
                    for d in range(HC):
                        last = nc.tensor.matmul(bank(A_ + h, B * KV), WqT[:, d, h * P:(h + 1) * P], KT[:, d, :],
                                                start=(d == 0), stop=(d == HC - 1))
                    last.then_inc(made, 1)

                def transpose(src, j, s):
                    for k in range(HC):
                        last = nc.tensor.transpose(tp[j % 2][:, k, :], src[:, j, k * P:(k + 1) * P], ident[:, :])
                    last.then_inc(s, 1)

                def scores(g, j):
                    batch = g // (NG // B)
                    keys = slice(batch * KV, (batch + 1) * KV)
                    pe.wait_ge(xnT_ready, g * GT + j + 1)
                    for k in range(HC):
                        last = nc.tensor.matmul(sc[g % 2][:, j, 0:KV], xnT[:, j, k, :], A_s[:, k, keys],
                                                start=(k == 0), stop=(k == HC - 1))
                    last.then_inc(scores_done, 1)

                def attend(g, j):
                    pe.wait_ge(exT_ready, g + 1)
                    if g or j >= 2:
                        pe.wait_ge(x1_done, g * GT + j - 1)
                    nc.tensor.matmul(op[j % 2][:, :], exT[:, j, :], V_s[:, g // (NG // B), :], start=True, stop=True)\
                      .then_inc(attn_done, 1)

                def values():
                    pe.wait_ge(v_in, 16)
                    for b in range(B):
                        free(V_ + b)
                        dst = bank(V_ + b, H, KV)
                        for k in range(HC):
                            nc.tensor.matmul(dst, ctxT[:, k, b * KV:(b + 1) * KV], Wv_s[:, k, :],
                                             start=(k == 0), stop=False)
                        nc.tensor.matmul(dst, ones[0:1, 0:KV], bias_s[0:1, 2, :], start=False, stop=True)\
                          .then_inc(made, 1)

                for s in range(STEPS):
                    if s < NG:
                        for j in range(GT):
                            pe.wait_ge(xn_ready, s * GT + j + 1)
                            if j >= 2:
                                pe.wait_ge(xnT_ready, s * GT + j - 1)
                            elif s >= 4:
                                pe.wait_ge(xn2T_ready, (s - 4) * GT + j + 3)
                            elif s >= 1:
                                pe.wait_ge(xnT_ready, (s - 1) * GT + j + 3)
                            transpose(xn, j, xn_transposed)
                    if 0 <= s - 1 < NG:
                        if s >= 4:
                            pe.wait_ge(logitsT_copied, s - 3)
                        for j in range(GT):
                            pe.wait_ge(exp_done, (s - 1) * GT + j + 1)
                            nc.tensor.transpose(ep[0:KV, j, :], ex[:, j, :], ident[:, :]).then_inc(ex_transposed, 1)
                    if s >= 4:
                        pe.wait_ge(logitsT_copied, s - 3)
                        if s >= 5:
                            pe.wait_ge(logits_copied, s - 4)
                        for j in range(GT):
                            nc.tensor.transpose(rt[:, j, :], logitsT[:, j, :], ident[0:E, 0:E]).then_inc(logits_done, 1)
                    if s == 0:
                        copied(V_ - 2)
                        copied(V_ - 1)
                        pe.wait_ge(router_in, 16)
                    for j in range(GT):
                        if 3 <= s < NG + 3:
                            g = s - 3
                            pe.wait_ge(xn2_ready, g * GT + j + 1)
                            if j >= 2:
                                pe.wait_ge(xn2T_ready, g * GT + j - 1)
                            elif s < NG:
                                pe.wait_ge(xnT_ready, s * GT + j + 3)
                            else:
                                pe.wait_ge(xn2T_ready, (g - 1) * GT + j + 3)
                            transpose(xn2[g % 2], j, xn2_transposed)
                        if s < NG:
                            scores(s, j)
                    if s == 0:
                        values()
                        copied(V_)
                        copied(V_ + 1)
                    if 0 <= s - 1 < NG:
                        for j in range(GT):
                            attend(s - 1, j)
                    if 3 <= s < NG + 3:
                        pe.wait_ge(exT_ready, min(s, NG))
                        pe.wait_ge(xn2T_ready, all_of(s - 3))
                        if s >= 4:
                            pe.wait_ge(logitsT_copied, s - 3)
                        for k in range(HC):
                            last = nc.tensor.matmul(ep[0:E, :, :], R_s[:, k, :], xn2T[:, :, k, :],
                                                    start=(k == 0), stop=(k == HC - 1))
                        last.then_inc(logitsT_done, 1)

        with ExitStack() as ctx:
            sb, pb, sem = keeper(ctx)
            TE = [P, NT, E]
            shifted = sb("shifted", TE)
            prob = sb("prob", TE)
            rest = sb("rest", TE)
            tie = sb("tie", TE)
            first_hot = sb("first_hot", TE)
            second_hot = sb("second_hot", TE)
            tmax = sb("tmax", [P, NT])
            psum_ = sb("psum_", [P, NT])
            prsum = sb("prsum", [P, NT])
            top1 = sb("top1", [P, NT])
            top2 = sb("top2", [P, NT])
            pick = sb("pick", [P, NT])
            wsum = sb("wsum", [P, NT])
            weight1 = sb("weight1", [P, NT])
            weight2 = sb("weight2", [P, NT])
            order = sb("order", [P, E])
            gates = sb("gates", [P, E, NT])
            kept = sb("kept", [P, E, NT], bf16)
            above = sb("above", [P, E, NT])
            level = sb("level", [P, E, NT])
            level_b = sb("level_b", [P, E, NT], bf16)
            room = sb("room", [P, E])
            n_above = sb("n_above", [P, E])
            before = sb("before", [P, P], bf16)
            all_ones = sb("all_ones", [P, P], bf16)
            scan = [sb(f"scan{n}", [P, E, 16 + NT]) for n in range(2)]
            counts = sb("counts", [P, E])
            most = sb("most", [P, 1])
            crowded = sb("crowded", [P, 1], i32)
            bit = sb("bit", [P, E], i32)
            reached = sb("reached", [P, E])
            found = sb("found", [P, E], i32)
            cut = sb("cut", [P, E], i32)
            trial = sb("trial", [P, E], i32)
            position = sb("position", [P, E, NT])
            drop = sb("drop", [P, E, NT])
            pos_i = sb("pos_i", [P, E, NT], i32)
            low_i = sb("low_i", [P, E, NT], i32)
            hot_of = [hot, sb("hot_odd", [P, PIECE, P], f32r)]
            facts_of = [facts, sb("facts_odd", [P, PIECE, ST, 4], f32r)]
            hot_1 = sb("hot_1", [P, NT, P], f32r)
            apart = [sb(f"apart{n}", [P, PIECE, P]) for n in range(2)]
            facts_1 = sb("facts_1", [P, NT, ST, 4], f32r)
            at_least_1 = sb("at_least_1", [P, NT, ST + 1])
            in_tile_1 = sb("in_tile_1", [P, NT, ST])
            one = sb("one", [P, 1])
            apart_done, hot_1_done = sem("apart_done"), sem("hot_1_done")
            at_least_1_done, facts_1_done = sem("at_least_1_done"), sem("facts_1_done")
            rounded_i = sb("rounded_i", [P, E], i32)
            rounded = sb("rounded", [P, E])
            has_tail = sb("has_tail", [P, E])
            marks_ready = sem("marks_ready")

            within = pb("within", [P, 2, E, NT])[:, 0, :, :]
            totals = pb("totals", [P, 2, E, NT])[:, 0, :, :]
            table = [pb(f"table{n}", [P, 512]) for n in range(2)]

            consts = sem("consts")
            exp_in, exp_out = sem("exp_in"), sem("exp_out")
            step = sem("step")
            kept_ready, counted = sem("kept_ready"), sem("counted")
            crowded_ready = sem("crowded_ready")
            trial_ready, trial_counted = sem("trial_ready"), sem("trial_counted")
            level_ready, level_counted = sem("level_ready"), sem("level_counted")
            block = ctx.enter_context(nc.Block())
            N_CONSTS = 15
            BITS = 30

            @block.gpsimd
            def _(pool):
                pool.memset(all_ones[:, :], 1.0).then_inc(consts, 1)
                pool.memset(before[:, :], 1.0).then_inc(consts, 1)
                pool.wait_ge(consts, 2)
                pool.affine_select(out=before[:, :], in_=before[:, :], compare_op=ALU.is_gt, fill=0.0,
                                   base=0, pattern=[[1, P]], channel_multiplier=-1).then_inc(consts, 1)
                pool.iota(order[:, :], [[-1, E]], base=E, channel_multiplier=0,
                          allow_small_or_imprecise_dtypes=True).then_inc(consts, 1)
                pool.iota(token[:, :], [[P, NT]], base=0, channel_multiplier=1,
                          allow_small_or_imprecise_dtypes=True).then_inc(consts, 1)
                pool.iota(slot_no[:, :], [[1, P]], base=0, channel_multiplier=0,
                          allow_small_or_imprecise_dtypes=True).then_inc(consts, 1)
                pool.iota(tile_edge[:, :], [[P, ST + 1]], base=0, channel_multiplier=0,
                          allow_small_or_imprecise_dtypes=True).then_inc(consts, 1)
                pool.iota(trash_row[:, :], [[P, ST]], base=T, channel_multiplier=1,
                          allow_small_or_imprecise_dtypes=True).then_inc(consts, 1)
                pool.memset(one[:, :], 1.0).then_inc(consts, 1)
                for n in range(2):
                    pool.memset(scan[n][:, :, 0:16], 0.0).then_inc(consts, 1)
                past = slice(E * NT, (E + AHEAD) * NT)
                pool.memset(pos[:, past], float(DROPPED)).then_inc(consts, 1)
                pool.memset(low[:, past], 0.0).then_inc(consts, 1)
                pool.memset(gate_head[:, past].bitcast(f32), 0.0).then_inc(consts, 1)
                pool.memset(gate_rest[:, past], 0.0).then_inc(consts, 1)
                pool.wait_ge(marks_ready, 1)
                pool.wait_ge(at_least_1_done, 1)
                pool.tensor_tensor(in_tile_1[:, :, :], at_least_1[:, :, 0:ST], at_least_1[:, :, 1:ST + 1], ALU.subtract)\
                    .then_inc(facts_1_done, 1)
                pool.wait_ge(facts_1_done, 1)
                for n, fact in enumerate((token[:, :], gate_head[:, NT:2 * NT].bitcast(f32), gate_rest[:, NT:2 * NT])):
                    pool.tensor_tensor(facts_1[:, :, :, n], in_tile_1[:, :, :],
                                       fact.unsqueeze(2).to_broadcast([P, NT, ST]), ALU.mult).then_inc(facts_1_done, 1)
                pool.tensor_copy(facts_1[:, :, :, 3], in_tile_1[:, :, :]).then_inc(facts_1_done, 1)
                pool.wait_ge(table_read, READS)
                for t in range(GATHERS_EARLY):
                    gather_first(t)

            @block.scalar
            def _(act):
                act.wait_ge(exp_in, 1)
                nc.scalar.activation(prob[:, :, :], shifted[:, :, :], ACT.Exp).then_inc(exp_out, 1)
                act.wait_ge(marks_ready, 1)
                act.wait_ge(consts, N_CONSTS)
                for c in range(NP):
                    if c >= 2:
                        act.wait_ge(hot_1_done, c - 1)
                    for t in range(PIECE):
                        at = NT + c * PIECE + t
                        nc.scalar.activation(apart[c % 2][:, t, :], slot_no[:, :], ACT.Square, scale=-1.0,
                                             bias=low[:, at:at + 1]).then_inc(apart_done, 1)
                    act.wait_ge(apart_done, (c + 1) * PIECE)
                    nc.scalar.activation(hot_1[:, c * PIECE:(c + 1) * PIECE, :], apart[c % 2][:, :, :], ACT.Relu,
                                         scale=-1.0, bias=one[:, 0:1]).then_inc(hot_1_done, 1)

            @block.vector
            def _(dve):
                chain = [0]

                def then(ins):
                    ins.then_inc(step, 1)
                    chain[0] += 1
                    dve.wait_ge(step, chain[0])

                def over_e(v):
                    return v.unsqueeze(2).to_broadcast(TE)

                lg = logits[:, :, :]
                then(nc.vector.tensor_reduce(tmax[:, :], lg, AX.X, ALU.max))
                nc.vector.tensor_tensor(shifted[:, :, :], lg, over_e(tmax[:, :]), ALU.subtract).then_inc(exp_in, 1)
                dve.wait_ge(exp_out, 1)
                then(nc.vector.tensor_reduce(psum_[:, :], prob[:, :, :], AX.X, ALU.add))
                then(nc.vector.reciprocal(prsum[:, :], psum_[:, :]))
                then(nc.vector.tensor_tensor(prob[:, :, :], prob[:, :, :], over_e(prsum[:, :]), ALU.mult))

                def top(values, best, hot_one):
                    then(nc.vector.tensor_reduce(best, values, AX.X, ALU.max))
                    then(nc.vector.tensor_tensor(tie[:, :, :], values, over_e(best), ALU.is_equal))
                    then(nc.vector.tensor_tensor(tie[:, :, :], tie[:, :, :], order[:, :].unsqueeze(1).to_broadcast(TE), ALU.mult))
                    then(nc.vector.tensor_reduce(pick[:, :], tie[:, :, :], AX.X, ALU.max))
                    then(nc.vector.tensor_tensor(hot_one, tie[:, :, :], over_e(pick[:, :]), ALU.is_equal))

                dve.wait_ge(consts, N_CONSTS)
                top(prob[:, :, :], top1[:, :], first_hot[:, :, :])
                then(nc.vector.scalar_tensor_tensor(rest[:, :, :], first_hot[:, :, :], -2.0, prob[:, :, :], ALU.mult, ALU.add))
                top(rest[:, :, :], top2[:, :], second_hot[:, :, :])
                then(nc.vector.scalar_tensor_tensor(wsum[:, :], top1[:, :], 1.0, top2[:, :], ALU.mult, ALU.add))
                then(nc.vector.tensor_scalar(wsum[:, :], wsum[:, :], 1e-9, None, ALU.add))
                then(nc.vector.reciprocal(wsum[:, :], wsum[:, :]))
                then(nc.vector.tensor_tensor(weight1[:, :], top1[:, :], wsum[:, :], ALU.mult))
                then(nc.vector.tensor_tensor(weight2[:, :], top2[:, :], wsum[:, :], ALU.mult))
                then(nc.vector.tensor_tensor(first_hot[:, :, :], first_hot[:, :, :], over_e(weight1[:, :]), ALU.mult))
                then(nc.vector.tensor_tensor(second_hot[:, :, :], second_hot[:, :, :], over_e(weight2[:, :]), ALU.mult))
                then(nc.vector.tensor_tensor(gates[:, :, :].rearrange("p e t -> p t e"), first_hot[:, :, :],
                                             second_hot[:, :, :], ALU.add))

                def running(dst, src):
                    then(nc.vector.tensor_copy(scan[0][:, :, 16:], src))
                    for k in range(5):
                        a, b = scan[k % 2], scan[(k + 1) % 2]
                        then(nc.vector.tensor_tensor(b[:, :, 16:], a[:, :, 16:], a[:, :, 16 - (1 << k):16 + NT - (1 << k)], ALU.add))
                    then(nc.vector.tensor_tensor(dst, scan[1][:, :, 16:], src, ALU.subtract))

                then(nc.vector.tensor_scalar(kept[:, :, :], gates[:, :, :], 0.0, None, ALU.is_gt))
                dve.sem_inc(kept_ready, 1)
                dve.wait_ge(counted, 1)
                then(nc.vector.tensor_reduce(counts[:, :], totals[:, :, :], AX.X, ALU.add))
                then(nc.vector.tensor_reduce(most[:, :], counts[:, :], AX.X, ALU.max))
                then(nc.vector.tensor_scalar(crowded[:, :], most[:, :], float(CAP), None, ALU.is_gt))
                dve.sem_inc(crowded_ready, 1)
                is_crowded = dve.value_load(crowded[0:1, 0:1], min_val=0, max_val=1)
                dve.nop()
                with dve.If(is_crowded == 1):
                    nc.vector.memset(cut[:, :], 0).then_inc(step, 1)
                    nc.vector.memset(bit[:, :], 1 << (BITS - 1)).then_inc(step, 1)
                    dve.wait_ge(step, chain[0] + 2)
                    base = chain[0] + 2
                    with dve.Fori(0, BITS) as r:
                        at = base + r * 7
                        nc.vector.tensor_tensor(trial[:, :], cut[:, :], bit[:, :], ALU.bitwise_or).then_inc(step, 1)
                        dve.wait_ge(step, at + 1)
                        nc.vector.tensor_tensor(kept[:, :, :], gates[:, :, :],
                                                trial[:, :].bitcast(f32).unsqueeze(2).to_broadcast([P, E, NT]),
                                                ALU.is_ge).then_inc(step, 1)
                        dve.wait_ge(step, at + 2)
                        dve.sem_inc(trial_ready, 1)
                        dve.wait_ge(trial_counted, r + 1)
                        nc.vector.tensor_reduce(reached[:, :], totals[:, :, :], AX.X, ALU.add).then_inc(step, 1)
                        dve.wait_ge(step, at + 3)
                        nc.vector.tensor_scalar(reached[:, :], reached[:, :], float(CAP), None, ALU.is_ge).then_inc(step, 1)
                        dve.wait_ge(step, at + 4)
                        nc.vector.tensor_tensor(found[:, :], reached[:, :], bit[:, :], ALU.mult).then_inc(step, 1)
                        dve.wait_ge(step, at + 5)
                        nc.vector.tensor_tensor(cut[:, :], cut[:, :], found[:, :], ALU.bitwise_or).then_inc(step, 1)
                        nc.vector.tensor_scalar(bit[:, :], bit[:, :], 1, None, ALU.logical_shift_right).then_inc(step, 1)
                        dve.wait_ge(step, at + 7)
                    chain[0] = base + BITS * 7
                    cut_f = cut[:, :].bitcast(f32).unsqueeze(2).to_broadcast([P, E, NT])
                    then(nc.vector.tensor_tensor(above[:, :, :], gates[:, :, :], cut_f, ALU.is_gt))
                    then(nc.vector.tensor_copy(kept[:, :, :], above[:, :, :]))
                    dve.sem_inc(trial_ready, 1)
                    dve.wait_ge(trial_counted, BITS + 1)
                    then(nc.vector.tensor_reduce(n_above[:, :], totals[:, :, :], AX.X, ALU.add))
                    then(nc.vector.tensor_scalar(room[:, :], n_above[:, :], -1.0, float(CAP), ALU.mult, ALU.add))
                    then(nc.vector.tensor_tensor(level[:, :, :], gates[:, :, :], cut_f, ALU.is_equal))
                    then(nc.vector.tensor_scalar(drop[:, :, :], gates[:, :, :], 0.0, None, ALU.is_gt))
                    then(nc.vector.tensor_tensor(level[:, :, :], level[:, :, :], drop[:, :, :], ALU.mult))
                    then(nc.vector.tensor_copy(kept[:, :, :], level[:, :, :]))
                    dve.sem_inc(trial_ready, 1)
                    dve.wait_ge(trial_counted, BITS + 2)
                    running(position[:, :, :], totals[:, :, :])
                    then(nc.vector.tensor_tensor(position[:, :, :], position[:, :, :], within[:, :, :], ALU.add))
                    then(nc.vector.tensor_tensor(position[:, :, :], position[:, :, :], room[:, :].unsqueeze(2).to_broadcast([P, E, NT]), ALU.is_lt))
                    then(nc.vector.tensor_tensor(level[:, :, :], level[:, :, :], position[:, :, :], ALU.mult))
                    then(nc.vector.tensor_tensor(kept[:, :, :], above[:, :, :], level[:, :, :], ALU.add))
                    dve.sem_inc(trial_ready, 1)
                    dve.wait_ge(trial_counted, BITS + 3)
                    end_of_search = chain[0]
                with dve.Else():
                    dve.sem_inc(step, end_of_search - (base - 2))
                dve.nop()

                live = slice(0, E * NT)

                def flat(v):
                    return v.rearrange("p e t -> p (e t)")

                running(position[:, :, :], totals[:, :, :])
                then(nc.vector.tensor_copy(n_kept[:, :], scan[1][:, :, 16 + NT - 1]))
                then(nc.vector.tensor_tensor(position[:, :, :], position[:, :, :], within[:, :, :], ALU.add))
                then(nc.vector.tensor_scalar(drop[:, :, :], kept[:, :, :], -float(DROPPED), float(DROPPED), ALU.mult, ALU.add))
                then(nc.vector.tensor_tensor(position[:, :, :], position[:, :, :], kept[:, :, :], ALU.mult))
                then(nc.vector.tensor_tensor(pos[:, live], flat(position[:, :, :]), flat(drop[:, :, :]), ALU.add))
                then(nc.vector.tensor_copy(flat(pos_i[:, :, :]), pos[:, live]))
                then(nc.vector.tensor_scalar(low_i[:, :, :], pos_i[:, :, :], P - 1, None, ALU.bitwise_and))
                then(nc.vector.tensor_copy(low[:, live], flat(low_i[:, :, :])))
                then(nc.vector.tensor_scalar(gates[:, :, :], gates[:, :, :], ffn_tanh[:, 0:1], None, ALU.mult))
                then(nc.vector.tensor_copy(gate_head[:, live], flat(gates[:, :, :])))
                then(nc.vector.tensor_tensor(gate_rest[:, live], flat(gates[:, :, :]), gate_head[:, live].bitcast(f32), ALU.subtract))
                dve.sem_inc(tallied, 1)
                dve.sem_inc(marks_ready, 1)
                edges = [P, NT, ST + 1]
                nc.vector.tensor_tensor(at_least_1[:, :, :], pos[:, NT:2 * NT].unsqueeze(2).to_broadcast(edges),
                                        tile_edge[:, :].unsqueeze(1).to_broadcast(edges), ALU.is_ge)\
                  .then_inc(at_least_1_done, 1)
                for c in range(NP):
                    mark_piece(0, c, c, hot_of[c % 2], facts_of[c % 2], buffers=2)
                then(nc.vector.tensor_scalar(rounded_i[:, :], scan[1][:, :, 16 + NT - 1], float(STEP - 1), None, ALU.add))
                then(nc.vector.tensor_scalar(rounded_i[:, :], rounded_i[:, :], 4096 - STEP, None, ALU.bitwise_and))
                then(nc.vector.tensor_copy(rounded[:, :], rounded_i[:, :]))
                then(nc.vector.tensor_scalar(has_tail[:, :], scan[1][:, :, 16 + NT - 1], float(TAIL), None, ALU.is_gt))
                then(nc.vector.tensor_scalar(rounded[:, :], rounded[:, :], float(CAP), None, ALU.subtract))
                then(nc.vector.tensor_tensor(rounded[:, :], rounded[:, :], has_tail[:, :], ALU.mult))
                then(nc.vector.tensor_scalar(tail_at[:, :], rounded[:, :], float(TAIL), None, ALU.add))
                read_table(table[0], 0, 0)
                read_table(table[1], 1, 1)

            @block.tensor
            def _(pe):
                pe.wait_ge(consts, N_CONSTS)
                kept_v = kept[:, :, :].rearrange("p e t -> p (e t)")

                def count():
                    nc.tensor.matmul(totals[:, :, :].rearrange("p e t -> p (e t)"), all_ones[:, :], kept_v, start=True, stop=True)
                    return nc.tensor.matmul(within[:, :, :].rearrange("p e t -> p (e t)"), before[:, :], kept_v, start=True, stop=True)

                pe.wait_ge(kept_ready, 1)
                count().then_inc(counted, 1)
                pe.wait_ge(crowded_ready, 1)
                is_crowded = pe.value_load(crowded[0:1, 0:1], min_val=0, max_val=1)
                pe.nop()
                with pe.If(is_crowded == 1):
                    with pe.Fori(0, BITS + 3) as r:
                        pe.wait_ge(trial_ready, r + 1)
                        count().then_inc(trial_counted, 1)
                pe.nop()
                for c in range(NP):
                    tally_piece(table[0], c, c, hot_of[c % 2], facts_of[c % 2])
                pe.wait_ge(facts_1_done, 5)
                for c in range(NP):
                    tiles = slice(c * PIECE, (c + 1) * PIECE)
                    pe.wait_ge(hot_1_done, c + 1)
                    tally_marks(table[1], c, hot_1[:, tiles, :], facts_1[:, tiles, :, :], tallied_1)

        routing.close()

        with ExitStack() as ctx:
            sb, pb, sem = keeper(ctx)
            wg_hd = [sb(f"wg_hd{n}", [P, HC, IC], f32r) for n in range(2)]
            wg_rs = [sb(f"wg_rs{n}", [P, HC, IC], f32r) for n in range(2)]
            wu_hd = [sb(f"wu_hd{n}", [P, HC, IC], f32r) for n in range(2)]
            wu_rs = [sb(f"wu_rs{n}", [P, HC, IC], f32r) for n in range(2)]
            wd_hd = [sb(f"wd_hd{n}", [P, NI, H], f32r) for n in range(2)]
            wd_rs = [sb(f"wd_rs{n}", [P, NI, H], f32r) for n in range(2)]
            xT_hd = [sb(f"xT_hd{n}", [P, HC, CAP], f32r) for n in range(2)]
            xT_rs = [sb(f"xT_rs{n}", [P, HC, CAP], f32r) for n in range(2)]
            xrow = [sb(f"xrow{n}", [P, H]) for n in range(XPREP)]
            h_hd = sb("h_hd", [P, NI, CAP], f32r)
            h_rs = sb("h_rs", [P, NI, CAP], f32r)
            silu = sb("silu", [P, 512])
            hfull = sb("hfull", [P, 512])
            gate_now = sb("gate_now", [P, ST])
            gather_now = sb("gather_now", [P, XPREP], i32)
            scatter_now = sb("scatter_now", [P, ST], i32)
            heads = (wg_hd, wu_hd, wd_hd)
            rests = (wg_rs, wu_rs, wd_rs)

            pg = [pb(f"pg{n}", [P, 512]) for n in range(2)]
            pu = [pb(f"pu{n}", [P, 512]) for n in range(2)]
            py = [pb(f"py{n}", [P, H]) for n in range(2)]
            px = pb("px", [P, HC, P])
            table_bank = pb("table_bank", [P, 512])

            w_head_done, w_split = sem("w_head_done"), sem("w_split")
            row_in = [sem(f"row_in{n}") for n in range(XPREP)]
            row_transposed, xT_head_done, xT_split = sem("row_transposed"), sem("xT_head_done"), sem("xT_split")
            gate_done, up_done = sem("gate_done"), sem("up_done")
            tail_gate_done, tail_up_done = sem("tail_gate_done"), sem("tail_up_done")
            tail_down_done = [sem(f"tail_down_done{n}") for n in range(ST - TAIL // P)]
            silu_done, hfull_done, h_head_done, h_split = sem("silu_done"), sem("hfull_done"), sem("h_head_done"), sem("h_split")
            down_done, y_added, y_gated, y_scattered = sem("down_done"), sem("y_added"), sem("y_gated"), sem("y_scattered")
            gate_copied, index_copied = sem("gate_copied"), sem("index_copied")
            y_free, h_cleared = sem("y_free"), sem("h_cleared")
            block = ctx.enter_context(nc.Block())
            PAIRS = NCH // 2
            XE = PAIRS * XPREP

            first_banks = [px[:, :, :]] + [b[:, :].rearrange("p (k n) -> p k n", k=HC) for b in py]

            def first_tile(k):
                return (k * 5) // 2

            UNIT = [(c0, w, it) for c0, w in BLOCKS for it in range(NI)]
            MAIN = [u for u in UNIT if u[0] < TAIL]
            TAILS = [u for u in UNIT if u[0] >= TAIL]
            NM, NTL = len(MAIN), len(TAILS)
            ROWS_AT = ({1: 0}, {0: 1, 1: 2})
            MT = TAIL // P

            @block.sync
            def _(sp):
                def fetch(e, c, number):
                    for part in range(3):
                        sp.wait_ge(w_split, number * 3 + (part - 2))
                        load_part(sp, e, c, part)

                fetch(0, 1, 1)
                with sp.Fori(1, PAIRS) as k:
                    for n in range(2):
                        fetch(0, k * 2 + n, k * 2 + n)
                with sp.Fori(1, E) as e:
                    with sp.Fori(0, PAIRS) as k:
                        for n in range(2):
                            fetch(e, k * 2 + n, e * NCH + k * 2 + n)
                fetch(E - 1, NCH - 1, E * NCH)

            @block.gpsimd
            def _(pool):
                for t in range(GATHERS_EARLY, ST):
                    gather_first(t)

                def gather_pair(e, k, copies, first=False):
                    for j in range(XPREP):
                        if not first:
                            pool.wait_ge(row_transposed, (e - 1) * XE + k * XPREP + (ST + j - XPREP + 1))
                        pool.tensor_copy(gather_now[:, j:j + 1], gather_row[:, bass.ds(e * ST + first_tile(k) + j, 1)])\
                            .then_inc(index_copied, 1)
                        wait_alone(pool, index_copied, copies + (j + 1))
                        pool.indirect_dma_start(xrow[j][:, :], None, xn2_rows,
                                                bass.IndirectOffsetOnAxis(ap=gather_now[:, j:j + 1], axis=0))\
                            .then_inc(row_in[j], 16)

                gather_pair(1, 0, 0, first=True)
                pool.wait_ge(row_transposed, ST)
                pool.sem_inc(y_free, 1)

                def gather_rest(e):
                    with pool.Fori(1, PAIRS) as k:
                        gather_pair(e + 1, k, e * (XE + 1) + k * XPREP)

                def scatter(e, copies):
                    pool.tensor_copy(scatter_now[:, :], scatter_row[:, bass.ds(e * ST, ST)]).then_inc(index_copied, 1)
                    pool.wait_ge(index_copied, copies + 1)
                    for t in range(ST):
                        wait_alone(pool, y_gated, e * ST + (t + 1))
                        pool.indirect_dma_start(out, bass.IndirectOffsetOnAxis(ap=scatter_now[:, t:t + 1], axis=0),
                                                y[:, t, :], None, compute_op=ALU.add).then_inc(y_scattered, 16)
                    pool.wait_ge(y_scattered, e * (ST * 16) + ST * 16)
                    pool.sem_inc(y_free, 1)

                with pool.Fori(0, E - 1) as e:
                    gather_rest(e)
                    wait_alone(pool, table_read, e * READS + (AHEAD + 1) * READS)
                    gather_pair(e + 2, 0, e * (XE + 1) + XE)
                    scatter(e, e * (XE + 1) + (XE + XPREP))
                gather_rest(E - 1)
                scatter(E - 1, (E - 1) * (XE + 1) + XE)

            @block.scalar
            def _(act):
                def split_weights(n, c, loaded):
                    act.wait_ge(w_loaded[c], loaded)
                    nc.scalar.activation(heads[c][n][:, :, :].rearrange("p a b -> p (a b)"), w_raw[c][:, :],
                                         ACT.Copy).then_inc(w_head_done, 1)

                def head_of_rows(par, t, number, bank=px[:, :, :]):
                    act.wait_ge(row_transposed, number)
                    nc.scalar.activation(xT_hd[par][:, :, bass.ds(t * P, P)], bank, ACT.Copy)\
                      .then_inc(xT_head_done, 1)

                def silu_and_head(q, gate_ready, number, c0, width, it):
                    b = q % 2
                    act.wait_ge(*gate_ready)
                    nc.scalar.activation(silu[:, 0:width], pg[b][:, 0:width], ACT.Silu).then_inc(silu_done, 1)
                    wait_alone(act, hfull_done, number + 2)
                    nc.scalar.activation(h_hd[:, it, bass.ds(c0, width)], hfull[:, 0:width], ACT.Copy)\
                      .then_inc(h_head_done, 1)

                for c in range(3):
                    split_weights(0, c, 16)
                for t in range(ST):
                    head_of_rows(0, t, t + 1, first_banks[t % 3])
                with act.Fori(0, E // 2) as p:
                    for par in range(2):
                        e = p * 2 + par
                        third = act.value_load(tail_at[0:1, bass.ds(e, 1)], min_val=TAIL + STEP - 2 * P, max_val=TAIL)
                        with act.Fori(0, PAIRS) as k:
                            m = e * PAIRS + k
                            for w in range(2):
                                u0 = m * (2 * UNITS) + w * UNITS
                                for q, (c0, width, it) in enumerate(UNIT):
                                    if q < NM:
                                        ready = (gate_done, m * (2 * NM) + (w * NM + q + 1))
                                    else:
                                        ready = (tail_gate_done, m * (2 * NTL) + (w * NTL + q - NM + 1))
                                    silu_and_head(q, ready, u0 + (q + 1), third if q >= NM else c0, width, it)
                                    if q < 3:
                                        split_weights(1 - w, q, m * 32 + (32 + 16 * w))
                                    if q in ROWS_AT[w]:
                                        j = ROWS_AT[w][q]
                                        head_of_rows(1 - par, first_tile(k) + j, m * XPREP + (ST + j + 1))
                        nc.scalar.activation(gate_now[:, :], slot_gate[:, bass.ds(e * ST, ST)], ACT.Copy)\
                          .then_inc(gate_copied, 1)
                        act.wait_ge(gate_copied, e + 1)
                        for t in range(ST):
                            act.wait_ge(y_added, e * (NCH * ST) + ((NCH - 1) * ST + t + 2))
                            nc.scalar.activation(y[:, t, :], y[:, t, :], ACT.Copy, scale=gate_now[:, t:t + 1])\
                              .then_inc(y_gated, 1)

            @block.vector
            def _(dve):
                def rest_of_weights(n, c, number):
                    dve.wait_ge(w_head_done, number)
                    nc.vector.tensor_tensor(rests[c][n][:, :, :].rearrange("p a b -> p (a b)"), w_raw[c][:, :],
                                            heads[c][n][:, :, :].rearrange("p a b -> p (a b)").bitcast(f32),
                                            ALU.subtract).then_inc(w_split, 1)

                def rest_of_rows(par, t, number, bank=px[:, :, :]):
                    dve.wait_ge(xT_head_done, number)
                    nc.vector.tensor_tensor(xT_rs[par][:, :, bass.ds(t * P, P)], bank,
                                            xT_hd[par][:, :, bass.ds(t * P, P)].bitcast(f32), ALU.subtract)\
                      .then_inc(xT_split, 1)

                def product(q, up_ready, number, c0, width, it):
                    dve.wait_ge(*up_ready)
                    dve.wait_ge(silu_done, number)
                    dve.wait_ge(h_split, number)
                    nc.vector.tensor_tensor(hfull[:, 0:width], silu[:, 0:width], pu[q % 2][:, 0:width],
                                            ALU.mult).then_inc(hfull_done, 1)

                def rest_of_h(q, up_ready, number, c0, width, it):
                    dve.wait_ge(h_head_done, number)
                    nc.vector.tensor_tensor(h_rs[:, it, bass.ds(c0, width)], hfull[:, 0:width],
                                            h_hd[:, it, bass.ds(c0, width)].bitcast(f32), ALU.subtract)\
                      .then_inc(h_split, 1)

                dve.sem_inc(y_added, 1)
                dve.sem_inc(hfull_done, 2)
                dve.sem_inc(h_split, 1)
                for h in (h_hd, h_rs):
                    nc.vector.memset(h[:, :, TAIL:CAP].bitcast(f32), 0.0).then_inc(h_cleared, 1)
                dve.wait_ge(h_cleared, 2)
                for c in range(3):
                    rest_of_weights(0, c, c + 1)
                for t in range(ST):
                    rest_of_rows(0, t, t + 1, first_banks[t % 3])
                with dve.Fori(0, E // 2) as p:
                    for par in range(2):
                        e = p * 2 + par
                        third = dve.value_load(tail_at[0:1, bass.ds(e, 1)], min_val=TAIL + STEP - 2 * P, max_val=TAIL)
                        with dve.Fori(0, PAIRS) as k:
                            m = e * PAIRS + k
                            for w in range(2):
                                u0 = m * (2 * UNITS) + w * UNITS
                                unit = [(q, (up_done, m * (2 * NM) + (w * NM + q + 1)) if q < NM else
                                         (tail_up_done, m * (2 * NTL) + (w * NTL + q - NM + 1)), u0 + (q + 1),
                                         third if q >= NM else c0, width, it)
                                        for q, (c0, width, it) in enumerate(UNIT)]
                                for q in range(NM):
                                    product(*unit[q])
                                    if q < NM - 1:
                                        rest_of_h(*unit[q])
                                        rest_of_weights(1 - w, q, m * 6 + (3 * w + 4 + q))
                                    if q in ROWS_AT[w]:
                                        j = ROWS_AT[w][q]
                                        rest_of_rows(1 - par, first_tile(k) + j, m * XPREP + (ST + j + 1))

                                between = {0: (rest_of_h, NM - 1), 1: (product, NM), 2: (rest_of_h, NM),
                                           3: (product, NM + 1), 4: (rest_of_h, NM + 1)}

                                def sums(anew):
                                    for t in range(ST):
                                        if t < MT:
                                            dve.wait_ge(down_done, m * (2 * MT) + (w * MT + t + 1))
                                        else:
                                            dve.wait_ge(tail_down_done[t - MT], m * 2 + (w + 1))
                                        if anew:
                                            nc.vector.tensor_copy(y[:, t, :], py[t % 2][:, :]).then_inc(y_added, 1)
                                        else:
                                            nc.vector.tensor_tensor(y[:, t, :], py[t % 2][:, :], y[:, t, :], ALU.add)\
                                              .then_inc(y_added, 1)
                                        if t in between:
                                            what, q = between[t]
                                            what(*unit[q])

                                if w == 0:
                                    dve.nop()
                                    with dve.If(k == 0):
                                        dve.wait_ge(y_free, e + 1)
                                        sums(True)
                                    with dve.Else():
                                        sums(False)
                                    dve.nop()
                                    mark_piece(e + AHEAD, k, e * NP + (k + NP), hot, facts)
                                else:
                                    sums(False)
                        read_table(table_bank, e + AHEAD, e + AHEAD)

            @block.tensor
            def _(pe):
                def transpose_rows(rows, bank=px[:, :, :]):
                    for k in range(HC):
                        last = nc.tensor.transpose(bank[:, k, :], rows[:, k * P:(k + 1) * P], ident[:, :])
                    last.then_inc(row_transposed, 1)

                def three_passes(dst, pairs):
                    last = None
                    for n, ((lhd, lrs), (rhd, rrs)) in enumerate(pairs):
                        nc.tensor.matmul(dst, lhd, rhd, start=(n == 0), stop=False)
                        nc.tensor.matmul(dst, lhd, rrs, start=False, stop=False)
                        last = nc.tensor.matmul(dst, lrs, rhd, start=False, stop=(n == len(pairs) - 1))
                    return last

                def gate_and_up(q, w, par, u0, c0, width, it, gate_sem, up_sem):
                    pe.wait_ge(hfull_done, u0 + (q + 1))
                    ic = slice(it * P, (it + 1) * P)
                    for (hd, rs), dst, s in (((wg_hd, wg_rs), pg, gate_sem), ((wu_hd, wu_rs), pu, up_sem)):
                        three_passes(dst[q % 2][:, 0:width],
                                     [((hd[w][:, c, ic], rs[w][:, c, ic]),
                                       (xT_hd[par][:, c, c0:c0 + width], xT_rs[par][:, c, c0:c0 + width]))
                                      for c in range(HC)]).then_inc(s, 1)

                def down(t, w, y0, s):
                    pe.wait_ge(y_added, y0 + max(t, 1))
                    sl = slice(t * P, (t + 1) * P)
                    three_passes(py[t % 2][:, :],
                                 [((h_hd[:, it, sl], h_rs[:, it, sl]), (wd_hd[w][:, it, :], wd_rs[w][:, it, :]))
                                  for it in range(NI)]).then_inc(s, 1)

                for t in range(ST):
                    pe.wait_ge(first_row_in[t], 16)
                    if t >= 3:
                        pe.wait_ge(xT_split, t - 2)
                    transpose_rows(y[:, t, :], first_banks[t % 3])
                with pe.Fori(0, E // 2) as p:
                    for par in range(2):
                        e = p * 2 + par
                        filled = pe.value_load(n_kept[0:1, bass.ds(e, 1)], min_val=0, max_val=T)
                        wait_alone(pe, xT_split, e * XE + ST)
                        with pe.Fori(0, PAIRS) as k:
                            m = e * PAIRS + k
                            for w in range(2):
                                u0 = m * (2 * UNITS) + w * UNITS
                                y0 = m * (2 * ST) + w * ST
                                pe.wait_ge(w_split, m * 6 + (3 * w + 3))
                                def next_rows(q):
                                    if q in ROWS_AT[w]:
                                        j = ROWS_AT[w][q]
                                        pe.wait_ge(row_in[j], m * 16 + 16)
                                        pe.wait_ge(xT_split, m * XPREP + (ST + j))
                                        transpose_rows(xrow[j])

                                def unit(q, c0, width, tail=False):
                                    it = UNIT[q][2]
                                    gate_and_up(q, w, par, u0, c0, width, it, *((tail_gate_done, tail_up_done) if tail
                                                                               else (gate_done, up_done)))

                                for q in range(NI):
                                    unit(q, *BLOCKS[0])
                                    next_rows(q)
                                    if w == 1 and q == 0:
                                        tally_piece(table_bank, k, e * NP + (k + NP), hot, facts)

                                def second_and_third(slots):
                                    start = BLOCKS[1][0]
                                    third = slots - 2 * P if slots > TAIL else slots
                                    for q in range(NI, 2 * NI):
                                        unit(q, start, third - start)
                                        next_rows(q)
                                    for q in range(2 * NI, 3 * NI):
                                        if slots > TAIL:
                                            unit(q, third, 2 * P, tail=True)
                                    if slots <= TAIL:
                                        pe.sem_inc(tail_gate_done, NTL)
                                        pe.sem_inc(tail_up_done, NTL)

                                def by_tokens(choices):
                                    if len(choices) == 1:
                                        second_and_third(choices[0])
                                        return
                                    half = len(choices) // 2
                                    pe.nop()
                                    with pe.If(filled > choices[half - 1]):
                                        by_tokens(choices[half:])
                                    with pe.Else():
                                        by_tokens(choices[:half])
                                    pe.nop()

                                by_tokens(list(range(BLOCKS[1][0] + LEAST, CAP + 1, STEP)))
                                for t in range(MT):
                                    for n, (c0, _) in enumerate(BLOCKS):
                                        if c0 == t * P:
                                            pe.wait_ge(h_split, u0 + (n + 1) * NI + 1)
                                    if t == MT - 2:
                                        pe.wait_ge(h_split, u0 + UNITS + 1)
                                    down(t, w, y0, down_done)
                                pe.nop()
                                with pe.If(filled > TAIL):
                                    down(MT, w, y0, tail_down_done[0])
                                with pe.Else():
                                    pe.sem_inc(tail_down_done[0], 1)
                                pe.nop()
                                with pe.If(filled > TAIL + P):
                                    down(MT + 1, w, y0, tail_down_done[1])
                                with pe.Else():
                                    pe.sem_inc(tail_down_done[1], 1)
                                pe.nop()


_INS = ['x', 'ctx_1024', 'g_xattn', 'g_ffn', 'L0_xattn_Wq', 'L0_xattn_bq', 'L0_xattn_Wk', 'L0_xattn_bk',
        'L0_xattn_Wv', 'L0_xattn_bv', 'L0_ffn_router_gate', 'L0_ffn_gate_w', 'L0_ffn_up_w', 'L0_ffn_down_w']


def kernel(**inputs):
    import numpy as _np
    import concourse.bacc as _bacc
    from concourse import mybir as _mybir
    from concourse.bass_utils import run_bass_kernel_spmd as _run

    nc = _bacc.Bacc("TRN2", target_bir_lowering=False, num_devices=1)
    arrays, args = {}, []
    for name in _INS:
        a = _np.ascontiguousarray(inputs[name])
        arrays[f"in_{name}_dram"] = a
        args.append(nc.dram_tensor(f"in_{name}_dram", a.shape, _mybir.dt.from_np(a.dtype), kind="ExternalInput").ap())
    args.append(nc.dram_tensor("out_dram", (T + CAP, H), _mybir.dt.float32, kind="ExternalOutput").ap())
    flamingo_layer(nc, *args)
    r = _run(nc, [arrays], core_ids=[0])
    return r.results[0]["out_dram"][:T].reshape(B, S, H)
```
